# Optimizing a Trainium2 kernel written in Bass

```python
import numpy as np
import jax
import jax.numpy as jnp

def _softmax(x, axis=-1):
    return jax.nn.softmax(x, axis=axis)

def _gelu(x):
    return jax.nn.gelu(x, approximate=True)

def _silu(x):
    return jax.nn.silu(x)

def _sigmoid(x):
    return jax.nn.sigmoid(x)

def _layernorm(x, axis=-1, eps=1e-05):
    m = jnp.mean(x, axis=axis, keepdims=True)
    v = jnp.var(x, axis=axis, keepdims=True)
    return (x - m) / jnp.sqrt(v + eps)

def _scatter_add(tgt, idx, src, axis=0):
    return tgt.at[idx].add(src)

def _segment_sum(src, seg, n):
    return jax.ops.segment_sum(src, seg, n)
kernel_name = 'mk_decoder_postln_d1_seqx_r8_e5fdfe'

def setup_inputs(seed: int=0):
    np.random.seed(seed)
    _w = jnp.asarray

    def _rec_inputs():
        import jax
        import jax.numpy as jnp
        _rk = jax.random.key(seed)
        x = 0.0003765 + 1 * jax.random.normal(jax.random.fold_in(_rk, 1), (16, 128, 256), jnp.float32)
        _lenS = 128 - jax.random.randint(jax.random.fold_in(_rk, 7), (16,), 0, max(1, 128 // 4) + 1, jnp.int32)
        _lenS2 = 128 - jax.random.randint(jax.random.fold_in(_rk, 8), (16,), 0, max(1, 128 // 4) + 1, jnp.int32)
        _ctx_2048P = jax.random.normal(jax.random.fold_in(_rk, 11), (16, 16, 256), jnp.float32)
        _ctx_2048c = jax.random.dirichlet(jax.random.fold_in(_rk, 511), 0.3 * jnp.ones((16,), jnp.float32), (16, 128))
        _ctx_2048t = jnp.einsum('bsk,bkd->bsd', _ctx_2048c, _ctx_2048P)
        _ctx_2048t = _ctx_2048t * jax.lax.rsqrt(jnp.mean(jnp.square(_ctx_2048t)) + 1e-12) * 0.953939
        ctx_2048 = -0.000292821 + 1.00034 * (_ctx_2048t + 0.3 * jax.random.normal(jax.random.fold_in(_rk, 611), (16, 128, 256), jnp.float32))
        return (x, ctx_2048)
    x, ctx_2048 = _rec_inputs()

    def _L0_attn_setup():
        import jax, jax.numpy as jnp
        import numpy as np
        import math
        NUM_HEADS = 16
        SPARSITY_THRESHOLD = 0.2
        MIN_TOKENS = 32

        def _forward(x, Wq, bq, Wk, bk, Wv, bv, Wo, bo, Wi, bi):
            B, S, H = x.shape
            nh = NUM_HEADS
            hd = H // nh
            importance = (x @ Wi + bi)[..., 0]
            sorted_desc = jnp.sort(importance, axis=-1)[:, ::-1]
            tidx = min(max(1, int(S * SPARSITY_THRESHOLD)), S - 1)
            threshold = sorted_desc[:, tidx][:, None]
            sparse_mask = (importance > threshold).astype(x.dtype)
            if MIN_TOKENS > 0 and S > MIN_TOKENS:
                _, top_idx = jax.lax.top_k(importance, min(MIN_TOKENS, S))
                rows = jnp.arange(B)[:, None]
                min_mask = jnp.zeros_like(importance).at[rows, top_idx].set(1.0)
                sparse_mask = jnp.maximum(sparse_mask, min_mask)
            mask = sparse_mask[:, :, None, None]
            q = (x @ Wq + bq).reshape(B, S, nh, hd)
            k = (x @ Wk + bk).reshape(B, S, nh, hd) * mask
            v = (x @ Wv + bv).reshape(B, S, nh, hd) * mask
            scale = 1.0 / math.sqrt(hd)
            scores = jnp.einsum('bqhd,bkhd->bhqk', q, k) * scale
            attn = jax.nn.softmax(scores, axis=-1)
            out = jnp.einsum('bhqk,bkhd->bqhd', attn, v).reshape(B, S, H)
            return out @ Wo + bo
        key = jax.random.key(seed)
        ks = jax.random.split(key, 11)
        B, S, H = (4, 256, 256)
        s = 0.02
        return {'x': jax.random.normal(ks[0], (B, S, H), jnp.float32), 'Wq': jax.random.normal(ks[1], (H, H), jnp.float32) * s, 'bq': jax.random.normal(ks[2], (H,), jnp.float32) * s, 'Wk': jax.random.normal(ks[3], (H, H), jnp.float32) * s, 'bk': jax.random.normal(ks[4], (H,), jnp.float32) * s, 'Wv': jax.random.normal(ks[5], (H, H), jnp.float32) * s, 'bv': jax.random.normal(ks[6], (H,), jnp.float32) * s, 'Wo': jax.random.normal(ks[7], (H, H), jnp.float32) * s, 'bo': jax.random.normal(ks[8], (H,), jnp.float32) * s, 'Wi': jax.random.normal(ks[9], (H, 1), jnp.float32) * s, 'bi': jax.random.normal(ks[10], (1,), jnp.float32) * s}
    _L0_attn_all = _L0_attn_setup()
    _L0_attn_in = {k: v for k, v in _L0_attn_all.items() if k in ('Wq', 'bq', 'Wk', 'bk', 'Wv', 'bv', 'Wo', 'bo', 'Wi', 'bi')}
    del _L0_attn_all

    def _L0_xattn_setup():
        import jax, jax.numpy as jnp
        import numpy as np
        key = jax.random.key(seed)
        k1, k2, k3, k4, k5 = jax.random.split(key, 5)
        B, D_MODEL, L = (2, 128, 256)
        HEAD_DIM = 8
        H = D_MODEL // HEAD_DIM
        return {'k': jax.random.normal(k1, (B, D_MODEL, L), dtype=jnp.float32), 'v': jax.random.normal(k2, (B, D_MODEL, L), dtype=jnp.float32), 'q': jax.random.normal(k3, (B, D_MODEL, L), dtype=jnp.float32), 'ssm_kernel': jax.random.normal(k4, (H, L), dtype=jnp.float32), 'D': jax.random.normal(k5, (H,), dtype=jnp.float32), 'head_dim': HEAD_DIM}
    _L0_xattn_all = _L0_xattn_setup()
    _L0_xattn_in = {k: v for k, v in _L0_xattn_all.items() if k in ('ssm_kernel', 'D')}
    del _L0_xattn_all

    def _L0_ffn_setup():
        import jax, jax.numpy as jnp
        import numpy as np
        TOPK = 2

        def _mlp(x, w1, w2, w3):
            a = jnp.dot(x, w1.T).astype(jnp.float32)
            b = jnp.dot(x, w3.T).astype(jnp.float32)
            h = (jax.nn.silu(a) * b).astype(x.dtype)
            return jnp.dot(h, w2.T)
        key = jax.random.key(seed)
        ks = jax.random.split(key, 8)
        B, S, D, I, E = (4, 256, 256, 176, 16)
        SI = I * 2
        sc = 0.02
        return {'x': jax.random.normal(ks[0], (B, S, D), jnp.bfloat16), 'gate_w': jax.random.normal(ks[1], (E, D), jnp.float32) * sc, 'w1': jax.random.normal(ks[2], (E, I, D), jnp.bfloat16) * sc, 'w2': jax.random.normal(ks[3], (E, D, I), jnp.bfloat16) * sc, 'w3': jax.random.normal(ks[4], (E, I, D), jnp.bfloat16) * sc, 'sw1': jax.random.normal(ks[5], (SI, D), jnp.bfloat16) * sc, 'sw2': jax.random.normal(ks[6], (D, SI), jnp.bfloat16) * sc, 'sw3': jax.random.normal(ks[7], (SI, D), jnp.bfloat16) * sc}
    _L0_ffn_all = _L0_ffn_setup()
    _L0_ffn_in = {k: v for k, v in _L0_ffn_all.items() if k in ('gate_w', 'w1', 'w2', 'w3', 'sw1', 'sw2', 'sw3')}
    del _L0_ffn_all
    return {'x': x, 'ctx_2048': ctx_2048, 'L0_attn_Wq': _L0_attn_in['Wq'], 'L0_attn_bq': _L0_attn_in['bq'], 'L0_attn_Wk': _L0_attn_in['Wk'], 'L0_attn_bk': _L0_attn_in['bk'], 'L0_attn_Wv': _L0_attn_in['Wv'], 'L0_attn_bv': _L0_attn_in['bv'], 'L0_attn_Wo': _L0_attn_in['Wo'], 'L0_attn_bo': _L0_attn_in['bo'], 'L0_attn_Wi': _L0_attn_in['Wi'], 'L0_attn_bi': _L0_attn_in['bi'], 'L0_xattn_ssm_kernel': _L0_xattn_in['ssm_kernel'], 'L0_xattn_D': _L0_xattn_in['D'], 'L0_ffn_gate_w': _L0_ffn_in['gate_w'], 'L0_ffn_w1': _L0_ffn_in['w1'], 'L0_ffn_w2': _L0_ffn_in['w2'], 'L0_ffn_w3': _L0_ffn_in['w3'], 'L0_ffn_sw1': _L0_ffn_in['sw1'], 'L0_ffn_sw2': _L0_ffn_in['sw2'], 'L0_ffn_sw3': _L0_ffn_in['sw3']}

def reference(x, ctx_2048, L0_attn_Wq, L0_attn_bq, L0_attn_Wk, L0_attn_bk, L0_attn_Wv, L0_attn_bv, L0_attn_Wo, L0_attn_bo, L0_attn_Wi, L0_attn_bi, L0_xattn_ssm_kernel, L0_xattn_D, L0_ffn_gate_w, L0_ffn_w1, L0_ffn_w2, L0_ffn_w3, L0_ffn_sw1, L0_ffn_sw2, L0_ffn_sw3):
    import jax
    import jax.numpy as jnp

    def _L0_attn_ref(x, Wq, bq, Wk, bk, Wv, bv, Wo, bo, Wi, bi):
        import jax, jax.numpy as jnp
        import numpy as np
        import math
        NUM_HEADS = 16
        SPARSITY_THRESHOLD = 0.2
        MIN_TOKENS = 32

        def _forward(x, Wq, bq, Wk, bk, Wv, bv, Wo, bo, Wi, bi):
            B, S, H = x.shape
            nh = NUM_HEADS
            hd = H // nh
            importance = (x @ Wi + bi)[..., 0]
            sorted_desc = jnp.sort(importance, axis=-1)[:, ::-1]
            tidx = min(max(1, int(S * SPARSITY_THRESHOLD)), S - 1)
            threshold = sorted_desc[:, tidx][:, None]
            sparse_mask = (importance > threshold).astype(x.dtype)
            if MIN_TOKENS > 0 and S > MIN_TOKENS:
                _, top_idx = jax.lax.top_k(importance, min(MIN_TOKENS, S))
                rows = jnp.arange(B)[:, None]
                min_mask = jnp.zeros_like(importance).at[rows, top_idx].set(1.0)
                sparse_mask = jnp.maximum(sparse_mask, min_mask)
            mask = sparse_mask[:, :, None, None]
            q = (x @ Wq + bq).reshape(B, S, nh, hd)
            k = (x @ Wk + bk).reshape(B, S, nh, hd) * mask
            v = (x @ Wv + bv).reshape(B, S, nh, hd) * mask
            scale = 1.0 / math.sqrt(hd)
            scores = jnp.einsum('bqhd,bkhd->bhqk', q, k) * scale
            attn = jax.nn.softmax(scores, axis=-1)
            out = jnp.einsum('bhqk,bkhd->bqhd', attn, v).reshape(B, S, H)
            return out @ Wo + bo
        return _forward(x, Wq, bq, Wk, bk, Wv, bv, Wo, bo, Wi, bi)

    def _L0_xattn_ref(k, v, q, ssm_kernel, D, head_dim):
        import jax, jax.numpy as jnp
        import numpy as np
        B, HD, L = k.shape
        H = HD // head_dim
        fft_size = 2 * L
        k_ = k.reshape(B, H, head_dim, L)
        v_ = v.reshape(B, H, head_dim, L)
        q_ = q.reshape(B, H, head_dim, L)
        kv = jnp.einsum('bhil,bhjl->bijhl', k_, v_)
        kv_f = jnp.fft.rfft(kv, n=fft_size)
        kernel_f = jnp.fft.rfft(ssm_kernel, n=fft_size)
        y = jnp.fft.irfft(kv_f * kernel_f, n=fft_size)[..., :L]
        out = y + kv * D[None, None, None, :, None]
        out = jnp.einsum('bijhl,bhil->bjhl', out, q_)
        out = jnp.transpose(out, (0, 2, 1, 3)).reshape(B, H * head_dim, L)
        return out.astype(k.dtype)

    def _L0_ffn_ref(x, gate_w, w1, w2, w3, sw1, sw2, sw3):
        import jax, jax.numpy as jnp
        import numpy as np
        TOPK = 2

        def _mlp(x, w1, w2, w3):
            a = jnp.dot(x, w1.T).astype(jnp.float32)
            b = jnp.dot(x, w3.T).astype(jnp.float32)
            h = (jax.nn.silu(a) * b).astype(x.dtype)
            return jnp.dot(h, w2.T)
        B, S, D = x.shape
        E = gate_w.shape[0]
        xf = x.reshape(-1, D)
        T = xf.shape[0]
        scores = jax.nn.sigmoid(jnp.dot(xf.astype(jnp.float32), gate_w.T))
        topv, topi = jax.lax.top_k(scores, TOPK)
        topv = topv / topv.sum(axis=-1, keepdims=True)
        dw = jnp.zeros((T, E), jnp.float32).at[jnp.arange(T)[:, None], topi].add(topv)
        y0 = _mlp(xf, sw1, sw2, sw3).astype(jnp.float32)

        def step(y, ws):
            e1, e2, e3, we = ws
            out = _mlp(xf, e1, e2, e3).astype(jnp.float32)
            return (y + out * we[:, None], None)
        y, _ = jax.lax.scan(step, y0, (w1, w2, w3, dw.T))
        return y.astype(x.dtype).reshape(B, S, D)
    x = _layernorm(x + _L0_attn_ref(x, L0_attn_Wq, L0_attn_bq, L0_attn_Wk, L0_attn_bk, L0_attn_Wv, L0_attn_bv, L0_attn_Wo, L0_attn_bo, L0_attn_Wi, L0_attn_bi), axis=-1)
    x = _layernorm(x + _L0_xattn_ref(ctx_2048, ctx_2048, x, L0_xattn_ssm_kernel, L0_xattn_D, 8), axis=-1)
    x = _layernorm(x + _L0_ffn_ref(x, L0_ffn_gate_w, L0_ffn_w1, L0_ffn_w2, L0_ffn_w3, L0_ffn_sw1, L0_ffn_sw2, L0_ffn_sw3), axis=-1)
    return x

_drawn_inputs = setup_inputs


def setup_inputs(seed=0):
    import zlib

    import numpy as np

    out = dict(_drawn_inputs(seed))
    spreads = {}
    factors = {'L0_attn_Wq': 8.0,
     'L0_attn_bq': 8.0,
     'L0_attn_Wk': 8.0,
     'L0_attn_bk': 8.0,
     'L0_attn_Wv': 6.392,
     'L0_attn_bv': 8.0,
     'L0_attn_Wo': 6.024,
     'L0_attn_Wi': 6.979,
     'L0_ffn_gate_w': 6.167,
     'L0_ffn_w1': 5.808,
     'L0_ffn_w2': 5.749,
     'L0_ffn_w3': 5.738,
     'L0_ffn_sw1': 2.894,
     'L0_ffn_sw2': 2.89,
     'L0_ffn_sw3': 2.879}
    for name, (base, spread) in spreads.items():
        noise = np.random.default_rng([zlib.crc32(name.encode()), seed]).standard_normal(out[name].shape)
        drawn = base * np.exp(spread * noise) if base else spread * noise
        out[name] = jnp.asarray(drawn.astype(out[name].dtype))
    for name, factor in factors.items():
        out[name] = (out[name] * factor).astype(out[name].dtype)
    return out
```

```python
from contextlib import ExitStack

import concourse.bass as bass
from concourse import mybir

F32 = mybir.dt.float32
BF16 = mybir.dt.bfloat16
ALU = mybir.AluOpType
ACT = mybir.ActivationFunctionType
AX = mybir.AxisListType

P = 128
B, S, D = 16, 128, 256
C = D // P
NH, HD = 16, 16
KEEP = 32
GROUPS = NH // 4
EPS = 1e-5
SCALE = HD ** -0.5
NEG = -3.0e38
HEADS, HEAD = 16, 8
DIAG = HEAD // 2 + 1
WRAP = HEAD + DIAG - 1
BH = B // 2
E, TOP, I = 16, 2, 176
KI = I // 2
SI = 2 * I
SP_ = [(0, P), (P, P), (2 * P, SI - 2 * P)]
NB = B * TOP
NT = NB + E - 1
ROWS = DIAG + 2 * 3

C_ID, C_TRI, C_IOTA, C_HM, C_ONES, C_E = 0, 128, 256, 288, 296, 424
C_STRI = C_E + GROUPS * P
C_N = C_STRI + P
C_M = C_N + 64
C_NEW = C_M + 16
C_W = C_NEW + E * NB


def decoder_layer(nc, x, xT, ctxd, ker, skip, Wq, Wk, Wv, Wo, cols, rows, consts, gate, w13, w2, sw13, sw2, out):
    with ExitStack() as ctx:
        def sb(name, shape, dt=F32):
            return ctx.enter_context(nc.sbuf_tensor(name, shape, dt))

        def ps(name, shape, dt=F32):
            return ctx.enter_context(nc.psum_tensor(name, shape, dt))

        def sem(name):
            return ctx.enter_context(nc.semaphore(name))

        cst = sb("cst", [P, C_W])
        ident = cst[:, C_ID:C_ID + P]
        tri = cst[:, C_TRI:C_TRI + P]
        iota = cst[:, C_IOTA:C_IOTA + KEEP]
        headmask = cst[:, C_HM:C_HM + 8]
        roomy = sb("roomy", [P, E * 2 * D])
        wq, wk, wv, wo = (roomy[:, k * C * D:(k + 1) * C * D].rearrange("p (c n) -> p c n", c=C) for k in range(4))
        colb = sb("colb", [P, 5])
        bqs = sb("bqs", [P, C])
        rowb = sb("rowb", [P, 3, D])
        xall = sb("xall", [P, B, D])
        imp = sb("imp", [P, B])
        
        impT = sb("impT", [B, 5, P])
        top8 = sb("top8", [B, 4, 8])
        chosenT = sb("chosenT", [B, P])
        chosen = sb("chosen", [P, B])
        place = sb("place", [P, B])
        pick = sb("pick", [P, B, KEEP])
        half = sb("half", [P, 2])

        xr = [sb(f"xr{j}", [P, D]) for j in range(2)]
        xTr = [sb(f"xTr{j}", [P, C, S]) for j in range(2)]
        xbo = [sb(f"xbo{j}", [P, D]) for j in range(2)]
        xsel = sb("xsel", [P, C, KEEP])
        qT = [sb(f"qT{j}", [P, C, S]) for j in range(2)]
        kbd = [sb(f"kbd{j}", [P, C, 8, KEEP]) for j in range(2)]
        vbd = [sb(f"vbd{j}", [P, GROUPS, 4, HD + 1]) for j in range(2)]
        negm = [sb(f"negm{j}", [P, NH]) for j in range(2)]
        zero_e = [sb(f"zero_e{j}", [P, NH]) for j in range(2)]
        mx = sb("mx", [P, NH])
        negT = sb("negT", [NH, S])
        probs = sb("probs", [P, GROUPS, S])
        den = sb("den", [P, NH])
        rec = sb("rec", [P, NH])
        attn = sb("attn", [P, D])
        attnT = sb("attnT", [P, C, S])
        res = [sb(f"res{j}", [P, D]) for j in range(2)]
        stats = sb("stats", [P, 6])
        mv = [sb(f"mv{j}", [P, 2]) for j in range(2)]
        vare = sb("vare", [P, 1])
        rstd = [sb(f"rstd{j}", [P, 1]) for j in range(2)]

        x1r = [sb(f"x1r{j}", [P, D]) for j in range(2)]
        x1q = roomy[:, 4 * C * D:4 * C * D + HEADS * C * B * WRAP].rearrange(
            "p (h c b w) -> p h c b w", h=HEADS, c=C, b=B)
        kerp = sb("kerp", [HEADS, 2 * D])
        skipc = sb("skipc", [HEADS, 1])
        ctxr = [sb(f"ctxr{j}", [P, C, B, WRAP]) for j in range(2)]
        toe = [sb(f"toe{j}", [P, 2 * P]) for j in range(2)]
        NKV, NPR = BH * DIAG * HEAD, BH * ROWS * HEAD
        room = sb("room", [P, 2 * C * (NKV + NPR)])
        kv = [room[:, j * C * NKV:(j + 1) * C * NKV].rearrange("p (c b d i) -> p c b d i", c=C, b=BH, d=DIAG)
              for j in range(2)]
        prod = [[room[:, 2 * C * NKV + (j * C + c) * NPR:2 * C * NKV + (j * C + c + 1) * NPR].rearrange(
            "p (b s i) -> p b s i", b=BH, s=ROWS) for c in range(C)] for j in range(2)]
        conv = sb("conv", [P, B, C, S])
        convr = [sb(f"convr{j}", [P, C, S]) for j in range(2)]
        x1s = [sb(f"x1s{j}", [P, D]) for j in range(2)]
        res2 = [sb(f"res2{j}", [P, D]) for j in range(2)]
        x2r = [sb(f"x2r{j}", [P, D]) for j in range(2)]

        used = [0]

        def late(*shape):
            names = "abc"[:len(shape)]
            size = 1
            for d in shape:
                size *= d
            part = room[:, used[0]:used[0] + size]
            used[0] += size
            if len(shape) == 1:
                return part
            return part.rearrange(f"p ({' '.join(names)}) -> p {' '.join(names)}", **dict(zip(names[1:], shape[1:])))
        gw = sb("gw", [P, C, E])
        w13s = sb("w13s", [P, C, E, 2 * I])
        w2s = roomy[0:KI, :].rearrange("p (e k n) -> p e k n", e=E, k=2)
        sw13s = sb("sw13s", [P, C, 2 * SI])
        sw2s = sb("sw2s", [P, 3, D])
        zeros = sb("zeros", [P, D])
        x2T = [sb(f"x2T{j}", [P, C, S]) for j in range(2)]
        x2all = xall
        z0 = conv[:, :, :, :].rearrange("p b c s -> p b (c s)")
        logit = sb("logit", [P, B, E])
        best = sb("best", [P, B, 8])
        bestix = sb("bestix", [P, B, 8], mybir.dt.uint32)
        ixf = sb("ixf", [P, NB])
        hot = late(NB, E)
        upto = late(E, NB)
        slot = late(NB, E)
        over = late(E, 16)
        tiles = sb("tiles", [P, E])
        endt = sb("endt", [P, E])
        base = sb("base", [P, E])
        posf = sb("posf", [P, NB])
        pos = sb("pos", [P, NB], mybir.dt.uint32)
        ended = sb("ended", [1, NT, E])
        ownf = sb("ownf", [1, NT])
        owner = sb("owner", [1, NT], mybir.dt.int32)
        sg = sb("sg", [P, B, TOP])
        sgsum = sb("sgsum", [P, B])
        wts = sb("wts", [P, B, TOP])
        ssil = sb("ssil", [P, SI])
        sh = sb("sh", [P, SI])
        shT = sb("shT", [P, 3, S])
        xs = [late(D) for j in range(2)]
        xsT = x2T
        sil = [late(I) for j in range(2)]
        hid = [late(I) for j in range(2)]
        hidT = [late(2, P)[0:KI] for j in range(2)]
        ys = [late(D) for j in range(2)]
        SLOTS = 4
        yg = [sb(f"yg{k}", [P, TOP, D]) for k in range(SLOTS - 1)]
        yg.append(pick[:, :, :].rearrange("p b k -> p (b k)").rearrange("p (t d) -> p t d", t=TOP))
        st3 = sb("st3", [P, B, 6])
        mv3 = sb("mv3", [P, B, 2])
        ve3 = sb("ve3", [P, B])
        rs3 = sb("rs3", [P, B])
        x2d = nc.dram_tensor("x2d", (B, S, D), F32).ap()
        x2Td = nc.dram_tensor("x2Td", (B, P, C, S), F32).ap()
        xsd = nc.dram_tensor("xsd", (NT * P, D), F32).ap()
        ysd = nc.dram_tensor("ysd", (NT * P, D), F32).ap()

        kerd = nc.dram_tensor("kerd", (HEADS, 2 * D), F32).ap()
        x1d = nc.dram_tensor("x1d", (B, S, D), F32).ap()

        p_kv = ps("p_kv", [P, 512])
        p_q = ps("p_q", [P, C, 256])
        p_s = ps("p_s", [P, 512])
        p_t = ps("p_t", [P, GROUPS, S])
        p_o = ps("p_o", [P, 512])
        p_y = ps("p_y", [P, 512])
        p_x = ps("p_x", [P, C, S])
        p_8 = ps("p_8", [P, 512])
        p_conv = [[p_kv[:, 0:320], p_q[:, :, :].rearrange("p c s -> p (c s)")[:, 0:320]],
                  [p_s[:, 0:320], p_8[:, 0:320]]]
        p_back = p_o[:, 0:256]
        p_logit = p_8[:, 0:E]
        p_rank, p_sum = p_o[:, :], p_y[:, :]
        p_a, p_b = p_kv[:, 0:SI], p_q[:, :, :].rearrange("p c s -> p (c s)")[:, 0:SI]
        p_hT = p_s[:, 0:3 * S].rearrange("p (k s) -> p k s", k=3)
        p_z = p_t[:, 0:2, :].rearrange("p g s -> p (g s)")
        p_xs = p_x
        p_ab = [p_kv[:, 0:SI], p_q[:, :, :].rearrange("p c s -> p (c s)")[:, 0:SI]]
        p_hid = p_s[0:KI, 0:2 * P].rearrange("p (k s) -> p k s", k=2)
        p_ye = p_t[:, 0:2, :].rearrange("p g s -> p (g s)")
        g_v = p_kv[:, 0:C * KEEP].rearrange("p (c k) -> p c k", c=C)
        k_v = p_kv[:, 64:64 + C * KEEP].rearrange("p (c k) -> p c k", c=C)
        v_v = p_kv[:, 128:128 + GROUPS * HD].rearrange("p (g d) -> p g d", g=GROUPS)
        o_v = p_o[:, 0:NH * (HD + 1)].rearrange("p (g r d) -> p g r d", g=GROUPS, r=4)

        cst_in = sem("cst_in")
        w_in = sem("w_in")
        xall_in = sem("xall_in")
        x_in = [sem(f"x_in{j}") for j in range(2)]
        imp_done = sem("imp_done")
        setup = sem("setup")
        impT_done = sem("impT_done")
        mask_done = sem("mask_done")
        maskT_done = sem("maskT_done")
        maskT_copied = sem("maskT_copied")
        count_done = sem("count_done")
        pick_done = sem("pick_done")
        dve = sem("dve")
        gathered = sem("gathered")
        q_done = sem("q_done")
        q_out = sem("q_out")
        xsel_ready = sem("xsel_ready")
        kv_done = sem("kv_done")
        kv_out = sem("kv_out")
        s_done = sem("s_done")
        negm_ready = sem("negm_ready")
        n_done = sem("n_done")
        n_out = sem("n_out")
        z_ready = sem("z_ready")
        t_done = sem("t_done")
        p_ready = sem("p_ready")
        o_done = sem("o_done")
        attn_ready = sem("attn_ready")
        a_done = sem("a_done")
        aT_ready = sem("aT_ready")
        y_done = sem("y_done")
        xbo_ready = sem("xbo_ready")
        res_ready = sem("res_ready")
        mv_ready = sem("mv_ready")
        pool = sem("pool")
        rstd_ready = sem("rstd_ready")
        x1_ready = sem("x1_ready")
        out_sem = sem("out_sem")
        x1T_done = sem("x1T_done")
        x1q_ready = sem("x1q_ready")
        x1_stored = [sem(f"x1_stored{j}") for j in range(2)]
        ker_in = sem("ker_in")
        ker_zero = sem("ker_zero")
        ker_sum = sem("ker_sum")
        ker_out = sem("ker_out")
        head_in = [sem(f"head_in{j}") for j in range(2)]
        kv_made = sem("kv_made")
        conv_done = sem("conv_done")
        prod_done = sem("prod_done")
        sum_done = sem("sum_done")
        x1_back = [sem(f"x1_back{j}") for j in range(2)]
        convr_ready = sem("convr_ready")
        back_done = sem("back_done")
        res2_ready = sem("res2_ready")
        stats2 = sem("stats2")
        mv2_ready = sem("mv2_ready")
        rstd2_ready = sem("rstd2_ready")
        x2_ready = sem("x2_ready")
        x2T_done = sem("x2T_done")
        x2T_ready = sem("x2T_ready")
        logit_done = sem("logit_done")
        logit_ready = sem("logit_ready")
        x2all_in = sem("x2all_in")
        ffn_in = sem("ffn_in")
        zero_ready = sem("zero_ready")
        xsd_zeroed = sem("xsd_zeroed")
        route = sem("route")
        hot_ready = sem("hot_ready")
        rank_done = sem("rank_done")
        pos_ready = sem("pos_ready")
        owner_ready = sem("owner_ready")
        scattered = sem("scattered")
        wts_ready = sem("wts_ready")
        sg_ready = sem("sg_ready")
        sa_done = sem("sa_done")
        ssil_ready = sem("ssil_ready")
        sh_ready = sem("sh_ready")
        shT_done = sem("shT_done")
        shT_ready = sem("shT_ready")
        z_done = sem("z_done")
        z0_ready = sem("z0_ready")
        xsT_done = sem("xsT_done")
        xsT_ready = sem("xsT_ready")
        ab_done = sem("ab_done")
        sil_ready = sem("sil_ready")
        hid_ready = sem("hid_ready")
        hidT_done = sem("hidT_done")
        hidT_ready = sem("hidT_ready")
        ye_done = sem("ye_done")
        ys_ready = sem("ys_ready")
        fin = sem("fin")
        mv3_ready = sem("mv3_ready")
        ve3_ready = sem("ve3_ready")
        rs3_ready = sem("rs3_ready")
        out_ready = sem("out_ready")
        out_stored = sem("out_stored")
        w2_in = sem("w2_in")
        x2T_stored = [sem(f"x2T_stored{j}") for j in range(2)]
        x2T_in = [sem(f"x2T_in{j}") for j in range(2)]
        xs_in = [sem(f"xs_in{j}") for j in range(2)]
        ys_stored = [sem(f"ys_stored{j}") for j in range(2)]
        y_in = [sem(f"y_in{k}") for k in range(SLOTS)]
        x2_stored = [sem(f"x2_stored{j}") for j in range(2)]

        x_v = x.rearrange("b s d -> s b d")
        out_v = out.rearrange("b s d -> s b d")

        def steps(eng, step, n=B, first=2, last=2):
            for b in range(first):
                step(b, b % 2)
            with eng.Fori(0, (n - first - last) // 2) as i:
                for j in range(2):
                    step(i * 2 + (first + j), j)
            for b in range(n - last, n):
                step(b, b % 2)

        def at(ap, b):
            if known(b):
                return ap[b]
            names = "pqrs"[:len(ap.shape) - 1]
            part = ap[(bass.ds(b, 1),) + (slice(None),) * (len(ap.shape) - 1)]
            return part.rearrange(f"o {' '.join(names)} -> (o {names[0]}) {' '.join(names[1:])}")

        def one(b):
            return slice(b, b + 1) if known(b) else bass.ds(b, 1)

        def head_steps(eng, step, fresh=2):
            for h in range(2):
                for f in range(2):
                    step(h, f, h % 2)
            with eng.Fori(0, (HEADS - 2) // 2) as i:
                for j in range(2):
                    for f in range(2):
                        step(i * 2 + (2 + j), f, j)

        def known(b):
            return isinstance(b, int)

        block = ctx.enter_context(nc.Block())

        @block.sync
        def _(sp):
            sp.dma_start(cst[:, :], consts).then_inc(cst_in, 16)
            sp.dma_start(rowb[:, :, :], rows.rearrange("(o a) d -> o a d", o=1).to_broadcast([P, 3, D])).then_inc(cst_in, 16)
            sp.dma_start(colb[:, :], cols).then_inc(cst_in, 16)
            sp.dma_start(xall[:, :, :], x_v).then_inc(xall_in, 16)
            for w, a in ((wq, Wq), (wk, Wk), (wv, Wv), (wo, Wo)):
                sp.dma_start(w[:, :, :], a.rearrange("(c p) n -> p c n", p=P)).then_inc(w_in, 16)

            def load(b, j):
                if not (known(b) and b < 2):
                    sp.wait_ge(res_ready, b - 1)
                sp.dma_start(xr[j][:, :], at(x, b)).then_inc(x_in[j], 16)
                sp.dma_start(xTr[j][:, :, :], at(xT, b)).then_inc(x_in[j], 16)
                if not (known(b) and b < 3):
                    store(b - 3, 1 - j)

            def store(b, j):
                sp.wait_ge(x1_ready, b + 1)
                sp.dma_start(at(x1d, b), x1r[j][:, :]).then_inc(x1_stored[j], 16)
            steps(sp, load, first=4)
            for b in range(B - 3, B):
                store(b, b % 2)

            def load_head(h, j):
                if known(h) and h < 2:
                    if h == 0:
                        sp.wait_ge(ker_out, 16)
                else:
                    sp.wait_ge(kv_made, h * 2 - 2)
                    sp.wait_ge(conv_done, h * 2 - 2)
                sp.dma_start(ctxr[j][:, :, :, :], at(ctxd, h)).then_inc(head_in[j], 16)
                row = kerd[one(h), D - P + 1:D - P + 2]
                sp.dma_start(toe[j][:, :], bass.AP(row.tensor, row.offset, [[1, P], [1, 2 * P]])).then_inc(head_in[j], 16)
            steps(sp, load_head, n=HEADS, last=0)

            def load_x1(b, j):
                if not (known(b) and b < 2):
                    sp.wait_ge(res2_ready, b - 1)
                else:
                    sp.wait_ge(x1_stored[j], 8 * B)
                sp.dma_start(x1s[j][:, :], at(x1d, b)).then_inc(x1_back[j], 16)
                if not (known(b) and b < 3):
                    store_x2(b - 3, 1 - j)

            def store_x2(b, j):
                sp.wait_ge(x2_ready, b + 1)
                sp.dma_start(at(x2d, b), x2r[j][:, :]).then_inc(x2_stored[j], 16)
                sp.wait_ge(x2T_ready, b + 1)
                sp.dma_start(at(x2Td, b), x2T[j][:, :, :]).then_inc(x2T_stored[j], 16)
            steps(sp, load_x1, first=4)
            for b in range(B - 3, B):
                store_x2(b, b % 2)
            for j in range(2):
                sp.wait_ge(x2_stored[j], 8 * B)
                sp.wait_ge(x2T_stored[j], 8 * B)
            sp.dma_start(x2all[:, :, :], x2d.rearrange("b s d -> s b d")).then_inc(x2all_in, 16)

            def load_x2T(b, j):
                if known(b) and b < 2:
                    sp.wait_ge(logit_done, B)
                else:
                    sp.wait_ge(sa_done, b - 1)
                sp.dma_start(x2T[j][:, :, :], at(x2Td, b)).then_inc(x2T_in[j], 16)
            steps(sp, load_x2T)

            xs_v = xsd.rearrange("(t p) d -> t p d", p=P)
            ys_v = ysd.rearrange("(t p) d -> t p d", p=P)

            def load_tile(t, j):
                if known(t) and t < 2:
                    sp.wait_ge(scattered, 16 * NB)
                else:
                    sp.wait_ge(xsT_done, t - 1)
                sp.dma_start(xs[j][:, :], at(xs_v, t)).then_inc(xs_in[j], 16)
                if not (known(t) and t < 3):
                    store_tile(t - 3, 1 - j)

            def store_tile(t, j):
                sp.wait_ge(ys_ready, t + 1)
                sp.dma_start(at(ys_v, t), ys[j][:, :]).then_inc(ys_stored[j], 16)
            steps(sp, load_tile, n=NT, first=4, last=1)
            for t in range(NT - 3, NT):
                store_tile(t, t % 2)

            for k in range(0, B, SLOTS):
                sp.wait_ge(out_ready, k + SLOTS)
                sp.dma_start(out_v[:, k:k + SLOTS, :], x2all[:, k:k + SLOTS, :]).then_inc(out_stored, 16)
            sp.wait_ge(out_stored, 16 * (B // SLOTS))

        @block.tensor
        def _(pe):
            pe.wait_ge(cst_in, 48)
            pe.wait_ge(imp_done, 1)
            pe.transpose(p_y[0:B, 0:P], imp[:, :], ident).then_inc(impT_done, 1)
            pe.wait_ge(mask_done, 1)
            pe.transpose(p_s[:, 0:B], chosenT[:, :], cst[0:B, C_ID:C_ID + B]).then_inc(maskT_done, 1)
            pe.wait_ge(maskT_copied, 1)
            pe.matmul(p_o[:, 0:B], tri, chosen[:, :], start=True, stop=True).then_inc(count_done, 1)
            pe.wait_ge(w_in, 64)
            pe.wait_ge(pick_done, 1)
            pe.wait_ge(setup, 3)

            def p1(b, j):
                pe.wait_ge(x_in[j], 32 + 32 * (b // 2) if known(b) else (b - j) * 16 + 32)
                if not (known(b) and b < 1):
                    pe.wait_ge(kv_out, b)
                    pe.wait_ge(q_out, b)
                for c in range(C):
                    last = pe.matmul(g_v[:, c, :], xr[j][:, c * P:(c + 1) * P],
                                     pick[:, b, :] if known(b) else pick[:, bass.ds(b, 1), :].rearrange("p o k -> p (o k)"),
                                     start=True, stop=True)
                last.then_inc(gathered, 1)
                for m in range(C):
                    for c in range(C):
                        last = pe.matmul(p_q[:, m, 0:S], wq[:, c, m * P:(m + 1) * P], xTr[j][:, c, :],
                                         start=(c == 0), stop=(c == C - 1))
                last.then_inc(q_done, 1)

            def p2(b, j):
                pe.wait_ge(xsel_ready, b + 1)
                for m in range(C):
                    for c in range(C):
                        pe.matmul(k_v[:, m, :], wk[:, c, m * P:(m + 1) * P], xsel[:, c, :],
                                  start=(c == 0), stop=(c == C - 1))
                for r in range(4):
                    for c in range(C):
                        last = pe.matmul(v_v[32 * r:32 * r + 32, :, :], xsel[:, c, :],
                                         wv[:, c, :].rearrange("p (g r d) -> p r g d", g=GROUPS, r=4)[:, r],
                                         start=(c == 0), stop=(c == C - 1))
                last.then_inc(kv_done, 1)

            def p3(b, j):
                pe.wait_ge(kv_out, b + 1)
                pe.wait_ge(q_out, b + 1)
                if not (known(b) and b < 1):
                    pe.wait_ge(n_out, b)
                for c in range(C):
                    last = pe.matmul(p_s[:, c * 256:(c + 1) * 256], qT[j][:, c, :], kbd[j][:, c, :, :],
                                     start=True, stop=True)
                last.then_inc(s_done, 1)

            def p4(b, j):
                pe.wait_ge(negm_ready, b + 1)
                pe.transpose(p_s[0:NH, 0:S], negm[j][:, :], ident).then_inc(n_done, 1)

            def p5(b, j):
                pe.wait_ge(n_out, b + 1)
                for g in range(GROUPS):
                    pe.matmul(p_t[:, g, :], kbd[j][:, g // 2, (g % 2) * 4:(g % 2) * 4 + 4, :], qT[j][:, g // 2, :],
                              start=True, stop=False)
                    last = pe.matmul(p_t[:, g, :], cst[0:NH, C_E + g * P:C_E + (g + 1) * P], negT[:, :],
                                     start=False, stop=True)
                last.then_inc(t_done, 1)

            def p6(b, j):
                pe.wait_ge(p_ready, b + 1)
                for g in range(GROUPS):
                    last = pe.matmul(o_v[:, g, :, :], probs[:, g, :], vbd[j][:, g, :, :], start=True, stop=True)
                last.then_inc(o_done, 1)

            def p7(b, j):
                pe.wait_ge(attn_ready, b + 1)
                if not (known(b) and b < 1):
                    pe.wait_ge(res_ready, b)
                for c in range(C):
                    last = pe.transpose(p_y[:, c * P:(c + 1) * P], attn[:, c * P:(c + 1) * P], ident)
                last.then_inc(a_done, 1)

            def p8(b, j):
                pe.wait_ge(aT_ready, b + 1)
                for c in range(C):
                    last = pe.matmul(p_y[:, 256:512], attnT[:, c, :], wo[:, c, :], start=(c == 0), stop=(c == C - 1))
                last.then_inc(y_done, 1)

            for f in (p1, p2, p3, p4):
                f(0, 0)

            def p9(b, j):
                pe.wait_ge(x1_ready, b + 1)
                if not (known(b) and b < 1):
                    pe.wait_ge(x1q_ready, b)
                for c in range(C):
                    last = pe.transpose(p_x[:, c, :], x1r[j][:, c * P:(c + 1) * P], ident)
                last.then_inc(x1T_done, 1)

            def step(b, j):
                more = not (known(b) and b == B - 1)
                p5(b, j)
                if more:
                    p1(b + 1, 1 - j)
                p6(b, j)
                if more:
                    p2(b + 1, 1 - j)
                p7(b, j)
                if more:
                    p3(b + 1, 1 - j)
                p8(b, j)
                if more:
                    p4(b + 1, 1 - j)
                if not (known(b) and b < 1):
                    p9(b - 1, 1 - j)
            steps(pe, step)
            p9(B - 1, 1)

            def convolve(h, f, j):
                u = h * 2 + f
                pe.wait_ge(head_in[j], 32 + 32 * (h // 2) if known(h) else (h - j) * 16 + 32)
                pe.wait_ge(kv_made, u + 1)
                if not (known(h) and h < 1):
                    pe.wait_ge(prod_done, u - 1)
                k = [kv[f][:, c, :, :, :] for c in range(C)]
                pe.matmul(p_conv[f][0], toe[j][:, 0:P], k[0], start=True, stop=True)
                pe.matmul(p_conv[f][1], toe[j][:, P:2 * P], k[0], start=True, stop=False)
                pe.matmul(p_conv[f][1], toe[j][:, 0:P], k[1], start=False, stop=True).then_inc(conv_done, 1)
            pe.wait_ge(q_out, B)
            pe.wait_ge(negm_ready, B)
            pe.wait_ge(n_out, B)
            head_steps(pe, convolve)

            pe.wait_ge(ffn_in, 16 * 4)

            def route(b, j):
                pe.wait_ge(x2_ready, b + 1)
                if not (known(b) and b < 1):
                    pe.wait_ge(x2T_ready, b)
                for c in range(C):
                    last = pe.transpose(p_x[:, c, :], x2r[j][:, c * P:(c + 1) * P], ident)
                last.then_inc(x2T_done, 1)

            def score(b, j):
                pe.wait_ge(x2T_ready, b + 1)
                if not (known(b) and b < 1):
                    pe.wait_ge(logit_ready, b)
                for c in range(C):
                    last = pe.matmul(p_logit, x2T[j][:, c, :], gw[:, c, :], start=(c == 0), stop=(c == C - 1))
                last.then_inc(logit_done, 1)

            def turn_back(b, j):
                pe.wait_ge(convr_ready, b + 1)
                if not (known(b) and b < 1):
                    pe.wait_ge(res2_ready, b)
                for c in range(C):
                    last = pe.transpose(p_back[:, c * P:(c + 1) * P], convr[j][:, c, :], ident)
                last.then_inc(back_done, 1)
                if not (known(b) and b < 2):
                    score(b - 2, j)
                if not (known(b) and b < 1):
                    route(b - 1, 1 - j)
            steps(pe, turn_back, last=0)
            score(B - 2, 0)
            route(B - 1, 1)
            score(B - 1, 1)

            pe.wait_ge(hot_ready, 1)
            pe.matmul(p_rank, cst[:, C_STRI:C_STRI + P], hot[:, :, :], start=True, stop=True)
            pe.matmul(p_sum, cst[:, C_ONES:C_ONES + P], hot[:, :, :].rearrange("p n e -> p e n"), start=True, stop=True).then_inc(rank_done, 1)

            def shared_up(b, j):
                pe.wait_ge(x2T_in[j], 16 + 16 * (b // 2) if known(b) else (b - j) * 8 + 16)
                for k, p in enumerate((p_a, p_b)):
                    for c in range(C):
                        last = pe.matmul(p, x2T[j][:, c, :], sw13s[:, c, k * SI:(k + 1) * SI],
                                         start=(c == 0), stop=(c == C - 1))
                last.then_inc(sa_done, 1)

            def shared_turn(b, j):
                pe.wait_ge(sh_ready, b + 1)
                if not (known(b) and b < 1):
                    pe.wait_ge(shT_ready, b)
                for k, (lo, n) in enumerate(SP_):
                    last = pe.transpose(p_hT[0:n, k, :], sh[:, lo:lo + n], ident)
                last.then_inc(shT_done, 1)

            def shared_down(b, j):
                pe.wait_ge(shT_ready, b + 1)
                if not (known(b) and b < 1):
                    pe.wait_ge(z0_ready, b)
                for k, (lo, n) in enumerate(SP_):
                    last = pe.matmul(p_z, shT[0:n, k, :], sw2s[0:n, k, :], start=(k == 0), stop=(k == 2))
                last.then_inc(z_done, 1)

            shared_up(0, 0)

            def shared(b, j):
                shared_turn(b, j)
                if not (known(b) and b == B - 1):
                    shared_up(b + 1, 1 - j)
                shared_down(b, j)
            steps(pe, shared)

            pe.wait_ge(owner_ready, 1)
            pe.wait_ge(w2_in, 16)
            pe.wait_ge(z0_ready, B)

            def expert(t):
                return pe.value_load(owner[0:1, one(t)], min_val=0, max_val=E - 1)

            def turn_in(t, j):
                pe.wait_ge(xs_in[j], 16 + 16 * (t // 2) if known(t) else (t - j) * 8 + 16)
                if not (known(t) and t < 1):
                    pe.wait_ge(xsT_ready, t)
                for c in range(C):
                    last = pe.transpose(p_xs[:, c, :], xs[j][:, c * P:(c + 1) * P], ident)
                last.then_inc(xsT_done, 1)

            def up(t, j):
                e = expert(t)
                pe.wait_ge(xsT_ready, t + 1)
                for c in range(C):
                    last = pe.matmul(p_ab[j], xsT[j][:, c, :],
                                     w13s[:, c, bass.ds(e, 1), :].rearrange("p o n -> p (o n)"),
                                     start=(c == 0), stop=(c == C - 1))
                last.then_inc(ab_done, 1)

            def turn_mid(t, j):
                pe.wait_ge(hid_ready, t + 1)
                if not (known(t) and t < 1):
                    pe.wait_ge(hidT_ready, t)
                for k in range(2):
                    last = pe.transpose(p_hid[:, k, :], hid[j][:, k * KI:(k + 1) * KI], ident)
                last.then_inc(hidT_done, 1)

            def down(t, j):
                e = expert(t)
                pe.wait_ge(hidT_ready, t + 1)
                if not (known(t) and t < 1):
                    pe.wait_ge(ys_ready, t)
                for k in range(2):
                    last = pe.matmul(p_ye, hidT[j][:, k, :],
                                     w2s[:, bass.ds(e, 1), k, :].rearrange("p o n -> p (o n)"),
                                     start=(k == 0), stop=(k == 1))
                last.then_inc(ye_done, 1)

            turn_in(0, 0)
            up(0, 0)

            def tile(t, j):
                more = not (known(t) and t == NT - 1)
                if more:
                    turn_in(t + 1, 1 - j)
                turn_mid(t, j)
                if more:
                    up(t + 1, 1 - j)
                down(t, j)
            steps(pe, tile, n=NT, last=1)

        @block.vector
        def _(v):
            done = [0]

            def chain(ins):
                ins.then_inc(dve, 1)
                done[0] += 1
                v.wait_ge(dve, done[0])

            for j in range(2):
                last = v.memset(vbd[j][:, :, :, :], 0.0)
            last.then_inc(dve, 1)
            done[0] += 1
            v.wait_ge(dve, done[0])
            for j in range(2):
                for r in range(4):
                    last = v.memset(vbd[j][32 * r:32 * r + 32, :, r, HD:HD + 1], 1.0)
            last.then_inc(setup, 1)
            v.memset(half[:, 0:1], EPS)
            v.memset(half[:, 1:2], -0.5).then_inc(setup, 1)
            v.wait_ge(cst_in, 48)
            v.wait_ge(xall_in, 16)
            v.tensor_scalar(bqs[:, :], colb[:, 0:C], SCALE, None, ALU.mult).then_inc(setup, 1)
            for b in range(B):
                last = v.tensor_tensor_reduce(z0[:, b, :], xall[:, b, :], rowb[:, 0, :], 1.0, 0.0, ALU.mult, ALU.add,
                                              imp[:, b:b + 1])
            chain(last)
            v.tensor_scalar(imp[:, :], imp[:, :], colb[:, 4:5], None, ALU.add).then_inc(imp_done, 1)
            v.wait_ge(impT_done, 1)
            chain(v.tensor_copy(impT[:, 0, :], p_y[0:B, 0:P]))
            for n in range(4):
                chain(v.max(top8[:, n, :], impT[:, n, :]))
                chain(v.match_replace(impT[:, n + 1, :], top8[:, n, :], impT[:, n, :], NEG))
            v.tensor_scalar(chosenT[:, :], impT[:, 4, :], NEG, None, ALU.is_equal).then_inc(mask_done, 1)
            v.wait_ge(maskT_done, 1)
            v.tensor_copy(chosen[:, :], p_s[:, 0:B]).then_inc(maskT_copied, 1)
            v.wait_ge(maskT_copied, 1)
            v.wait_ge(count_done, 1)
            chain(v.tensor_tensor(place[:, :], chosen[:, :], p_o[:, 0:B], ALU.mult))
            v.tensor_tensor(pick[:, :, :], iota.rearrange("p (o k) -> p o k", o=1).to_broadcast([P, B, KEEP]),
                            place[:, :].rearrange("p (b o) -> p b o", o=1).to_broadcast([P, B, KEEP]),
                            ALU.is_equal).then_inc(pick_done, 1)
            links = done[0]

            def link(ins, b, n):
                ins.then_inc(dve, 1)
                return ins

            def d1(b, j):
                v.wait_ge(gathered, b + 1)
                v.tensor_copy(xsel[:, :, :], g_v).then_inc(xsel_ready, 1)

            def d2(b, j):
                v.wait_ge(kv_done, b + 1)
                for c in range(C):
                    v.scalar_tensor_tensor(out=kbd[j][:, c, :, :],
                                           in0=k_v[:, c, :].rearrange("p (o k) -> p o k", o=1).to_broadcast([P, 8, KEEP]),
                                           scalar=colb[:, C + c:C + c + 1],
                                           in1=headmask.rearrange("p (h o) -> p h o", o=1).to_broadcast([P, 8, KEEP]),
                                           op0=ALU.add, op1=ALU.mult)
                for r in range(4):
                    q = slice(32 * r, 32 * r + 32)
                    last = v.tensor_tensor(vbd[j][q, :, r, 0:HD], v_v[q, :, :],
                                           rowb[q, 2, :].rearrange("p (g r d) -> p r g d", g=GROUPS, r=4)[:, r],
                                           ALU.add)
                last.then_inc(kv_out, 1)

            def d3(b, j):
                v.wait_ge(s_done, b + 1)
                v.tensor_reduce(mx[:, :], p_s[:, :].rearrange("p (h k) -> p h k", k=KEEP), AX.X, ALU.max,
                                negate=True).then_inc(dve, 1)
                v.wait_ge(dve, links + (1 if known(b) and b == 0 else CH * b))
                v.tensor_scalar(negm[j][:, :], mx[:, :], 0.0, None, ALU.min).then_inc(negm_ready, 1)

            def d6(b, j):
                v.wait_ge(z_ready, b + 1)
                v.wait_ge(o_done, b + 1)
                ov = o_v.rearrange("p g r d -> p (g r) d")
                v.scalar_tensor_tensor(out=den[:, :], in0=zero_e[j][:, :], scalar=float(S - KEEP),
                                       in1=ov[:, :, HD], op0=ALU.mult, op1=ALU.add).then_inc(dve, 1)
                v.wait_ge(dve, links + 2 + CH * b)
                v.reciprocal(rec[:, :], den[:, :]).then_inc(dve, 1)
                v.wait_ge(dve, links + 3 + CH * b)
                v.tensor_tensor(attn[:, :].rearrange("p (h d) -> p h d", d=HD), ov[:, :, 0:HD],
                                rec[:, :].rearrange("p (h o) -> p h o", o=1).to_broadcast([P, NH, HD]),
                                ALU.mult).then_inc(attn_ready, 1)

            def d8(b, j):
                more = not (known(b) and b == B - 1)
                v.wait_ge(xbo_ready, b + 1)
                v.wait_ge(y_done, b + 1)
                v.tensor_tensor(res[j][:, :], p_y[:, 256:512], xbo[j][:, :], ALU.add).then_inc(res_ready, 1)
                v.wait_ge(res_ready, b + 1)
                v.bn_stats(stats[:, :], res[j][:, :]).then_inc(dve, 1)
                n = 4 + (1 if more else 0)
                v.wait_ge(dve, links + n + CH * b)
                if not (known(b) and b == 0):
                    d9(b - 1, 1 - j)
                v.bn_aggr(mv[j][:, :], stats[:, :]).then_inc(mv_ready, 1)

            def d9(b, j):
                v.wait_ge(rstd_ready, b + 1)
                if not (known(b) and b < 2):
                    v.wait_ge(x1_stored[j], (b - j) * 8)
                v.tensor_scalar(x1r[j][:, :], res[j][:, :], mv[j][:, 0:1], rstd[j][:, 0:1], ALU.subtract,
                                ALU.mult).then_inc(x1_ready, 1)

            CH = 4
            d1(0, 0)
            d2(0, 0)
            d3(0, 0)

            def step(b, j):
                more = not (known(b) and b == B - 1)
                if more:
                    d1(b + 1, 1 - j)
                d6(b, j)
                if more:
                    d2(b + 1, 1 - j)
                    d3(b + 1, 1 - j)
                d8(b, j)
            steps(v, step)
            d9(B - 1, 1)

            def window(ap, n):
                return bass.AP(ap.tensor, ap.offset, [list(ap.ap[0]), [WRAP, BH], [1, n], [1, HEAD]])

            def products(h, f, j):
                u = h * 2 + f
                v.wait_ge(conv_done, u + 1)
                if not (known(h) and h < 1):
                    v.wait_ge(sum_done, u - 1)
                if not (known(h) and u == 0):
                    v.wait_ge(prod_done, u)
                for c in range(C):
                    q = x1q[:, one(h), c, f * BH:(f + 1) * BH, 0:HEAD]
                    y = p_conv[f][c].rearrange("p (b d i) -> p b d i", b=BH, d=DIAG)
                    v.tensor_tensor(prod[f][c][:, :, 0:DIAG, :], y, window(q, DIAG), ALU.mult)
                    o = prod[f][c][:, :, :, :]
                    o = bass.AP(o.tensor, o.offset + DIAG * HEAD + 1, [list(o.ap[0]), [ROWS * HEAD, BH],
                                                                      [2 * HEAD + 1, 3], [1, HEAD]])
                    qq = bass.AP(q.tensor, q.offset, [list(q.ap[0]), [WRAP, BH], [0, 3], [1, HEAD]])
                    last = v.tensor_tensor(o, y[:, :, 1:4, :], qq, ALU.mult)
                last.then_inc(prod_done, 1)

            def sums(h, f, j):
                for c in range(C):
                    dst = conv[:, f * BH:(f + 1) * BH, c, h * HEAD:(h + 1) * HEAD] if known(h) else \
                        conv[:, f * BH:(f + 1) * BH, c, bass.ds(h * HEAD, HEAD)]
                    last = v.tensor_reduce(dst, prod[f][c][:, :, :, :].rearrange("p b s i -> p b i s"), AX.X, ALU.add)
                last.then_inc(sum_done, 1)

            for j in range(2):
                for c in range(C):
                    last = v.memset(prod[j][c][:, :, :, :], 0.0)
            last.then_inc(setup, 1)
            v.wait_ge(setup, 4)
            v.wait_ge(x1q_ready, B)

            def step(h, f, j):
                products(h, f, j)
                if f == 1:
                    sums(h, 0, j)
                elif not (known(h) and h == 0):
                    sums(h - 1, 1, 1 - j)
            head_steps(v, step)
            v.wait_ge(prod_done, 2 * HEADS)
            sums(HEADS - 1, 1, 1)

            def second(b, j):
                v.wait_ge(x1_back[j], 16 + 16 * (b // 2) if known(b) else (b - j) * 8 + 16)
                v.wait_ge(back_done, b + 1)
                if not (known(b) and b < 2):
                    v.wait_ge(x2_ready, b - 1)
                v.tensor_tensor(res2[j][:, :], p_back, x1s[j][:, :], ALU.add).then_inc(res2_ready, 1)
                v.wait_ge(res2_ready, b + 1)
                v.bn_stats(stats[:, :], res2[j][:, :]).then_inc(stats2, 1)
                v.wait_ge(stats2, b + 1)
                if known(b) and b == 0:
                    v.bn_aggr(mv[j][:, :], stats[:, :]).then_inc(mv2_ready, 1)
                else:
                    x2(b - 1, 1 - j)
                    v.bn_aggr(mv[j][:, :], stats[:, :]).then_inc(mv2_ready, 1)

            def x2(b, j):
                v.wait_ge(rstd2_ready, b + 1)
                if not (known(b) and b < 2):
                    v.wait_ge(x2_stored[j], (b - j) * 8)
                v.tensor_scalar(x2r[j][:, :], res2[j][:, :], mv[j][:, 0:1], rstd[j][:, 0:1], ALU.subtract,
                                ALU.mult).then_inc(x2_ready, 1)

            def scores_out(b, j):
                v.wait_ge(logit_done, b + 1)
                if known(b):
                    v.tensor_copy(logit[:, b, :], p_logit).then_inc(logit_ready, 1)
                else:
                    v.tensor_scalar(logit[:, one(b), :].rearrange("p o e -> p (o e)"), p_logit, 1.0, None,
                                    ALU.mult).then_inc(logit_ready, 1)
            def second_step(b, j):
                second(b, j)
                if not (known(b) and b < 3):
                    scores_out(b - 3, 1 - j)
            steps(v, second_step, first=4)
            x2(B - 1, 1)
            for b in range(B - 3, B):
                scores_out(b, b % 2)

            n = [0]

            def then(ins):
                ins.then_inc(route, 1)
                n[0] += 1
                v.wait_ge(route, n[0])
            v.wait_ge(logit_ready, B)
            for b in range(B):
                last = v.max(best[:, b, :], logit[:, b, :])
            then(last)
            for b in range(B):
                last = v.max_index(bestix[:, b, :], best[:, b, :], logit[:, b, :])
            then(last)
            then(v.tensor_copy(ixf[:, :].rearrange("p (b k) -> p b k", k=TOP), bestix[:, :, 0:TOP]))
            v.tensor_tensor(hot[:, :, :],
                            cst[:, C_N:C_N + E].rearrange("p (o e) -> p o e", o=1).to_broadcast([P, NB, E]),
                            ixf[:, :].rearrange("p (n o) -> p n o", o=1).to_broadcast([P, NB, E]),
                            ALU.is_equal).then_inc(hot_ready, 1)
            v.wait_ge(hot_ready, 1)
            v.wait_ge(rank_done, 1)
            then(v.tensor_tensor_scan(upto[:, :, :].rearrange("p e n -> p (e n)"),
                                      cst[:, C_NEW:C_NEW + E * NB], p_sum, 0.0, ALU.mult, ALU.add))
            then(v.tensor_tensor(over[:, :, :],
                                 upto[:, :, NB - 1:NB].to_broadcast([P, E, 16]),
                                 cst[:, C_M:C_M + 16].rearrange("p (o m) -> p o m", o=1).to_broadcast([P, E, 16]),
                                 ALU.is_gt))
            then(v.tensor_reduce(tiles[:, :], over[:, :, :], AX.X, ALU.add))
            then(v.tensor_tensor_scan(endt[:, :], cst[:, C_ONES:C_ONES + E], tiles[:, :], 0.0, ALU.mult, ALU.add))
            then(v.tensor_tensor(base[:, :], endt[:, :], tiles[:, :], ALU.subtract))
            then(v.tensor_tensor(slot[:, :, :], upto[:, :, :].rearrange("p e n -> p n e"),
                                 p_sum.rearrange("p (e n) -> p n e", e=E), ALU.subtract))
            then(v.tensor_tensor(slot[:, :, :], slot[:, :, :], p_rank.rearrange("p (n e) -> p n e", e=E), ALU.add))
            then(v.tensor_scalar(base[:, :], base[:, :], float(P), None, ALU.mult))
            then(v.tensor_tensor(slot[:, :, :], slot[:, :, :],
                                 base[:, :].rearrange("p (o e) -> p o e", o=1).to_broadcast([P, NB, E]), ALU.add))
            then(v.tensor_tensor(slot[:, :, :], slot[:, :, :], hot[:, :, :], ALU.mult))
            then(v.tensor_reduce(posf[:, :], slot[:, :, :], AX.X, ALU.add))
            v.tensor_copy(pos[:, :], posf[:, :]).then_inc(pos_ready, 1)
            then(v.tensor_tensor(ended[:, :, :],
                                 endt[0:1, :].rearrange("p (o e) -> p o e", o=1).to_broadcast([1, NT, E]),
                                 cst[0:1, C_N:C_N + NT].rearrange("p (t o) -> p t o", o=1).to_broadcast([1, NT, E]),
                                 ALU.is_le))
            then(v.tensor_reduce(ownf[:, :], ended[:, :, :], AX.X, ALU.add))
            v.tensor_scalar(owner[:, :], ownf[:, :], float(E - 1), None, ALU.min).then_inc(owner_ready, 1)
            v.wait_ge(sg_ready, 1)
            then(v.tensor_tensor(sgsum[:, :], sg[:, :, 0], sg[:, :, 1], ALU.add))
            then(v.reciprocal(sgsum[:, :], sgsum[:, :]))
            v.tensor_tensor(wts[:, :, :], sg[:, :, :],
                            sgsum[:, :].rearrange("p (b o) -> p b o", o=1).to_broadcast([P, B, TOP]),
                            ALU.mult).then_inc(wts_ready, 1)
            v.wait_ge(x2all_in, 16)

            def shared_h(b, j):
                v.wait_ge(ssil_ready, b + 1)
                v.tensor_tensor(sh[:, :], ssil[:, :], p_b, ALU.mult).then_inc(sh_ready, 1)

            def shared_z(b, j):
                v.wait_ge(z_done, b + 1)
                v.tensor_tensor(z0[:, one(b), :].rearrange("p o d -> p (o d)"), p_z,
                                x2all[:, one(b), :].rearrange("p o d -> p (o d)"), ALU.add).then_inc(z0_ready, 1)
            shared_h(0, 0)

            def shared(b, j):
                if not (known(b) and b == B - 1):
                    shared_h(b + 1, 1 - j)
                shared_z(b, j)
            steps(v, shared)

            def hidden(t, j):
                v.wait_ge(sil_ready, t + 1)
                v.tensor_tensor(hid[j][:, :], sil[j][:, :], p_ab[j][:, I:2 * I], ALU.mult).then_inc(hid_ready, 1)

            def y_out(t, j):
                v.wait_ge(ye_done, t + 1)
                if not (known(t) and t < 2):
                    v.wait_ge(ys_stored[j], (t - j) * 8)
                v.tensor_copy(ys[j][:, :], p_ye).then_inc(ys_ready, 1)
            hidden(0, 0)

            def tile(t, j):
                if not (known(t) and t == NT - 1):
                    hidden(t + 1, 1 - j)
                y_out(t, j)
            steps(v, tile, n=NT, last=1)

            v.wait_ge(wts_ready, 1)
            m = [0]

            def four(k, f):
                for b in range(k, k + SLOTS):
                    f(b).then_inc(fin, 1)
                    m[0] += 1
                v.wait_ge(fin, m[0])
            for k in range(0, B, SLOTS):
                for s_ in range(SLOTS):
                    v.wait_ge(y_in[s_], 32 * (k // SLOTS + 1))
                for i in range(TOP):
                    four(k, lambda b: v.scalar_tensor_tensor(out=z0[:, b, :], in0=yg[b - k][:, i, :],
                                                             scalar=wts[:, b, i:i + 1], in1=z0[:, b, :],
                                                             op0=ALU.mult, op1=ALU.add))
                four(k, lambda b: v.bn_stats(st3[:, b, :], z0[:, b, :]))
                for b in range(k, k + SLOTS):
                    last = v.bn_aggr(mv3[:, b, :], st3[:, b, :])
                last.then_inc(mv3_ready, 1)
                v.wait_ge(rs3_ready, k // SLOTS + 1)
                for b in range(k, k + SLOTS):
                    v.tensor_scalar(x2all[:, b, :], z0[:, b, :], mv3[:, b, 0:1], rs3[:, b:b + 1], ALU.subtract,
                                    ALU.mult).then_inc(out_ready, 1)

        @block.scalar
        def _(a):
            a.wait_ge(setup, 3)

            def a1(b, j):
                a.wait_ge(q_done, b + 1)
                for c in range(C):
                    last = a.activation(qT[j][:, c, :], p_q[:, c, 0:S], ACT.Identity, bias=bqs[:, c:c + 1], scale=SCALE)
                last.then_inc(q_out, 1)

            def a4(b, j):
                a.wait_ge(n_done, b + 1)
                a.copy(negT[:, :], p_s[0:NH, 0:S]).then_inc(n_out, 1)
                a.activation(zero_e[j][:, :], negm[j][:, :], ACT.Exp).then_inc(z_ready, 1)

            def a5(b, j):
                a.wait_ge(t_done, b + 1)
                if not (known(b) and b < 2):
                    a.wait_ge(x1T_done, b - 1)
                a.activation(probs[:, :, :], p_t[:, :, :], ACT.Exp).then_inc(p_ready, 1)
                if not (known(b) and b < 2):
                    a9(b - 2)

            def a9(b):
                for lo, n in ((0, HEAD), (HEAD, WRAP - HEAD)):
                    last = a.copy(x1q[:, :, :, one(b), lo:lo + n].rearrange("p h c o i -> p c h (o i)"),
                                  p_x[:, :, :].rearrange("p c (h i) -> p c h i", i=HEAD)[:, :, :, 0:n])
                last.then_inc(x1q_ready, 1)

            def a7(b, j):
                a.wait_ge(a_done, b + 1)
                a.copy(attnT[:, :, :], p_y[:, 0:256].rearrange("p (c s) -> p c s", c=C)).then_inc(aT_ready, 1)

            a1(0, 0)
            a4(0, 0)

            def step(b, j):
                more = not (known(b) and b == B - 1)
                a5(b, j)
                if more:
                    a1(b + 1, 1 - j)
                a7(b, j)
                if more:
                    a4(b + 1, 1 - j)
            steps(a, step)
            for b in (B - 2, B - 1):
                a.wait_ge(x1T_done, b + 1)
                a9(b)

            a.wait_ge(sum_done, 2 * HEADS)

            def fetch(b, j):
                if not (known(b) and b < 2):
                    a.wait_ge(back_done, b - 1)
                if known(b):
                    a.copy(convr[j][:, :, :], conv[:, b, :, :]).then_inc(convr_ready, 1)
                else:
                    a.copy(convr[j][:, :, :], conv[:, bass.ds(b, 1), :, :].rearrange("p o c s -> p (o c) s")).then_inc(convr_ready, 1)
                if not (known(b) and b < 2):
                    x2T_copy(b - 2, j)

            def x2T_copy(b, j):
                a.wait_ge(x2T_done, b + 1)
                if not (known(b) and b < 2):
                    a.wait_ge(x2T_stored[j], (b - j) * 8)
                a.copy(x2T[j][:, :, :], p_x[:, :, :]).then_inc(x2T_ready, 1)
            steps(a, fetch)
            for b in (B - 2, B - 1):
                x2T_copy(b, b % 2)
            a.wait_ge(route, 1)
            a.activation(sg[:, :, :], best[:, :, 0:TOP], ACT.Sigmoid).then_inc(sg_ready, 1)

            def shared_silu(b, j):
                a.wait_ge(sa_done, b + 1)
                a.activation(ssil[:, :], p_a, ACT.Silu).then_inc(ssil_ready, 1)

            def shared_hT(b, j):
                a.wait_ge(shT_done, b + 1)
                a.copy(shT[:, 0:2, :], p_hT[:, 0:2, :])
                a.copy(shT[0:SP_[2][1], 2, :], p_hT[0:SP_[2][1], 2, :]).then_inc(shT_ready, 1)
            shared_silu(0, 0)

            def shared(b, j):
                shared_hT(b, j)
                if not (known(b) and b == B - 1):
                    shared_silu(b + 1, 1 - j)
            steps(a, shared)

            def xsT_copy(t, j):
                a.wait_ge(xsT_done, t + 1)
                a.copy(xsT[j][:, :, :], p_xs[:, :, :]).then_inc(xsT_ready, 1)

            def silu(t, j):
                a.wait_ge(ab_done, t + 1)
                a.activation(sil[j][:, :], p_ab[j][:, 0:I], ACT.Silu).then_inc(sil_ready, 1)

            def hidT_copy(t, j):
                a.wait_ge(hidT_done, t + 1)
                a.copy(hidT[j][:, :, :], p_hid).then_inc(hidT_ready, 1)
            xsT_copy(0, 0)
            silu(0, 0)

            def tile(t, j):
                more = not (known(t) and t == NT - 1)
                if more:
                    xsT_copy(t + 1, 1 - j)
                hidT_copy(t, j)
                if more:
                    silu(t + 1, 1 - j)
            steps(a, tile, n=NT, last=1)

        @block.gpsimd
        def _(g):
            g.memset(kerp[:, :], 0.0).then_inc(ker_zero, 1)
            g.wait_ge(ker_zero, 1)
            g.dma_start(kerp[:, D:2 * D], ker).then_inc(ker_in, 16)
            g.dma_start(skipc[:, :], skip).then_inc(ker_in, 16)
            g.wait_ge(ker_in, 32)
            g.tensor_tensor(kerp[:, D:D + 1], kerp[:, D:D + 1], skipc[:, :], ALU.add).then_inc(ker_sum, 1)
            g.wait_ge(ker_sum, 1)
            g.dma_start(kerd, kerp[:, :]).then_inc(ker_out, 16)
            g.memset(zeros[:, :], 0.0).then_inc(zero_ready, 1)
            g.wait_ge(zero_ready, 1)
            g.dma_start(xsd.rearrange("(p t) d -> p t d", p=P),
                        zeros[:, :].rearrange("p (o d) -> p o d", o=1).to_broadcast([P, NT, D])).then_inc(xsd_zeroed, 16)
            g.dma_start(gw[:, :, :], gate).then_inc(ffn_in, 16)
            g.dma_start(w13s[:, :, :, :], w13).then_inc(ffn_in, 16)
            g.dma_start(sw13s[:, :, :], sw13).then_inc(ffn_in, 16)
            g.dma_start(sw2s[:, :, :], sw2).then_inc(ffn_in, 16)
            g.wait_ge(setup, 3)

            def step(b, j):
                g.wait_ge(x_in[j], 32 + 32 * (b // 2) if known(b) else (b - j) * 16 + 32)
                if not (known(b) and b < 2):
                    g.wait_ge(res_ready, b - 1)
                g.tensor_tensor(xbo[j][:, :], xr[j][:, :], rowb[:, 1, :], ALU.add).then_inc(xbo_ready, 1)
                if not (known(b) and b < 1):
                    norm(b - 1, 1 - j)

            def norm(b, j):
                g.wait_ge(mv_ready, b + 1)
                g.tensor_tensor(vare[:, :], mv[j][:, 1:2], half[:, 0:1], ALU.add).then_inc(pool, 1)
                g.wait_ge(pool, b + 1)
                g.tensor_tensor(rstd[j][:, :], vare[:, :], half[:, 1:2], ALU.pow).then_inc(rstd_ready, 1)
            steps(g, step)
            norm(B - 1, 1)

            def multiply(h, f, j):
                u = h * 2 + f
                g.wait_ge(head_in[j], 32 + 32 * (h // 2) if known(h) else (h - j) * 16 + 32)
                if not (known(h) and h < 1):
                    g.wait_ge(conv_done, u - 1)
                for c in range(C):
                    k = ctxr[j][:, c, f * BH:(f + 1) * BH, 0:HEAD]
                    a0 = bass.AP(k.tensor, k.offset, [list(k.ap[0]), [WRAP, BH], [0, DIAG], [1, HEAD]])
                    a1 = bass.AP(k.tensor, k.offset, [list(k.ap[0]), [WRAP, BH], [1, DIAG], [1, HEAD]])
                    last = g.tensor_tensor(kv[f][:, c, :, :, :], a0, a1, ALU.mult)
                last.then_inc(kv_made, 1)
            head_steps(g, multiply)

            g.wait_ge(sum_done, 2 * HEADS)
            g.dma_start(w2s, w2).then_inc(w2_in, 16)

            def norm2(b, j):
                g.wait_ge(mv2_ready, b + 1)
                g.tensor_tensor(vare[:, :], mv[j][:, 1:2], half[:, 0:1], ALU.add).then_inc(pool, 1)
                g.wait_ge(pool, B + b + 1 if known(b) else b + (B + 1))
                g.tensor_tensor(rstd[j][:, :], vare[:, :], half[:, 1:2], ALU.pow).then_inc(rstd2_ready, 1)
            steps(g, norm2)

            def norm3(k):
                r = slice(k * SLOTS, (k + 1) * SLOTS)
                g.wait_ge(mv3_ready, k + 1)
                g.tensor_tensor(ve3[:, r], mv3[:, r, 1], half[:, 0:1].to_broadcast([P, SLOTS]), ALU.add
                                ).then_inc(ve3_ready, 1)
                g.wait_ge(ve3_ready, k + 1)
                g.tensor_tensor(rs3[:, r], ve3[:, r], half[:, 1:2].to_broadcast([P, SLOTS]), ALU.pow
                                ).then_inc(rs3_ready, 1)

            g.wait_ge(xsd_zeroed, 16)
            g.wait_ge(x2all_in, 16)
            g.wait_ge(pos_ready, 1)
            for n in range(NB):
                g.indirect_dma_start(xsd, bass.IndirectOffsetOnAxis(pos[:, n:n + 1], 0), x2all[:, n // TOP, :], None
                                     ).then_inc(scattered, 16)
            for j in range(2):
                g.wait_ge(ys_stored[j], 16 * ((NT + 1 - j) // 2))
            for b in range(B):
                if b >= SLOTS:
                    g.wait_ge(fin, b // SLOTS * 3 * SLOTS - SLOTS)
                for i in range(TOP):
                    g.indirect_dma_start(yg[b % SLOTS][:, i, :], None, ysd,
                                         bass.IndirectOffsetOnAxis(pos[:, b * TOP + i:b * TOP + i + 1], 0)
                                         ).then_inc(y_in[b % SLOTS], 16)
                if b % SLOTS == SLOTS - 1 and b > SLOTS:
                    norm3(b // SLOTS - 1)
            norm3(B // SLOTS - 1)


def tables():
    import numpy as np
    t = np.zeros((P, C_W), np.float32)
    i = np.arange(P)
    t[:, C_ID:C_ID + P] = np.eye(P)
    t[:, C_TRI:C_TRI + P] = i[:, None] <= i[None, :]
    t[:, C_IOTA:C_IOTA + KEEP] = np.arange(1, KEEP + 1)
    t[:, C_HM:C_HM + 8] = i[:, None] // HD == np.arange(8)[None, :]
    t[:, C_ONES:C_ONES + P] = 1.0
    e = np.arange(GROUPS * P)
    t[:, C_STRI:C_STRI + P] = i[:, None] < i[None, :]
    t[:, C_N:C_N + 64] = np.arange(64)
    t[:, C_M:C_M + 16] = np.arange(16) * P
    t[:, C_NEW:C_NEW + E * NB] = np.arange(E * NB) % NB != 0
    t[0:NH, C_E:C_E + GROUPS * P] = np.arange(NH)[:, None] == (e // P * 4 + e % P // KEEP)[None, :]
    return t


def kernel(**inputs):
    import numpy as np
    import concourse.bacc as bacc
    from concourse.bass_utils import run_bass_kernel_spmd

    nc = bacc.Bacc("TRN2", target_bir_lowering=False, num_devices=1)
    a = {k: np.asarray(v) for k, v in inputs.items()}
    x = a["x"]
    bq, bk, bi = a["L0_attn_bq"], a["L0_attn_bk"], a["L0_attn_bi"]
    arrays = {
        "x": x,
        "xT": np.ascontiguousarray(x.reshape(B, S, C, P).transpose(0, 3, 2, 1)),
        "ctx": np.ascontiguousarray(np.take(
            a["ctx_2048"].reshape(B, HEADS, HEAD, C, P)[:, :, :, :, ::-1], np.arange(WRAP) % HEAD, axis=2
        ).transpose(1, 4, 3, 0, 2)),
        "ker": a["L0_xattn_ssm_kernel"],
        "skip": a["L0_xattn_D"].reshape(HEADS, 1),
        "Wq": a["L0_attn_Wq"], "Wk": a["L0_attn_Wk"], "Wv": a["L0_attn_Wv"], "Wo": a["L0_attn_Wo"],
        "cols": np.ascontiguousarray(np.concatenate([bq.reshape(C, P).T, bk.reshape(C, P).T,
                                                     np.broadcast_to(bi, (P, 1))], axis=1)),
        "rows": np.stack([a["L0_attn_Wi"].reshape(-1), a["L0_attn_bo"], a["L0_attn_bv"]]),
        "consts": tables(),
        "gate": np.ascontiguousarray(a["L0_ffn_gate_w"].T.reshape(C, P, E).transpose(1, 0, 2)),
        "w13": np.ascontiguousarray(np.concatenate([a["L0_ffn_w1"], a["L0_ffn_w3"]], axis=1)
                                    .reshape(E, 2 * I, C, P).transpose(3, 2, 0, 1)),
        "w2": np.ascontiguousarray(a["L0_ffn_w2"].reshape(E, D, 2, KI).transpose(3, 0, 2, 1)),
        "sw13": np.ascontiguousarray(np.concatenate([a["L0_ffn_sw1"], a["L0_ffn_sw3"]], axis=0)
                                     .reshape(2 * SI, C, P).transpose(2, 1, 0)),
        "sw2": np.ascontiguousarray(np.pad(a["L0_ffn_sw2"], ((0, 0), (0, 3 * P - SI))).reshape(D, 3, P)
                                    .transpose(2, 1, 0)),
    }
    args = [nc.dram_tensor(f"in_{n}_dram", v.shape, mybir.dt.from_np(v.dtype), kind="ExternalInput").ap()
            for n, v in arrays.items()]
    out = nc.dram_tensor("out_0_dram", (B, S, D), F32, kind="ExternalOutput").ap()
    decoder_layer(nc, *args, out)
    r = run_bass_kernel_spmd(nc, [{f"in_{n}_dram": v for n, v in arrays.items()}], core_ids=[0])
    return r.results[0]["out_0_dram"]
```

```python
from contextlib import ExitStack

import concourse.bass as bass
from concourse import mybir

F32 = mybir.dt.float32
BF16 = mybir.dt.bfloat16
U32 = mybir.dt.uint32
ALU = mybir.AluOpType
ACT = mybir.ActivationFunctionType
AX = mybir.AxisListType

P = 128
B, S, D = 16, 128, 256
C = D // P
NH, HD = 16, 16
KEEP = 32
GROUPS = NH // 4
EPS = 1e-5
SCALE = HD ** -0.5
NEG = -3.0e38
HEADS, HEAD = 16, 8
DIAG = HEAD // 2 + 1
WRAP = HEAD + DIAG - 1
BH = B // 2
E, TOP, I = 16, 2, 176
KI = I // 2
SI = 2 * I
SP_ = [(0, P), (P, P), (2 * P, SI - 2 * P)]
NB = B * TOP
NT = NB + E - 1
FIRST, TURN = 3, 8
NG = (NT - FIRST - 4) // TURN
ROW = D + 2
ROWS = DIAG + 2 * 3
BY_PE = 4

C_ID, C_TRI, C_IOTA, C_HM, C_ONES, C_N = 0, 128, 256, 288, 296, 424
C_M = C_N + 64
C_NEW = C_M + 16
C_PAIR = C_NEW + E * NB
C_W = C_PAIR + NB + 2


B_STRI = P + GROUPS * P
B_ONES = B_STRI + P
B_W = B_ONES + P


def decoder_layer(nc, x, constb, xT, ctxd, ker, skip, Wq, Wk, Wv, Wo, cols, rows, consts, gate, w13, w2, sw13, sw2, out):
    with ExitStack() as ctx:
        def sb(name, shape, dt=F32):
            return ctx.enter_context(nc.sbuf_tensor(name, shape, dt))

        def ps(name, shape, dt=F32):
            return ctx.enter_context(nc.psum_tensor(name, shape, dt))

        def sem(name):
            return ctx.enter_context(nc.semaphore(name))

        cst = sb("cst", [P, C_W])
        cstb = sb("cstb", [P, B_W], BF16)
        identb = cstb[:, 0:P]
        headrow = cstb[0:2 * NH, P:P + GROUPS * P]
        ident = cst[:, C_ID:C_ID + P]
        tri = cst[:, C_TRI:C_TRI + P]
        iota = cst[:, C_IOTA:C_IOTA + KEEP]
        headmask = cst[:, C_HM:C_HM + 8]
        roomy = sb("roomy", [P, E * 2 * D])
        wq, wk, wv, wo = (roomy[:, k * C * D:(k + 1) * C * D].rearrange("p (c n) -> p c n", c=C) for k in range(4))
        colb = sb("colb", [P, 5])
        bqs = sb("bqs", [P, C])
        rowb = sb("rowb", [P, 3, D])
        xall = sb("xall", [P, B, ROW])
        imp = sb("imp", [P, B])
        
        impT = sb("impT", [B, 5, P])
        top8 = sb("top8", [B, 4, 8])
        chosenT = sb("chosenT", [B, P])
        chosen = sb("chosen", [P, B])
        place = sb("place", [P, B])
        pick = sb("pick", [P, B, KEEP])
        half = sb("half", [P, 2])

        xbo = [sb(f"xbo{j}", [P, D]) for j in range(2)]
        qT = [sb(f"qT{j}", [P, C, S]) for j in range(2)]
        kbd = [sb(f"kbd{j}", [P, C, 8, KEEP]) for j in range(2)]
        neg2 = [sb(f"neg2{j}", [P, 2, NH], BF16) for j in range(2)]
        negm = [sb(f"negm{j}", [P, NH]) for j in range(2)]
        zero_e = [sb(f"zero_e{j}", [P, NH]) for j in range(2)]
        mx = sb("mx", [P, NH])
        negT = sb("negT", [2 * NH, S], BF16)
        probs = sb("probs", [P, GROUPS, S])
        den = sb("den", [P, NH])
        rec = sb("rec", [P, NH])
        attn = sb("attn", [P, D])
        attnT = sb("attnT", [P, C, S])
        res = [sb(f"res{j}", [P, D]) for j in range(2)]
        stats = sb("stats", [P, 6])
        mv = [sb(f"mv{j}", [P, 2]) for j in range(2)]
        vare = sb("vare", [P, 1])
        rstd = [sb(f"rstd{j}", [P, 1]) for j in range(2)]

        x1r = [sb(f"x1r{j}", [P, D]) for j in range(2)]
        x1q = roomy[:, 4 * C * D:4 * C * D + HEADS * C * B * WRAP].rearrange(
            "p (h c b w) -> p h c b w", h=HEADS, c=C, b=B)
        kerp = sb("kerp", [HEADS, 2 * D])
        skipc = sb("skipc", [HEADS, 1])
        ctxr = [sb(f"ctxr{j}", [P, C, B, WRAP]) for j in range(2)]
        toe = [sb(f"toe{j}", [P, 2 * P]) for j in range(2)]
        NKV, NPR = BH * DIAG * HEAD, BH * ROWS * HEAD
        room = sb("room", [P, 2 * C * (NKV + NPR)])
        kv = [room[:, j * C * NKV:(j + 1) * C * NKV].rearrange("p (c b d i) -> p c b d i", c=C, b=BH, d=DIAG)
              for j in range(2)]
        prod = [room[:, 2 * C * NKV + j * C * NPR:2 * C * NKV + (j + 1) * C * NPR].rearrange(
            "p (c b s i) -> p c b s i", c=C, b=BH, s=ROWS) for j in range(2)]
        VBN = B * NH * (HD + 1)
        shared_room = sb("shared_room", [P, VBN + 2 * C * B * KEEP])
        vbd = shared_room[:, 0:VBN].rearrange("p (b g r d) -> p b g r d", b=B, g=GROUPS, r=4)
        xsel = shared_room[:, VBN:VBN + C * B * KEEP].rearrange("p (c n) -> p c n", c=C)
        keyT = shared_room[:, VBN + C * B * KEEP:VBN + 2 * C * B * KEEP].rearrange("p (c n) -> p c n", c=C)
        conv = [shared_room[:, j * D:(j + 1) * D].rearrange("p (c f b i) -> p c f b i", c=C, f=2, b=BH) for j in range(2)]
        part = [sb(f"part{j}", [P, C, 2, BH, HEAD]) for j in range(2)]
        x1s = [sb(f"x1s{j}", [P, D]) for j in range(2)]
        res2 = [sb(f"res2{j}", [P, D]) for j in range(2)]
        x2r = [sb(f"x2r{j}", [P, D]) for j in range(2)]

        used = [0]

        def late(*shape):
            names = "abc"[:len(shape)]
            size = 1
            for d in shape:
                size *= d
            part = room[:, used[0]:used[0] + size]
            used[0] += size
            if len(shape) == 1:
                return part
            return part.rearrange(f"p ({' '.join(names)}) -> p {' '.join(names)}", **dict(zip(names[1:], shape[1:])))
        gw = sb("gw", [P, C, E])
        w13s = sb("w13s", [P, C, E, 2 * I])
        w2s = roomy[0:KI, :].rearrange("p (e k n) -> p e k n", e=E, k=2)
        sw13s = sb("sw13s", [P, C, 2 * SI])
        sw2s = sb("sw2s", [P, 3, D])
        zeros = room[:, 0:2 * ROW].rearrange("p (o d) -> p o d", o=2)
        x2T = [sb(f"x2T{j}", [P, C, S]) for j in range(2)]
        x2all = xall
        early = w13s[:, :, :, :].rearrange("p c e n -> p (c e n)")
        qall = early[:, B * D:2 * B * D].rearrange("p (c n) -> p c n", c=C)
        xg = [early[:, (2 * B + 4 * j) * D:(2 * B + 4 * (j + 1)) * D].rearrange("p (c n) -> p c n", c=C) for j in range(2)]
        junk = w13s[:, :, :, :].rearrange("p c e n -> p (c e n)")[:, 0:B * D].rearrange("p (b d) -> p b d", b=B)
        z0 = shared_room[:, 0:B * D].rearrange("p (b d) -> p b d", b=B)
        logit = sb("logit", [P, B, E])
        best = sb("best", [P, B, 8])
        bestix = sb("bestix", [P, B, 8], U32)
        ixf = sb("ixf", [P, NB])
        hot = sb("hot", [P, NB, E], BF16)
        upto = late(E, NB)
        slot = late(NB, E)
        over = late(E, 16)
        tiles = sb("tiles", [P, E])
        endt = sb("endt", [P, E])
        base = sb("base", [P, E])
        posf = sb("posf", [P, NB])
        pos = sb("pos", [P, NB], U32)
        ended = sb("ended", [1, NT, E])
        ownf = sb("ownf", [1, NT])
        owner = sb("owner", [1, NT], mybir.dt.int32)
        sg = sb("sg", [P, B, TOP])
        sgsum = sb("sgsum", [P, B])
        wts = sb("wts", [P, B, TOP])
        ssil = probs[:, :, :].rearrange("p g s -> p (g s)")[:, 0:SI]
        sh = sb("sh", [P, SI])
        shT = sb("shT", [P, 3, S])
        xs = [late(ROW) for j in range(2)]
        idr = [sb(f"idr{k}", [P, 1], U32) for k in range(4)]
        share = [sb(f"share{k}", [P, 1]) for k in range(4)]
        xsT = x2T
        x2S = qT
        sil = [late(I) for j in range(2)]
        hid = [late(I) for j in range(2)]
        hidT = [late(2, P)[0:KI] for j in range(2)]
        ys = [late(D) for j in range(2)]
        SLOTS = 4
        yg = w13s[:, :, :, :].rearrange("p c e n -> p (c e n)")[:, 0:B * TOP * D].rearrange(
            "p (t b d) -> p t b d", b=B, t=TOP)
        st3 = sb("st3", [P, B, 6])
        mv3 = sb("mv3", [P, B, 2])
        ve3 = sb("ve3", [P, B])
        rs3 = sb("rs3", [P, B])
        nm3 = sb("nm3", [P, B])
        x2Td = nc.dram_tensor("x2Td", (B, P, C, S), F32).ap()
        xsd = nc.dram_tensor("xsd", (NT * P, ROW), F32).ap()
        ypd = nc.dram_tensor("ypd", ((NB + 2) * P, D), F32).ap()

        kerd = nc.dram_tensor("kerd", (HEADS, 2 * D), F32).ap()
        x1d = nc.dram_tensor("x1d", (B, S, D), F32).ap()

        p_kv = ps("p_kv", [P, 512])
        p_qs = ps("p_qs", [P, 2, 512])
        p_q = p_qs[:, 0, :].rearrange("p (c s) -> p c s", c=C)
        p_s = p_qs[:, 1, :]
        p_valq = p_qs[:, :, :].rearrange("p a (c s) -> p (a c) s", c=C)
        p_t = ps("p_t", [P, GROUPS, S])
        p_o = ps("p_o", [P, 512])
        p_y = ps("p_y", [P, 512])
        p_x2 = ps("p_x2", [P, 512])
        p_x = p_x2[:, 0:C * S].rearrange("p (c s) -> p c s", c=C)
        p_8 = ps("p_8", [P, 512])
        p_conv = [[p_kv[:, 0:320], p_q[:, :, :].rearrange("p c s -> p (c s)")[:, 0:320]],
                  [p_s[:, 0:320], p_8[:, 0:320]]]
        p_back = p_o[:, 0:256]
        p_proj = p_qs[:, 0, 0:D]
        p_logit = p_o[:, 2 * P:2 * P + E]
        p_part = [bank[:, 0:P].rearrange("p (c b i) -> p c b i", c=C, b=BH)
                  for bank in (p_t[:, :, :].rearrange("p g s -> p (g s)"), p_y)]
        p_rank, p_sum = p_o[:, :], p_y[:, :]
        p_a, p_b = p_kv[:, 0:SI], p_q[:, :, :].rearrange("p c s -> p (c s)")[:, 0:SI]
        p_hT = p_s[:, 0:3 * S].rearrange("p (k s) -> p k s", k=3)
        p_z = p_t[:, 0:2, :].rearrange("p g s -> p (g s)")
        p_xs = p_x
        p_ab = [p_kv[:, 0:SI], p_q[:, :, :].rearrange("p c s -> p (c s)")[:, 0:SI]]
        p_hid = p_s[0:KI, 0:2 * P].rearrange("p (k s) -> p k s", k=2)
        p_ye = p_t[:, 0:2, :].rearrange("p g s -> p (g s)")
        p_qall = [[p_kv[:, :], p_8[:, :]], [p_t[:, :, :].rearrange("p g s -> p (g s)"), p_x2[:, :]]]
        p_sel = [p_kv[:, :], p_8[:, :]]
        p_key = [p_t[:, :, :].rearrange("p g s -> p (g s)"), p_x2[:, :]]
        p_val = [p_valq[:, 0:2, :], p_valq[:, 2:4, :]]
        p_neg = p_s[0:2 * NH, 0:S // 2].bitcast(BF16)
        o_v = p_o[:, 0:NH * (HD + 1)].rearrange("p (g r d) -> p g r d", g=GROUPS, r=4)

        cst_in = sem("cst_in")
        w_in = sem("w_in")
        xall_in = [sem(f"xall_in{q}") for q in range(4)]
        wq_in = sem("wq_in")
        cstb_in = sem("cstb_in")
        late_in = sem("late_in")
        x_in = [sem(f"x_in{j}") for j in range(2)]
        qall_done = sem("qall_done")
        qall_out = sem("qall_out")
        gate_in = sem("gate_in")
        w13_in = sem("w13_in")
        imp_done = sem("imp_done")
        setup = sem("setup")
        impT_done = sem("impT_done")
        mask_done = sem("mask_done")
        maskT_done = sem("maskT_done")
        maskT_copied = sem("maskT_copied")
        count_done = sem("count_done")
        pick_done = sem("pick_done")
        dve = sem("dve")
        gathered = sem("gathered")
        xsel_out = sem("xsel_out")
        key_done = sem("key_done")
        key_out = sem("key_out")
        val_done = sem("val_done")
        val_out = sem("val_out")
        kbd_ready = sem("kbd_ready")
        neg2_ready = sem("neg2_ready")
        q_out = sem("q_out")
        s_done = sem("s_done")
        negm_ready = sem("negm_ready")
        n_done = sem("n_done")
        n_out = sem("n_out")
        z_ready = sem("z_ready")
        t_done = sem("t_done")
        p_ready = sem("p_ready")
        o_done = sem("o_done")
        attn_ready = sem("attn_ready")
        a_done = sem("a_done")
        aT_ready = sem("aT_ready")
        y_done = sem("y_done")
        xbo_ready = sem("xbo_ready")
        res_ready = sem("res_ready")
        mv_ready = sem("mv_ready")
        pool = sem("pool")
        rstd_ready = sem("rstd_ready")
        x1_ready = sem("x1_ready")
        out_sem = sem("out_sem")
        x1T_done = sem("x1T_done")
        x1q_ready = sem("x1q_ready")
        x1_stored = [sem(f"x1_stored{j}") for j in range(2)]
        ker_in = sem("ker_in")
        ker_zero = sem("ker_zero")
        ker_sum = sem("ker_sum")
        ker_out = sem("ker_out")
        head_in = [sem(f"head_in{j}") for j in range(2)]
        kv_made = sem("kv_made")
        conv_done = sem("conv_done")
        prod_done = sem("prod_done")
        sum_done = sem("sum_done")
        x1_back = [sem(f"x1_back{j}") for j in range(2)]
        part_done = sem("part_done")
        part_ready = sem("part_ready")
        back_done = sem("back_done")
        res2_ready = sem("res2_ready")
        stats2 = sem("stats2")
        mv2_ready = sem("mv2_ready")
        rstd2_ready = sem("rstd2_ready")
        x2_ready = sem("x2_ready")
        x2T_done = sem("x2T_done")
        x2T_ready = sem("x2T_ready")
        logit_done = sem("logit_done")
        logit_ready = sem("logit_ready")
        ffn_in = sem("ffn_in")
        zero_ready = sem("zero_ready")
        xsd_zeroed = sem("xsd_zeroed")
        route = sem("route")
        hot_ready = sem("hot_ready")
        rank_done = sem("rank_done")
        pos_ready = sem("pos_ready")
        owner_ready = sem("owner_ready")
        scattered = sem("scattered")
        wts_ready = sem("wts_ready")
        sg_ready = sem("sg_ready")
        sa_done = sem("sa_done")
        ssil_ready = sem("ssil_ready")
        sh_ready = sem("sh_ready")
        shT_done = sem("shT_done")
        shT_ready = sem("shT_ready")
        z_done = sem("z_done")
        z0_ready = sem("z0_ready")
        xsT_done = sem("xsT_done")
        xsT_ready = sem("xsT_ready")
        ab_done = sem("ab_done")
        sil_ready = sem("sil_ready")
        hid_ready = sem("hid_ready")
        hidT_done = sem("hidT_done")
        hidT_ready = sem("hidT_ready")
        ye_done = sem("ye_done")
        ys_ready = sem("ys_ready")
        fin = sem("fin")
        mv3_ready = sem("mv3_ready")
        ve3_ready = sem("ve3_ready")
        rs3_ready = sem("rs3_ready")
        st3_ready = sem("st3_ready")
        pair_sum = sem("pair_sum")
        out_ready = sem("out_ready")
        out_stored = sem("out_stored")
        w2_in = sem("w2_in")
        x2T_stored = [sem(f"x2T_stored{j}") for j in range(2)]
        id_ready = sem("id_ready")
        pairs_next = sem("pairs_next")
        x2T_in = [sem(f"x2T_in{j}") for j in range(2)]
        xs_in = [sem(f"xs_in{j}") for j in range(2)]
        ys_stored = [sem(f"ys_stored{j}") for j in range(2)]
        y_in = [sem(f"y_in{k}") for k in range(SLOTS)]
        x2_stored = [sem(f"x2_stored{j}") for j in range(2)]

        x_v = x.rearrange("b s d -> s b d")

        def steps(eng, step, n=B, first=2, last=2, ways=2):
            for b in range(first):
                step(b, b % ways)
            assert (n - first - last) % ways == 0
            with eng.Fori(0, (n - first - last) // ways) as i:
                for k in range(ways):
                    step(i * ways + (first + k), (first + k) % ways)
            for b in range(n - last, n):
                step(b, b % ways)

        def at(ap, b):
            if known(b):
                return ap[b]
            names = "pqrs"[:len(ap.shape) - 1]
            part = ap[(bass.ds(b, 1),) + (slice(None),) * (len(ap.shape) - 1)]
            return part.rearrange(f"o {' '.join(names)} -> (o {names[0]}) {' '.join(names[1:])}")

        def one(b):
            return slice(b, b + 1) if known(b) else bass.ds(b, 1)

        def place_values(copy, n, r):
            src = p_valq[n * KEEP:(n + 1) * KEEP, :, :].rearrange("p n (g r d) -> p n g r d", g=GROUPS, r=4)[:, :, :, r]
            dst = vbd[r * KEEP:(r + 1) * KEEP, :, :, r, 0:HD].rearrange("p (n q) g d -> p q n g d", q=4)[:, n]
            return copy(dst, src)

        def known(b):
            return isinstance(b, int)

        block = ctx.enter_context(nc.Block())

        @block.sync
        def _(sp):
            sp.dma_start(rowb[:, :, :], rows.rearrange("(o a) d -> o a d", o=1).to_broadcast([P, 3, D])).then_inc(cst_in, 16)
            sp.dma_start(colb[:, :], cols).then_inc(cst_in, 16)
            sp.dma_start(cst[:, 0:C_NEW], consts[:, 0:C_NEW]).then_inc(cst_in, 16)
            for q in range(4):
                sp.dma_start(xall[:, q * 4:q * 4 + 4, 0:D], x_v[:, q * 4:q * 4 + 4, :]).then_inc(xall_in[q], 16)
            sp.dma_start(cstb[:, :], constb).then_inc(cstb_in, 16)
            sp.wait_ge(x_in[1], 32)
            sp.dma_start(cst[:, C_NEW:C_W], consts[:, C_NEW:C_W]).then_inc(late_in, 16)

            def store(b, j):
                sp.wait_ge(x1_ready, b + 1)
                sp.dma_start(at(x1d, b), x1r[j][:, :]).then_inc(x1_stored[j], 16)
            steps(sp, store)

            def load_head(h, j):
                if known(h) and h < 2:
                    if h == 0:
                        sp.wait_ge(ker_out, 16)
                else:
                    sp.wait_ge(kv_made, h * 2 - 2)
                    sp.wait_ge(conv_done, h * 2 - 2)
                sp.dma_start(ctxr[j][:, :, :, :], at(ctxd, h)).then_inc(head_in[j], 16)
                row = kerd[one(h), D - P + 1:D - P + 2]
                sp.dma_start(toe[j][:, :], bass.AP(row.tensor, row.offset, [[1, P], [1, 2 * P]])).then_inc(head_in[j], 16)

            def load_x1(h, j):
                if known(h) and h < 2:
                    if h == 0:
                        for k in range(2):
                            sp.wait_ge(x1_stored[k], 8 * B)
                else:
                    sp.wait_ge(res2_ready, h - 1)
                sp.dma_start(x1s[j][:, :], x1d[:, h * HEAD:(h + 1) * HEAD, :] if known(h) else
                             x1d[:, bass.ds(h * HEAD, HEAD), :]).then_inc(x1_back[j], 16)

            def store_x2(h, j):
                sp.wait_ge(x2_ready, h + 1)
                sp.dma_start(x2all[:, one(h), 0:D].rearrange("p o d -> p (o d)"), x2r[j][:, :]).then_inc(x2_stored[j], 16)

            def load_x2T(b, j):
                if known(b) and b < 2:
                    sp.wait_ge(x2T_stored[b], 16)
                else:
                    sp.wait_ge(sa_done, b - 1)
                sp.dma_start(x2S[j][:, :, :], at(x2Td, b)).then_inc(x2T_in[j], 16)

            def store_x2T(h, j):
                sp.wait_ge(x2T_ready, h + 1)
                sp.dma_start(at(x2Td, h), x2T[j][:, :, :]).then_inc(x2T_stored[j], 16)

            def second(h, j):
                load_head(h, j)
                if not (known(h) and h < 1):
                    load_x1(h - 1, 1 - j)
                if not (known(h) and h < 4):
                    store_x2(h - 4, j)
                if not (known(h) and h < 5):
                    store_x2T(h - 5, 1 - j)
            steps(sp, second, n=HEADS, first=5, last=1)
            load_x1(HEADS - 1, 1)
            store_x2(HEADS - 4, 0)
            store_x2T(HEADS - 5, 1)
            for b in range(2):
                load_x2T(b, b)
            for h in range(HEADS - 4, HEADS):
                if h + 1 < HEADS:
                    store_x2(h + 1, 1 - h % 2)
                store_x2T(h, h % 2)
            for j in range(2):
                sp.wait_ge(x2T_stored[j], 8 * HEADS)
            steps(sp, lambda b, j: load_x2T(b + 2, j), n=HEADS - 2)

            xs_v = xsd.rearrange("(t p) d -> t p d", p=P)

            def load_tile(t, j):
                if known(t) and t < 2:
                    if t == 0:
                        sp.wait_ge(scattered, 16 * NB)
                else:
                    sp.wait_ge(xsT_done, t - 1)
                    sp.wait_ge(id_ready, t - 1)
                sp.dma_start(xs[j][:, :], at(xs_v, t)).then_inc(xs_in[j], 16)
            steps(sp, load_tile, n=NT, last=1)
            for j in range(2):
                sp.wait_ge(ys_stored[j], 16 * ((NT + 1 - j) // 2))
            yp_v = ypd[0:NB * P, :].rearrange("(i b p) d -> i p b d", i=TOP, p=P)
            for k in range(B // SLOTS):
                for i in range(TOP):
                    sp.dma_start(yg[:, i, k * SLOTS:(k + 1) * SLOTS, :],
                                 at(yp_v, i)[:, k * SLOTS:(k + 1) * SLOTS, :]).then_inc(y_in[k], 16)
            for h in range(HEADS):
                sp.wait_ge(out_ready, h + 1)
                sp.dma_start(out[:, h * HEAD:(h + 1) * HEAD, :], x2all[:, h, 0:D]).then_inc(out_stored, 16)
            sp.wait_ge(out_stored, 16 * HEADS)

        @block.tensor
        def _(pe):
            def queries(g):
                if g == 0:
                    pe.wait_ge(wq_in, 16)
                pe.wait_ge(x_in[g % 2], 16 + 16 * (g // 2))
                if g == 2:
                    pe.wait_ge(xsel_out, C)
                for m in range(C):
                    for c in range(C):
                        last = pe.matmul(p_qall[g % 2][m], wq[:, c, m * P:(m + 1) * P], xg[g % 2][:, c, :],
                                         start=(c == 0), stop=(c == C - 1))
                last.then_inc(qall_done, 1)
            pe.wait_ge(cst_in, 48)
            queries(0)
            pe.wait_ge(imp_done, 1)
            pe.transpose(p_y[0:B, 0:P], imp[:, :], ident).then_inc(impT_done, 1)
            pe.wait_ge(mask_done, 1)
            pe.transpose(p_s[:, 0:B], chosenT[:, :], cst[0:B, C_ID:C_ID + B]).then_inc(maskT_done, 1)
            pe.wait_ge(maskT_copied, 1)
            pe.matmul(p_o[:, 0:B], tri, chosen[:, :], start=True, stop=True).then_inc(count_done, 1)
            pe.wait_ge(setup, 3)
            pe.wait_ge(pick_done, 1)
            pe.wait_ge(qall_out, 1)
            for c in range(C):
                for b in range(B):
                    last = pe.matmul(p_sel[c][:, b * KEEP:(b + 1) * KEEP], xall[:, b, c * P:(c + 1) * P],
                                     pick[:, b, :], start=True, stop=True)
                last.then_inc(gathered, 1)
            pe.wait_ge(w_in, 48)
            pe.wait_ge(cstb_in, 16)
            queries(1)
            queries(2)
            pe.wait_ge(qall_out, 2)
            pe.wait_ge(xsel_out, C)
            for m in range(C):
                for c in range(C):
                    last = pe.matmul(p_key[m], wk[:, c, m * P:(m + 1) * P], xsel[:, c, :],
                                     start=(c == 0), stop=(c == C - 1))
            last.then_inc(key_done, 1)
            for n in range(B // 4):
                o = p_val[n // 2][:, n % 2, :]
                for c in range(C):
                    pe.matmul(o, xsel[:, c, n * P:(n + 1) * P], wv[:, c, :], start=(c == 0), stop=False)
                last = pe.matmul(o, cst[0:1, C_ONES:C_ONES + P], rowb[0:1, 2, :], start=False, stop=True)
            last.then_inc(val_done, 1)
            pe.wait_ge(key_out, 1)
            queries(3)
            pe.wait_ge(val_out, 2)
            pe.wait_ge(qall_out, 4)

            def scores(b, j):
                pe.wait_ge(kbd_ready, b + 1)
                pe.wait_ge(q_out, b + 1)
                if not (known(b) and b < 1):
                    pe.wait_ge(n_out, b)
                for c in range(C):
                    last = pe.matmul(p_s[:, c * 256:(c + 1) * 256], qT[j][:, c, :], kbd[j][:, c, :, :],
                                     start=True, stop=True)
                last.then_inc(s_done, 1)

            def turn_max(b, j):
                pe.wait_ge(neg2_ready, b + 1)
                pe.transpose(p_neg, neg2[j][:, :, :].rearrange("p t h -> p (t h)"), identb).then_inc(n_done, 1)

            def scores_T(b, j):
                pe.wait_ge(n_out, b + 1)
                if not (known(b) and b < 1):
                    pe.wait_ge(p_ready, b)
                for g in range(GROUPS):
                    pe.matmul(p_t[:, g, :], kbd[j][:, g // 2, (g % 2) * 4:(g % 2) * 4 + 4, :], qT[j][:, g // 2, :],
                              start=True, stop=False)
                    last = pe.matmul(p_t[:, g, :], headrow[:, g * P:(g + 1) * P], negT[:, :],
                                     start=False, stop=True)
                last.then_inc(t_done, 1)

            def weigh(b, j):
                pe.wait_ge(p_ready, b + 1)
                for g in range(GROUPS):
                    last = pe.matmul(o_v[:, g, :, :], probs[:, g, :],
                                     vbd[:, one(b), g, :, :].rearrange("p o r d -> p (o r) d"), start=True, stop=True)
                last.then_inc(o_done, 1)

            def turn_attn(b, j):
                pe.wait_ge(attn_ready, b + 1)
                for c in range(C):
                    last = pe.transpose(p_y[:, c * P:(c + 1) * P], attn[:, c * P:(c + 1) * P], ident)
                last.then_inc(a_done, 1)

            def project(b, j):
                pe.wait_ge(aT_ready, b + 1)
                if not (known(b) and b < 1):
                    pe.wait_ge(res_ready, b)
                for c in range(C):
                    last = pe.matmul(p_proj, attnT[:, c, :], wo[:, c, :], start=(c == 0), stop=(c == C - 1))
                last.then_inc(y_done, 1)

            def turn_x1(b, j):
                pe.wait_ge(x1_ready, b + 1)
                if not (known(b) and b < 1):
                    pe.wait_ge(x1q_ready, b)
                for c in range(C):
                    last = pe.transpose(p_x[:, c, :], x1r[j][:, c * P:(c + 1) * P], ident)
                last.then_inc(x1T_done, 1)

            scores(0, 0)
            turn_max(0, 0)
            scores_T(0, 0)
            scores(1, 1)
            weigh(0, 0)
            turn_max(1, 1)
            scores_T(1, 1)
            turn_attn(0, 0)

            def step(b, j):
                def has(d):
                    return not known(b) or b + d < B
                if has(2):
                    scores(b + 2, j)
                if has(1):
                    weigh(b + 1, 1 - j)
                project(b, j)
                if has(2):
                    turn_max(b + 2, j)
                if not (known(b) and b < 2):
                    turn_x1(b - 2, j)
                if has(2):
                    scores_T(b + 2, j)
                if has(1):
                    turn_attn(b + 1, 1 - j)
            steps(pe, step, first=3, last=3)
            turn_x1(B - 2, 0)
            turn_x1(B - 1, 1)

            def convolve(h, f, j):
                u = h * 2 + f
                pe.wait_ge(head_in[j], 32 + 32 * (h // 2) if known(h) else (h - j) * 16 + 32)
                pe.wait_ge(kv_made, u + 1)
                if not (known(h) and h < 1):
                    pe.wait_ge(prod_done, u - 1)
                k = [kv[f][:, c, :, :, :] for c in range(C)]
                pe.matmul(p_conv[f][0], toe[j][:, 0:P], k[0], start=True, stop=True)
                pe.matmul(p_conv[f][1], toe[j][:, P:2 * P], k[0], start=True, stop=False)
                pe.matmul(p_conv[f][1], toe[j][:, 0:P], k[1], start=False, stop=True).then_inc(conv_done, 1)

            def add(h, f, j):
                u = h * 2 + f
                pe.wait_ge(prod_done, u + 1)
                if not (known(h) and h < 1):
                    pe.wait_ge(part_ready, u - 1)
                for s in range(BY_PE):
                    last = pe.matmul(p_part[f], ident, prod[f][:, :, :, s, :], start=(s == 0), stop=(s == BY_PE - 1))
                last.then_inc(part_done, 1)

            def turn_back(h, j):
                pe.wait_ge(sum_done, h * 2 + 2)
                pe.wait_ge(part_ready, h * 2 + 2)
                if not (known(h) and h < 1):
                    pe.wait_ge(res2_ready, h)
                if not (known(h) and h < 4):
                    pe.wait_ge(logit_ready, h - 3)
                for c in range(C):
                    for share in (conv, part):
                        last = pe.matmul(p_back[:, c * P:(c + 1) * P],
                                         share[j][:, c, :, :, :].rearrange("p f b i -> p (f b i)"), ident,
                                         start=(share is conv), stop=(share is part))
                last.then_inc(back_done, 1)

            def turn_x2(h, j):
                pe.wait_ge(x2_ready, h + 1)
                if not (known(h) and h < 1):
                    pe.wait_ge(x2T_ready, h)
                for c in range(C):
                    last = pe.transpose(p_x[:, c, :], x2r[j][:, c * P:(c + 1) * P], ident)
                last.then_inc(x2T_done, 1)

            def score(h, j, turned):
                pe.wait_ge(x2T_ready, h + 1)
                if not (known(h) and h < 1):
                    pe.wait_ge(logit_ready, h)
                pe.wait_ge(res2_ready, turned)
                for c in range(C):
                    last = pe.matmul(p_logit, x2T[j][:, c, :], gw[:, c, :], start=(c == 0), stop=(c == C - 1))
                last.then_inc(logit_done, 1)
            pe.wait_ge(q_out, B)
            pe.wait_ge(n_out, B)
            pe.wait_ge(p_ready, B)
            convolve(0, 0, 0)
            convolve(0, 1, 0)
            pe.wait_ge(gate_in, 16)

            def second(h, j):
                more = not (known(h) and h == HEADS - 1)
                if not (known(h) and h < 3):
                    turn_x2(h - 3, 1 - j)
                if not (known(h) and h < 4):
                    score(h - 4, j, h - 1)
                if more:
                    convolve(h + 1, 0, 1 - j)
                if not (known(h) and h < 1):
                    turn_back(h - 1, 1 - j)
                add(h, 0, j)
                if more:
                    convolve(h + 1, 1, 1 - j)
                add(h, 1, j)
            steps(pe, second, n=HEADS, first=4, last=2)
            turn_x2(HEADS - 3, 1)
            score(HEADS - 4, 0, HEADS - 1)
            turn_back(HEADS - 1, 1)
            score(HEADS - 3, 1, HEADS)
            for h in (HEADS - 2, HEADS - 1):
                turn_x2(h, h % 2)
                score(h, h % 2, HEADS)

            def shared_up(b, j):
                pe.wait_ge(x2T_in[j], 16 + 16 * (b // 2) if known(b) else (b - j) * 8 + 16)
                for k, p in enumerate((p_a, p_b)):
                    for c in range(C):
                        last = pe.matmul(p, x2S[j][:, c, :], sw13s[:, c, k * SI:(k + 1) * SI],
                                         start=(c == 0), stop=(c == C - 1))
                last.then_inc(sa_done, 1)

            def shared_turn(b, j):
                pe.wait_ge(sh_ready, b + 1)
                if not (known(b) and b < 1):
                    pe.wait_ge(shT_ready, b)
                for k, (lo, n) in enumerate(SP_):
                    last = pe.transpose(p_hT[0:n, k, :], sh[:, lo:lo + n], ident)
                last.then_inc(shT_done, 1)

            def shared_down(b, j):
                pe.wait_ge(shT_ready, b + 1)
                if not (known(b) and b < 1):
                    pe.wait_ge(z0_ready, b)
                for k, (lo, n) in enumerate(SP_):
                    last = pe.matmul(p_z, shT[0:n, k, :], sw2s[0:n, k, :], start=(k == 0), stop=(k == 2))
                last.then_inc(z_done, 1)

            def rank():
                pe.wait_ge(hot_ready, 1)
                pe.matmul(p_rank, cstb[:, B_STRI:B_STRI + P], hot[:, :, :], start=True, stop=True)
                pe.matmul(p_sum, cstb[:, B_ONES:B_ONES + P], hot[:, :, :].rearrange("p n e -> p e n"), start=True, stop=True
                          ).then_inc(rank_done, 1)

            pe.wait_ge(ffn_in, 16 * 2)
            shared_up(0, 0)

            def shared(b, j):
                shared_turn(b, j)
                if not (known(b) and b == B - 1):
                    shared_up(b + 1, 1 - j)
                shared_down(b, j)
                if known(b) and b == 0:
                    rank()
            steps(pe, shared)

            pe.wait_ge(owner_ready, 1)
            pe.wait_ge(w2_in, 16)
            pe.wait_ge(w13_in, 16 * E)
            pe.wait_ge(z0_ready, B)

            def expert(t):
                return pe.value_load(owner[0:1, one(t)], min_val=0, max_val=E - 1)

            def turn_in(t, j):
                pe.wait_ge(xs_in[j], 16 + 16 * (t // 2) if known(t) else (t - j) * 8 + 16)
                if not (known(t) and t < 1):
                    pe.wait_ge(xsT_ready, t)
                for c in range(C):
                    last = pe.transpose(p_xs[:, c, :], xs[j][:, c * P:(c + 1) * P], ident)
                last.then_inc(xsT_done, 1)

            def up(t, j, e):
                pe.wait_ge(xsT_ready, t + 1)
                for c in range(C):
                    last = pe.matmul(p_ab[j], xsT[j][:, c, :],
                                     w13s[:, c, bass.ds(e, 1), :].rearrange("p o n -> p (o n)"),
                                     start=(c == 0), stop=(c == C - 1))
                last.then_inc(ab_done, 1)

            def turn_mid(t, j):
                pe.wait_ge(hid_ready, t + 1)
                if not (known(t) and t < 1):
                    pe.wait_ge(hidT_ready, t)
                for k in range(2):
                    last = pe.transpose(p_hid[:, k, :], hid[j][:, k * KI:(k + 1) * KI], ident)
                last.then_inc(hidT_done, 1)

            def down(t, j, e):
                pe.wait_ge(hidT_ready, t + 1)
                if not (known(t) and t < 1):
                    pe.wait_ge(ys_ready, t)
                for k in range(2):
                    last = pe.matmul(p_ye, hidT[j][:, k, :],
                                     w2s[:, bass.ds(e, 1), k, :].rearrange("p o n -> p (o n)"),
                                     start=(k == 0), stop=(k == 1))
                last.then_inc(ye_done, 1)

            turn_in(0, 0)
            turn_in(1, 1)

            def tile(t, j, e, following, late):
                def has(d):
                    return not known(t) or t + d < NT
                turn_mid(t, j)
                if has(1):
                    up(t + 1, 1 - j, following)
                found = expert(t + 2) if late else None
                if has(2):
                    turn_in(t + 2, j)
                down(t, j, e)
                return found

            def run(t, j, n):
                e, following = expert(t), expert(t + 1)
                for k in range(n):
                    e, following = following, tile(t + k, (j + k) % 2, e, following, k < n - 1 and not (known(t) and t + k + 2 >= NT))
            up(0, 0, expert(0))
            run(0, 0, FIRST)
            with pe.Fori(0, NG) as i:
                run(i * TURN + FIRST, FIRST % 2, TURN)
            run(FIRST + NG * TURN, (FIRST + NG * TURN) % 2, NT - FIRST - NG * TURN)

        @block.vector
        def _(v):
            done = [0]

            def chain(ins):
                ins.then_inc(dve, 1)
                done[0] += 1
                v.wait_ge(dve, done[0])

            v.memset(vbd[:, :, :, :, :], 0.0).then_inc(setup, 1)
            v.wait_ge(setup, 1)
            for r in range(4):
                v.memset(vbd[32 * r:32 * r + 32, :, :, r, HD:HD + 1], 1.0)
            v.memset(half[:, 0:1], EPS)
            v.memset(half[:, 1:2], -0.5).then_inc(setup, 1)
            v.wait_ge(cst_in, 48)
            v.tensor_scalar(bqs[:, :], colb[:, 0:C], SCALE, None, ALU.mult).then_inc(setup, 1)
            for b in range(B):
                if b % 4 == 0:
                    v.wait_ge(xall_in[b // 4], 16)
                last = v.tensor_tensor_reduce(junk[:, b, :], xall[:, b, 0:D], rowb[:, 0, :], 1.0, 0.0, ALU.mult, ALU.add,
                                              imp[:, b:b + 1])
            chain(last)
            v.tensor_scalar(imp[:, :], imp[:, :], colb[:, 4:5], None, ALU.add).then_inc(imp_done, 1)
            v.wait_ge(impT_done, 1)
            chain(v.tensor_copy(impT[:, 0, :], p_y[0:B, 0:P]))
            for n in range(4):
                chain(v.max(top8[:, n, :], impT[:, n, :]))
                chain(v.match_replace(impT[:, n + 1, :], top8[:, n, :], impT[:, n, :], NEG))
            v.tensor_scalar(chosenT[:, :], impT[:, 4, :], NEG, None, ALU.is_equal).then_inc(mask_done, 1)
            v.wait_ge(maskT_done, 1)
            v.tensor_copy(chosen[:, :], p_s[:, 0:B]).then_inc(maskT_copied, 1)
            v.wait_ge(maskT_copied, 1)
            v.wait_ge(count_done, 1)
            chain(v.tensor_tensor(place[:, :], chosen[:, :], p_o[:, 0:B], ALU.mult))
            v.tensor_tensor(pick[:, :, :], iota.rearrange("p (o k) -> p o k", o=1).to_broadcast([P, B, KEEP]),
                            place[:, :].rearrange("p (b o) -> p b o", o=1).to_broadcast([P, B, KEEP]),
                            ALU.is_equal).then_inc(pick_done, 1)
            v.wait_ge(gathered, 1)
            v.tensor_copy(xsel[:, 0, :], p_sel[0]).then_inc(xsel_out, 1)
            v.wait_ge(val_done, 1)
            for n in (0, 1):
                for r in range(4):
                    last = place_values(v.tensor_copy, n, r)
            last.then_inc(val_out, 1)

            links = done[0] + 8

            def chain_at(b, n):
                if known(b) and b == B - 1:
                    return links + 6 * b - 3 + n
                return b * 6 + (links + n)

            def chase(b, j, n):
                v.wait_ge(s_done, b + 1)
                if not (known(b) and b < 1):
                    v.wait_ge(neg2_ready, b)
                v.tensor_reduce(mx[:, :], p_s[:, :].rearrange("p (h k) -> p h k", k=KEEP), AX.X, ALU.max,
                                negate=True).then_inc(dve, 1)
                v.wait_ge(dve, n(1))
                v.tensor_scalar(neg2[j][:, 0, :], mx[:, :], 0.0, None, ALU.min).then_inc(dve, 1)
                v.wait_ge(dve, n(2))
                v.scalar_tensor_tensor(out=neg2[j][:, 1, :], in0=mx[:, :], scalar=0.0, in1=neg2[j][:, 0, :],
                                       op0=ALU.min, op1=ALU.subtract).then_inc(dve, 1)
                v.wait_ge(dve, n(3))
                v.tensor_tensor(negm[j][:, :], neg2[j][:, 0, :], neg2[j][:, 1, :], ALU.add).then_inc(neg2_ready, 1)

            def normalise(b, j, n):
                v.wait_ge(z_ready, b + 1)
                v.wait_ge(o_done, b + 1)
                ov = o_v.rearrange("p g r d -> p (g r) d")
                v.scalar_tensor_tensor(out=den[:, :], in0=zero_e[j][:, :], scalar=float(S - KEEP),
                                       in1=ov[:, :, HD], op0=ALU.mult, op1=ALU.add).then_inc(dve, 1)
                v.wait_ge(dve, n(1))
                v.reciprocal(rec[:, :], den[:, :]).then_inc(dve, 1)
                v.wait_ge(dve, n(2))
                v.tensor_tensor(attn[:, :].rearrange("p (h d) -> p h d", d=HD), ov[:, :, 0:HD],
                                rec[:, :].rearrange("p (h o) -> p h o", o=1).to_broadcast([P, NH, HD]),
                                ALU.mult).then_inc(attn_ready, 1)

            def layer1(b, j):
                v.wait_ge(xbo_ready, b + 1)
                v.wait_ge(y_done, b + 1)
                if not (known(b) and b < 2):
                    v.wait_ge(x1_ready, b - 1)
                v.tensor_tensor(res[j][:, :], p_proj, xbo[j][:, :], ALU.add).then_inc(res_ready, 1)
                v.wait_ge(res_ready, b + 1)
                v.bn_stats(stats[:, :], res[j][:, :]).then_inc(dve, 1)
                v.wait_ge(dve, chain_at(b, {B - 2: 3, B - 1: 1}.get(b, 6) if known(b) else 6))
                if not (known(b) and b == 0):
                    x1_out(b - 1, 1 - j)
                v.bn_aggr(mv[j][:, :], stats[:, :]).then_inc(mv_ready, 1)

            def x1_out(b, j):
                v.wait_ge(rstd_ready, b + 1)
                if not (known(b) and b < 2):
                    v.wait_ge(x1_stored[j], (b - j) * 8)
                    v.wait_ge(x1T_done, b - 1)
                v.tensor_scalar(x1r[j][:, :], res[j][:, :], mv[j][:, 0:1], rstd[j][:, 0:1], ALU.subtract,
                                ALU.mult).then_inc(x1_ready, 1)

            chase(0, 0, lambda n: done[0] + n)
            chase(1, 1, lambda n: done[0] + 3 + n)
            normalise(0, 0, lambda n: done[0] + 6 + n)

            def step(b, j):
                if not known(b) or b + 2 < B:
                    chase(b + 2, j, lambda n: chain_at(b, n))
                if not known(b) or b + 1 < B:
                    before = 0 if known(b) and b + 2 >= B else 3
                    normalise(b + 1, 1 - j, lambda n: chain_at(b, before + n))
                layer1(b, j)
            steps(v, step, first=3, last=3)
            x1_out(B - 1, 1)

            def window(ap, n):
                return bass.AP(ap.tensor, ap.offset, [list(ap.ap[0]), [WRAP, BH], [1, n], [1, HEAD]])

            def products(h, f, j):
                u = h * 2 + f
                v.wait_ge(conv_done, u + 1)
                if not (known(h) and h < 1):
                    v.wait_ge(sum_done, u - 1)
                    v.wait_ge(part_done, u - 1)
                if not (known(h) and u == 0):
                    v.wait_ge(prod_done, u)
                for c in range(C):
                    q = x1q[:, one(h), c, f * BH:(f + 1) * BH, 0:HEAD]
                    y = p_conv[f][c].rearrange("p (b d i) -> p b d i", b=BH, d=DIAG)
                    v.tensor_tensor(prod[f][:, c, :, 0:DIAG, :], y, window(q, DIAG), ALU.mult)
                    o = prod[f][:, c, :, :, :]
                    o = bass.AP(o.tensor, o.offset + DIAG * HEAD + 1, [list(o.ap[0]), [ROWS * HEAD, BH],
                                                                      [2 * HEAD + 1, 3], [1, HEAD]])
                    qq = bass.AP(q.tensor, q.offset, [list(q.ap[0]), [WRAP, BH], [0, 3], [1, HEAD]])
                    last = v.tensor_tensor(o, y[:, :, 1:4, :], qq, ALU.mult)
                last.then_inc(prod_done, 1)

            def sums(h, f, j):
                if not (known(h) and h < 2):
                    v.wait_ge(back_done, h - 1)
                for c in range(C):
                    last = v.tensor_reduce(conv[j][:, c, f, :, :], prod[f][:, c, :, BY_PE:ROWS, :].rearrange("p b s i -> p b i s"),
                                           AX.X, ALU.add)
                last.then_inc(sum_done, 1)

            for j in range(2):
                last = v.memset(prod[j][:, :, :, :, :], 0.0)
            last.then_inc(setup, 1)
            v.wait_ge(setup, 4)
            v.wait_ge(x1q_ready, B)
            v.wait_ge(o_done, B)

            def second(b, j):
                v.wait_ge(x1_back[j], 16 + 16 * (b // 2) if known(b) else (b - j) * 8 + 16)
                v.wait_ge(back_done, b + 1)
                if not (known(b) and b < 2):
                    v.wait_ge(x2_ready, b - 1)
                v.tensor_tensor(res2[j][:, :], p_back, x1s[j][:, :], ALU.add).then_inc(res2_ready, 1)
                if not (known(b) and b < 3):
                    scores_out(b - 3, 1 - j)
                v.wait_ge(res2_ready, b + 1)
                v.bn_stats(stats[:, :], res2[j][:, :]).then_inc(stats2, 1)
                v.wait_ge(stats2, b + 1)
                if known(b) and b == 0:
                    v.bn_aggr(mv[j][:, :], stats[:, :]).then_inc(mv2_ready, 1)
                else:
                    x2(b - 1, 1 - j)
                    v.bn_aggr(mv[j][:, :], stats[:, :]).then_inc(mv2_ready, 1)

            def x2(b, j):
                v.wait_ge(rstd2_ready, b + 1)
                if not (known(b) and b < 2):
                    v.wait_ge(x2_stored[j], (b - j) * 8)
                v.tensor_scalar(x2r[j][:, :], res2[j][:, :], mv[j][:, 0:1], rstd[j][:, 0:1], ALU.subtract,
                                ALU.mult).then_inc(x2_ready, 1)

            def scores_out(b, j):
                v.wait_ge(logit_done, b + 1)
                if known(b):
                    v.tensor_copy(logit[:, b, :], p_logit).then_inc(logit_ready, 1)
                else:
                    v.tensor_scalar(logit[:, one(b), :].rearrange("p o e -> p (o e)"), p_logit, 1.0, None,
                                    ALU.mult).then_inc(logit_ready, 1)

            def second_step(h, j):
                products(h, 0, j)
                if not (known(h) and h < 1):
                    sums(h - 1, 1, 1 - j)
                products(h, 1, j)
                sums(h, 0, j)
                if not (known(h) and h < 1):
                    second(h - 1, 1 - j)
            steps(v, second_step, n=HEADS, first=4, last=0)
            v.wait_ge(prod_done, 2 * HEADS)
            sums(HEADS - 1, 1, 1)
            second(HEADS - 1, 1)
            x2(HEADS - 1, 1)
            for h in range(HEADS - 3, HEADS):
                scores_out(h, h % 2)

            def shared_h(b, j):
                v.wait_ge(ssil_ready, b + 1)
                v.tensor_tensor(sh[:, :], ssil[:, :], p_b, ALU.mult).then_inc(sh_ready, 1)

            def shared_z(b, j):
                v.wait_ge(z_done, b + 1)
                v.tensor_tensor(z0[:, one(b), :].rearrange("p o d -> p (o d)"), p_z,
                                x2all[:, one(b), 0:D].rearrange("p o d -> p (o d)"), ALU.add).then_inc(z0_ready, 1)
            def shared(b, j):
                if known(b) and b < 2:
                    return
                if not (known(b) and b == B - 1):
                    shared_h(b + 1, 1 - j)
                shared_z(b, j)

            n = [0]

            def then(ins):
                ins.then_inc(route, 1)
                n[0] += 1
                v.wait_ge(route, n[0])
            v.wait_ge(logit_ready, B)
            for b in range(B):
                last = v.max(best[:, b, :], logit[:, b, :])
            then(last)
            for b in range(B):
                last = v.max_index(bestix[:, b, :], best[:, b, :], logit[:, b, :])
            then(last)
            shared_h(0, 0)
            then(v.tensor_copy(ixf[:, :].rearrange("p (b k) -> p b k", k=TOP), bestix[:, :, 0:TOP]))
            v.tensor_tensor(hot[:, :, :],
                            cst[:, C_N:C_N + E].rearrange("p (o e) -> p o e", o=1).to_broadcast([P, NB, E]),
                            ixf[:, :].rearrange("p (n o) -> p n o", o=1).to_broadcast([P, NB, E]),
                            ALU.is_equal).then_inc(hot_ready, 1)
            v.wait_ge(hot_ready, 1)
            for j in range(2):
                v.wait_ge(x2_stored[j], 8 * B)
            shared_h(1, 1)
            shared_z(0, 0)
            v.wait_ge(rank_done, 1)
            v.wait_ge(late_in, 16)
            then(v.tensor_tensor_scan(upto[:, :, :].rearrange("p e n -> p (e n)"),
                                      cst[:, C_NEW:C_NEW + E * NB], p_sum, 0.0, ALU.mult, ALU.add))
            then(v.tensor_tensor(over[:, :, :],
                                 upto[:, :, NB - 1:NB].to_broadcast([P, E, 16]),
                                 cst[:, C_M:C_M + 16].rearrange("p (o m) -> p o m", o=1).to_broadcast([P, E, 16]),
                                 ALU.is_gt))
            then(v.tensor_reduce(tiles[:, :], over[:, :, :], AX.X, ALU.add))
            then(v.tensor_tensor_scan(endt[:, :], cst[:, C_ONES:C_ONES + E], tiles[:, :], 0.0, ALU.mult, ALU.add))
            then(v.tensor_tensor(base[:, :], endt[:, :], tiles[:, :], ALU.subtract))
            then(v.tensor_tensor(slot[:, :, :], upto[:, :, :].rearrange("p e n -> p n e"),
                                 p_sum.rearrange("p (e n) -> p n e", e=E), ALU.subtract))
            then(v.tensor_tensor(slot[:, :, :], slot[:, :, :], p_rank.rearrange("p (n e) -> p n e", e=E), ALU.add))
            then(v.tensor_scalar(base[:, :], base[:, :], float(P), None, ALU.mult))
            shared_h(2, 0)
            shared_z(1, 1)
            then(v.tensor_tensor(slot[:, :, :], slot[:, :, :],
                                 base[:, :].rearrange("p (o e) -> p o e", o=1).to_broadcast([P, NB, E]), ALU.add))
            then(v.tensor_tensor(slot[:, :, :], slot[:, :, :], hot[:, :, :], ALU.mult))
            then(v.tensor_reduce(posf[:, :], slot[:, :, :], AX.X, ALU.add))
            v.tensor_copy(pos[:, :], posf[:, :]).then_inc(pos_ready, 1)
            then(v.tensor_tensor(ended[:, :, :],
                                 endt[0:1, :].rearrange("p (o e) -> p o e", o=1).to_broadcast([1, NT, E]),
                                 cst[0:1, C_N:C_N + NT].rearrange("p (t o) -> p t o", o=1).to_broadcast([1, NT, E]),
                                 ALU.is_le))
            then(v.tensor_reduce(ownf[:, :], ended[:, :, :], AX.X, ALU.add))
            v.tensor_scalar(owner[:, :], ownf[:, :], float(E - 1), None, ALU.min).then_inc(owner_ready, 1)
            v.wait_ge(sg_ready, 1)
            then(v.tensor_tensor(sgsum[:, :], sg[:, :, 0], sg[:, :, 1], ALU.add))
            then(v.reciprocal(sgsum[:, :], sgsum[:, :]))
            v.tensor_tensor(wts[:, :, :], sg[:, :, :],
                            sgsum[:, :].rearrange("p (b o) -> p b o", o=1).to_broadcast([P, B, TOP]),
                            ALU.mult).then_inc(wts_ready, 1)
            steps(v, shared)

            def hidden(t, j):
                v.wait_ge(sil_ready, t + 1)
                v.tensor_tensor(hid[j][:, :], sil[j][:, :], p_ab[j][:, I:2 * I], ALU.mult).then_inc(hid_ready, 1)

            def y_out(t, k):
                j = k % 2
                v.wait_ge(ye_done, t + 1)
                v.wait_ge(id_ready, t + 1)
                if not (known(t) and t < 2):
                    v.wait_ge(ys_stored[j], (t - j) * 8)
                v.tensor_scalar(ys[j][:, :], p_ye, share[k][:, 0:1], None, ALU.mult).then_inc(ys_ready, 1)
            hidden(0, 0)

            def tile(t, k):
                if not (known(t) and t == NT - 1):
                    hidden(t + 1, 1 - k % 2)
                y_out(t, k)
            steps(v, tile, n=NT, first=4, last=3, ways=4)

            for k in range(0, B, SLOTS):
                v.wait_ge(pair_sum, k // SLOTS + 1)
                v.tensor_tensor(z0[:, k:k + SLOTS, :], yg[:, 0, k:k + SLOTS, :], z0[:, k:k + SLOTS, :], ALU.add
                                ).then_inc(fin, 1)
                v.wait_ge(fin, k // SLOTS + 1)
                for b in range(k, k + SLOTS):
                    last = v.bn_stats(st3[:, b, :], z0[:, b, :])
                last.then_inc(st3_ready, 1)
                v.wait_ge(st3_ready, k // SLOTS + 1)
                for b in range(k, k + SLOTS):
                    last = v.bn_aggr(mv3[:, b, :], st3[:, b, :])
                last.then_inc(mv3_ready, 1)

        @block.scalar
        def _(a):
            def load_x(g):
                if g >= 2:
                    a.wait_ge(qall_done, g - 1)
                a.dma_start(xg[g % 2][:, :, :], xT[g]).then_inc(x_in[g % 2], 16)
            a.dma_start(wq[:, :, :], Wq.rearrange("(c p) n -> p c n", p=P)).then_inc(wq_in, 16)
            load_x(0)
            a.wait_ge(xall_in[2], 16)
            load_x(1)
            for w, dram in ((wk, Wk), (wv, Wv), (wo, Wo)):
                a.dma_start(w[:, :, :], dram.rearrange("(c p) n -> p c n", p=P)).then_inc(w_in, 16)
            a.wait_ge(setup, 3)

            def queries_all(g):
                a.wait_ge(qall_done, g + 1)
                for c in range(C):
                    last = a.activation(qall[:, c, g * 4 * S:(g + 1) * 4 * S], p_qall[g % 2][c], ACT.Identity,
                                        bias=bqs[:, c:c + 1], scale=SCALE)
                last.then_inc(qall_out, 1)
            queries_all(0)
            load_x(2)
            a.wait_ge(gathered, C)
            a.copy(xsel[:, 1, :], p_sel[1]).then_inc(xsel_out, 1)
            queries_all(1)
            load_x(3)
            queries_all(2)
            a.wait_ge(key_done, 1)
            for m in range(C):
                last = a.activation(keyT[:, m, :], p_key[m], ACT.Identity, bias=colb[:, C + m:C + m + 1])
            last.then_inc(key_out, 1)
            a.wait_ge(val_done, 1)
            for n in (2, 3):
                for r in range(4):
                    last = place_values(a.copy, n, r)
            last.then_inc(val_out, 1)

            queries_all(3)
            a.wait_ge(qall_out, 4)

            def queries_out(b, j):
                a.copy(qT[j][:, :, :], qall[:, :, b * S:(b + 1) * S] if known(b) else qall[:, :, bass.ds(b * S, S)]
                       ).then_inc(q_out, 1)

            def max_out(b, j):
                a.wait_ge(n_done, b + 1)
                if not (known(b) and b < 1):
                    a.wait_ge(t_done, b)
                a.copy(negT[:, :], p_neg).then_inc(n_out, 1)
                a.activation(zero_e[j][:, :], negm[j][:, :], ACT.Exp).then_inc(z_ready, 1)

            def exps(b, j):
                a.wait_ge(t_done, b + 1)
                if not (known(b) and b < 1):
                    a.wait_ge(o_done, b)
                a.activation(probs[:, :, :], p_t[:, :, :], ACT.Exp).then_inc(p_ready, 1)

            def attn_out(b, j):
                a.wait_ge(a_done, b + 1)
                a.copy(attnT[:, :, :], p_y[:, 0:256].rearrange("p (c s) -> p c s", c=C)).then_inc(aT_ready, 1)

            def x1q_copy(b):
                for lo, n in ((0, HEAD), (HEAD, WRAP - HEAD)):
                    last = a.copy(x1q[:, :, :, one(b), lo:lo + n].rearrange("p h c o i -> p c h (o i)"),
                                  p_x[:, :, :].rearrange("p c (h i) -> p c h i", i=HEAD)[:, :, :, 0:n])
                last.then_inc(x1q_ready, 1)
            queries_out(0, 0)
            queries_out(1, 1)
            max_out(0, 0)
            exps(0, 0)
            queries_out(2, 0)
            max_out(1, 1)
            exps(1, 1)

            def step(b, j):
                def has(d):
                    return not known(b) or b + d < B
                if not (known(b) and b < 3):
                    a.wait_ge(x1T_done, b - 2)
                attn_out(b, j)
                if has(3):
                    queries_out(b + 3, 1 - j)
                if not (known(b) and b < 3):
                    x1q_copy(b - 3)
                if has(2):
                    max_out(b + 2, j)
                    exps(b + 2, j)
            steps(a, step, first=3, last=3)
            a.wait_ge(x1T_done, B - 2)
            x1q_copy(B - 3)
            for b in (B - 2, B - 1):
                a.wait_ge(x1T_done, b + 1)
                x1q_copy(b)

            def part_out(h, f, j):
                a.wait_ge(part_done, h * 2 + (f + 1))
                if not (known(h) and h < 2):
                    a.wait_ge(back_done, h - 1)
                a.copy(part[j][:, :, f, :, :], p_part[f]).then_inc(part_ready, 1)

            def x2T_copy(h, j):
                a.wait_ge(x2T_done, h + 1)
                if not (known(h) and h < 2):
                    a.wait_ge(x2T_stored[j], (h - j) * 8)
                a.copy(x2T[j][:, :, :], p_x[:, :, :]).then_inc(x2T_ready, 1)

            def second(h, j):
                if not (known(h) and h < 3):
                    x2T_copy(h - 3, 1 - j)
                part_out(h, 0, j)
                part_out(h, 1, j)
            steps(a, second, n=HEADS, first=4, last=0)
            for h in range(HEADS - 3, HEADS):
                x2T_copy(h, h % 2)
            a.wait_ge(route, 1)
            a.activation(sg[:, :, :], best[:, :, 0:TOP], ACT.Sigmoid).then_inc(sg_ready, 1)

            def shared_silu(b, j):
                a.wait_ge(sa_done, b + 1)
                a.activation(ssil[:, :], p_a, ACT.Silu).then_inc(ssil_ready, 1)

            def shared_hT(b, j):
                a.wait_ge(shT_done, b + 1)
                a.copy(shT[:, 0:2, :], p_hT[:, 0:2, :])
                a.copy(shT[0:SP_[2][1], 2, :], p_hT[0:SP_[2][1], 2, :]).then_inc(shT_ready, 1)
            shared_silu(0, 0)

            def shared(b, j):
                shared_hT(b, j)
                if not (known(b) and b == B - 1):
                    shared_silu(b + 1, 1 - j)
            steps(a, shared)

            def xsT_copy(t, j):
                a.wait_ge(xsT_done, t + 1)
                a.copy(xsT[j][:, :, :], p_xs[:, :, :]).then_inc(xsT_ready, 1)

            def silu(t, j):
                a.wait_ge(ab_done, t + 1)
                a.activation(sil[j][:, :], p_ab[j][:, 0:I], ACT.Silu).then_inc(sil_ready, 1)

            def hidT_copy(t, j):
                a.wait_ge(hidT_done, t + 1)
                a.copy(hidT[j][:, :, :], p_hid).then_inc(hidT_ready, 1)
            xsT_copy(0, 0)
            xsT_copy(1, 1)
            silu(0, 0)

            def tile(t, j):
                def has(d):
                    return not known(t) or t + d < NT
                hidT_copy(t, j)
                if has(1):
                    silu(t + 1, 1 - j)
                if has(2):
                    xsT_copy(t + 2, j)
            steps(a, tile, n=NT, first=3, last=2)

            for k in range(0, B, SLOTS):
                a.wait_ge(rs3_ready, 2 * (k // SLOTS + 1))
                for b in range(k, k + SLOTS):
                    a.activation(x2all[:, b, 0:D], z0[:, b, :], ACT.Identity, bias=nm3[:, b:b + 1],
                                 scale=rs3[:, b:b + 1]).then_inc(out_ready, 1)

        @block.gpsimd
        def _(g):
            g.memset(kerp[:, :], 0.0).then_inc(ker_zero, 1)
            g.wait_ge(ker_zero, 1)
            g.dma_start(kerp[:, D:2 * D], ker).then_inc(ker_in, 16)
            g.dma_start(skipc[:, :], skip).then_inc(ker_in, 16)
            g.wait_ge(ker_in, 32)
            g.tensor_tensor(kerp[:, D:D + 1], kerp[:, D:D + 1], skipc[:, :], ALU.add).then_inc(ker_sum, 1)
            g.wait_ge(ker_sum, 1)
            g.dma_start(kerd, kerp[:, :]).then_inc(ker_out, 16)
            g.dma_start(gw[:, :, :], gate).then_inc(gate_in, 16)
            g.dma_start(sw13s[:, :, :], sw13).then_inc(ffn_in, 16)
            g.dma_start(sw2s[:, :, :], sw2).then_inc(ffn_in, 16)
            g.wait_ge(setup, 3)

            def blocks(b, j):
                g.tensor_tensor(kbd[j][:, :, :, :],
                                keyT[:, :, b * KEEP:(b + 1) * KEEP].rearrange("p c (o k) -> p c o k", o=1)
                                .to_broadcast([P, C, 8, KEEP]) if known(b) else
                                keyT[:, :, bass.ds(b * KEEP, KEEP)].rearrange("p c (o k) -> p c o k", o=1)
                                .to_broadcast([P, C, 8, KEEP]),
                                headmask.rearrange("p (c h k) -> p c h k", c=1, k=1).to_broadcast([P, C, 8, KEEP]),
                                ALU.mult).then_inc(kbd_ready, 1)

            def residual(b, j):
                g.tensor_tensor(xbo[j][:, :], xall[:, one(b), 0:D].rearrange("p o d -> p (o d)"), rowb[:, 1, :],
                                ALU.add).then_inc(xbo_ready, 1)

            def norm(b, j):
                g.wait_ge(mv_ready, b + 1)
                g.tensor_tensor(vare[:, :], mv[j][:, 1:2], half[:, 0:1], ALU.add).then_inc(pool, 1)
                g.wait_ge(pool, b + 1)
                g.tensor_tensor(rstd[j][:, :], vare[:, :], half[:, 1:2], ALU.pow).then_inc(rstd_ready, 1)

            for q in range(4):
                g.wait_ge(xall_in[q], 16)
            residual(0, 0)
            residual(1, 1)
            g.wait_ge(key_out, 1)
            blocks(0, 0)
            blocks(1, 1)
            g.wait_ge(t_done, 1)
            blocks(2, 0)
            g.memset(zeros[:, :, :], 0.0).then_inc(zero_ready, 1)
            g.wait_ge(zero_ready, 1)
            g.wait_ge(late_in, 16)
            g.tensor_copy(zeros[:, :, D].bitcast(U32), cst[:, C_PAIR + NB:C_PAIR + NB + 2]).then_inc(zero_ready, 1)
            g.wait_ge(zero_ready, 2)
            xs_z = xsd.rearrange("(t p) d -> p t d", p=P)
            for j in range(2):
                g.dma_start(xs_z[:, j:NT:2, :], zeros[:, j:j + 1, :].to_broadcast([P, (NT + 1 - j) // 2, ROW])
                            ).then_inc(xsd_zeroed, 16)

            def step(b, j):
                if not (known(b) and b < 1):
                    if not known(b) or b + 3 < B:
                        g.wait_ge(t_done, b + 2)
                    g.wait_ge(res_ready, b)
                    norm(b - 1, 1 - j)
                else:
                    g.wait_ge(t_done, 2)
                if not known(b) or b + 3 < B:
                    blocks(b + 3, 1 - j)
                if not (known(b) and (b < 1 or b + 1 >= B)):
                    residual(b + 1, 1 - j)
            steps(g, step, first=3, last=3)
            norm(B - 1, 1)

            g.wait_ge(xsd_zeroed, 32)
            def multiply(h, f, j):
                u = h * 2 + f
                g.wait_ge(head_in[j], 32 + 32 * (h // 2) if known(h) else (h - j) * 16 + 32)
                if not (known(h) and h < 1):
                    g.wait_ge(conv_done, u - 1)
                for c in range(C):
                    k = ctxr[j][:, c, f * BH:(f + 1) * BH, 0:HEAD]
                    a0 = bass.AP(k.tensor, k.offset, [list(k.ap[0]), [WRAP, BH], [0, DIAG], [1, HEAD]])
                    a1 = bass.AP(k.tensor, k.offset, [list(k.ap[0]), [WRAP, BH], [1, DIAG], [1, HEAD]])
                    last = g.tensor_tensor(kv[f][:, c, :, :, :], a0, a1, ALU.mult)
                last.then_inc(kv_made, 1)

            def norm2(b, j):
                g.wait_ge(mv2_ready, b + 1)
                g.tensor_tensor(vare[:, :], mv[j][:, 1:2], half[:, 0:1], ALU.add).then_inc(pool, 1)
                g.wait_ge(pool, B + b + 1 if known(b) else b + (B + 1))
                g.tensor_tensor(rstd[j][:, :], vare[:, :], half[:, 1:2], ALU.pow).then_inc(rstd2_ready, 1)

            g.wait_ge(q_out, B)
            assert HEADS == E

            def second(h, j):
                g.dma_start(w13s[:, :, one(h), :], w13[:, :, one(h), :]).then_inc(w13_in, 16)
                multiply(h, 0, j)
                multiply(h, 1, j)
                if not (known(h) and h < 3):
                    norm2(h - 3, 1 - j)
            steps(g, second, n=HEADS, first=4, last=0)
            g.wait_ge(prod_done, 2 * HEADS)
            g.dma_start(w2s, w2).then_inc(w2_in, 16)
            for h in range(HEADS - 3, HEADS):
                norm2(h, h % 2)

            def norm3(k):
                r = slice(k * SLOTS, (k + 1) * SLOTS)
                g.wait_ge(mv3_ready, k + 1)
                g.tensor_scalar(nm3[:, r], mv3[:, r, 0], -1.0, None, ALU.mult).then_inc(ve3_ready, 1)
                g.tensor_tensor(ve3[:, r], mv3[:, r, 1], half[:, 0:1].to_broadcast([P, SLOTS]), ALU.add
                                ).then_inc(ve3_ready, 1)
                g.wait_ge(ve3_ready, 2 * (k + 1))
                g.tensor_tensor(rs3[:, r], ve3[:, r], half[:, 1:2].to_broadcast([P, SLOTS]), ALU.pow
                                ).then_inc(rs3_ready, 1)
                g.wait_ge(rs3_ready, 2 * k + 1)
                g.tensor_tensor(nm3[:, r], nm3[:, r], rs3[:, r], ALU.mult).then_inc(rs3_ready, 1)

            g.wait_ge(xsd_zeroed, 32)
            for j in range(2):
                g.wait_ge(x2_stored[j], 8 * B)
            g.wait_ge(pos_ready, 1)
            g.wait_ge(wts_ready, 1)
            for i in range(TOP):
                if i > 0:
                    g.wait_ge(scattered, 16 * B * i)
                g.tensor_copy(x2all[:, :, D].bitcast(U32), cst[:, C_PAIR + i * B:C_PAIR + (i + 1) * B]
                              ).then_inc(pairs_next, 1)
                g.tensor_copy(x2all[:, :, D + 1], wts[:, :, i]).then_inc(pairs_next, 1)
                g.wait_ge(pairs_next, 2 * (i + 1))
                for b in range(B):
                    n = b * TOP + i
                    g.indirect_dma_start(xsd, bass.IndirectOffsetOnAxis(pos[:, n:n + 1], 0), x2all[:, b, :], None
                                         ).then_inc(scattered, 16)

            def places(t, k):
                g.wait_ge(xs_in[k % 2], 16 + 16 * (t // 2) if known(t) else (t - k % 2) * 8 + 16)
                if not (known(t) and t < 4):
                    g.wait_ge(ys_stored[k % 2], (t - 2 - k % 2) * 8)
                g.tensor_tensor(share[k][:, :], xs[k % 2][:, D + 1:D + 2], cst[:, C_M:C_M + 1], ALU.add)
                g.tensor_tensor(idr[k][:, :], xs[k % 2][:, D:D + 1].bitcast(U32), cst[:, C_M:C_M + 1].bitcast(U32),
                                ALU.add).then_inc(id_ready, 1)

            def store_tile(t, k):
                g.wait_ge(ys_ready, t + 1)
                g.wait_ge(id_ready, min(t + 2, NT) if known(t) else t + 2)
                if not (known(t) and t + 2 >= NT):
                    places(t + 2, (k + 2) % 4)
                g.indirect_dma_start(ypd, bass.IndirectOffsetOnAxis(idr[k][:, 0:1], 0), ys[k % 2][:, :], None
                                     ).then_inc(ys_stored[k % 2], 16)
            places(0, 0)
            places(1, 1)
            steps(g, store_tile, n=NT, first=4, last=3, ways=4)
            def pairs(k):
                r = slice(k * SLOTS, (k + 1) * SLOTS)
                g.wait_ge(y_in[k], 16 * TOP)
                g.tensor_tensor(yg[:, 0, r, :], yg[:, 0, r, :], yg[:, 1, r, :], ALU.add).then_inc(pair_sum, 1)
            pairs(0)
            for k in range(B // SLOTS):
                if k + 1 < B // SLOTS:
                    pairs(k + 1)
                norm3(k)


def tables():
    import numpy as np
    t = np.zeros((P, C_W), np.float32)
    i = np.arange(P)
    t[:, C_ID:C_ID + P] = np.eye(P)
    t[:, C_TRI:C_TRI + P] = i[:, None] <= i[None, :]
    t[:, C_IOTA:C_IOTA + KEEP] = np.arange(1, KEEP + 1)
    t[:, C_HM:C_HM + 8] = i[:, None] // HD == np.arange(8)[None, :]
    t[:, C_ONES:C_ONES + P] = 1.0
    t[:, C_N:C_N + 64] = np.arange(64)
    t[:, C_M:C_M + 16] = np.arange(16) * P
    t[:, C_NEW:C_NEW + E * NB] = np.arange(E * NB) % NB != 0
    t[:, C_PAIR:C_PAIR + NB + 2] = i[:, None] + np.arange(NB + 2) * P
    return t


def tables_bf16(bf16):
    import numpy as np
    t = np.zeros((P, B_W), np.float32)
    t[:, 0:P] = np.eye(P)
    n = np.arange(GROUPS * P)
    t[0:2 * NH, P:B_STRI] = np.arange(2 * NH)[:, None] % NH == (n // P * 4 + n % P // KEEP)[None, :]
    t[:, B_STRI:B_ONES] = np.arange(P)[:, None] < np.arange(P)[None, :]
    t[:, B_ONES:] = 1.0
    return t.astype(bf16)


def kernel(**inputs):
    import numpy as np
    import concourse.bacc as bacc
    from concourse.bass_utils import run_bass_kernel_spmd

    nc = bacc.Bacc("TRN2", target_bir_lowering=False, num_devices=1)
    a = {k: np.asarray(v) for k, v in inputs.items()}
    x = a["x"]
    bq, bk, bi = a["L0_attn_bq"], a["L0_attn_bk"], a["L0_attn_bi"]
    arrays = {
        "x": x,
        "constb": tables_bf16(a["L0_ffn_w1"].dtype),
        "xT": np.ascontiguousarray(x.reshape(4, 4, S, C, P).transpose(0, 4, 3, 1, 2).reshape(4, P, C, 4 * S)),
        "ctx": np.ascontiguousarray(np.take(
            a["ctx_2048"].reshape(B, HEADS, HEAD, C, P)[:, :, :, :, ::-1], np.arange(WRAP) % HEAD, axis=2
        ).transpose(1, 4, 3, 0, 2)),
        "ker": a["L0_xattn_ssm_kernel"],
        "skip": a["L0_xattn_D"].reshape(HEADS, 1),
        "Wq": a["L0_attn_Wq"], "Wk": a["L0_attn_Wk"], "Wv": a["L0_attn_Wv"], "Wo": a["L0_attn_Wo"],
        "cols": np.ascontiguousarray(np.concatenate([bq.reshape(C, P).T, bk.reshape(C, P).T,
                                                     np.broadcast_to(bi, (P, 1))], axis=1)),
        "rows": np.stack([a["L0_attn_Wi"].reshape(-1), a["L0_attn_bo"], a["L0_attn_bv"]]),
        "consts": tables(),
        "gate": np.ascontiguousarray(a["L0_ffn_gate_w"].T.reshape(C, P, E).transpose(1, 0, 2)),
        "w13": np.ascontiguousarray(np.concatenate([a["L0_ffn_w1"], a["L0_ffn_w3"]], axis=1)
                                    .reshape(E, 2 * I, C, P).transpose(3, 2, 0, 1)),
        "w2": np.ascontiguousarray(a["L0_ffn_w2"].reshape(E, D, 2, KI).transpose(3, 0, 2, 1)),
        "sw13": np.ascontiguousarray(np.concatenate([a["L0_ffn_sw1"], a["L0_ffn_sw3"]], axis=0)
                                     .reshape(2 * SI, C, P).transpose(2, 1, 0)),
        "sw2": np.ascontiguousarray(np.pad(a["L0_ffn_sw2"], ((0, 0), (0, 3 * P - SI))).reshape(D, 3, P)
                                    .transpose(2, 1, 0)),
    }
    args = [nc.dram_tensor(f"in_{n}_dram", v.shape, mybir.dt.from_np(v.dtype), kind="ExternalInput").ap()
            for n, v in arrays.items()]
    out = nc.dram_tensor("out_0_dram", (B, S, D), F32, kind="ExternalOutput").ap()
    decoder_layer(nc, *args, out)
    r = run_bass_kernel_spmd(nc, [{f"in_{n}_dram": v for n, v in arrays.items()}], core_ids=[0])
    return r.results[0]["out_0_dram"]
```

```python
from contextlib import ExitStack

import concourse.bass as bass
from concourse import mybir

F32 = mybir.dt.float32
BF16 = mybir.dt.bfloat16
U32 = mybir.dt.uint32
ALU = mybir.AluOpType
ACT = mybir.ActivationFunctionType
AX = mybir.AxisListType

P = 128
B, S, D = 16, 128, 256
C = D // P
NH, HD = 16, 16
KEEP = 32
GROUPS = NH // 4
EPS = 1e-5
SCALE = HD ** -0.5
NEG = -3.0e38
HEADS, HEAD = 16, 8
DIAG = HEAD // 2 + 1
WRAP = HEAD + DIAG - 1
BH = B // 2
E, TOP, I = 16, 2, 176
KI = I // 2
SI = 2 * I
SP_ = [(0, P), (P, P), (2 * P, SI - 2 * P)]
NB = B * TOP
NT = NB + E - 1
FIRST, TURN = 3, 10
NG = (NT - FIRST - 4) // TURN
ROW = D + 2
ROWS = DIAG + 2 * 3
W2_PARTS = 8
BY_PE = 4

C_ID, C_TRI, C_IOTA, C_HM, C_ONES, C_N = 0, 128, 256, 288, 296, 424
C_M = C_N + 64
C_NEW = C_M + 16
C_PAIR = C_NEW + E * NB
C_W = C_PAIR + NB + 2


B_STRI = P + GROUPS * P
B_ONES = B_STRI + P
B_W = B_ONES + P


def decoder_layer(nc, x, constb, xT, ctxd, ker, skip, Wq, Wk, Wv, Wo, cols, rows, consts, gate, w13, w2, sw13, sw2, out):
    with ExitStack() as ctx:
        def sb(name, shape, dt=F32):
            return ctx.enter_context(nc.sbuf_tensor(name, shape, dt))

        def ps(name, shape, dt=F32):
            return ctx.enter_context(nc.psum_tensor(name, shape, dt))

        def sem(name):
            return ctx.enter_context(nc.semaphore(name))

        cst = sb("cst", [P, C_W])
        cstb = sb("cstb", [P, B_W], BF16)
        identb = cstb[:, 0:P]
        headrow = cstb[0:2 * NH, P:P + GROUPS * P]
        ident = cst[:, C_ID:C_ID + P]
        tri = cst[:, C_TRI:C_TRI + P]
        iota = cst[:, C_IOTA:C_IOTA + KEEP]
        headmask = cst[:, C_HM:C_HM + 8]
        roomy = sb("roomy", [P, E * 2 * D])
        wq, wk, wv, wo = (roomy[:, k * C * D:(k + 1) * C * D].rearrange("p (c n) -> p c n", c=C) for k in range(4))
        colb = sb("colb", [P, 5])
        bqs = sb("bqs", [P, C])
        rowb = sb("rowb", [P, 3, D])
        xall = sb("xall", [P, B, ROW])
        imp = sb("imp", [P, B])
        
        impT = sb("impT", [B, 5, P])
        top8 = sb("top8", [B, 4, 8])
        chosenT = sb("chosenT", [B, P])
        chosen = sb("chosen", [P, B])
        place = sb("place", [P, B])
        half = sb("half", [P, 2])

        xbo = [sb(f"xbo{j}", [P, D]) for j in range(2)]
        qT = [sb(f"qT{j}", [P, C, S]) for j in range(2)]
        kbd = [sb(f"kbd{j}", [P, C, 8, KEEP]) for j in range(2)]
        neg2 = [sb(f"neg2{j}", [P, 2, NH], BF16) for j in range(2)]
        negm = [sb(f"negm{j}", [P, NH]) for j in range(2)]
        zero_e = [sb(f"zero_e{j}", [P, NH]) for j in range(2)]
        mx = sb("mx", [P, NH])
        negT = sb("negT", [2 * NH, S], BF16)
        probs = sb("probs", [P, GROUPS, S])
        den = sb("den", [P, NH])
        rec = sb("rec", [P, NH])
        attn = sb("attn", [P, D])
        attnT = sb("attnT", [P, C, S])
        res = [sb(f"res{j}", [P, D]) for j in range(2)]
        stats = sb("stats", [P, 6])
        mv = [sb(f"mv{j}", [P, 2]) for j in range(2)]
        vare = sb("vare", [P, 1])
        rstd = [sb(f"rstd{j}", [P, 1]) for j in range(2)]

        x1r = [sb(f"x1r{j}", [P, D]) for j in range(2)]
        x1q = roomy[:, 4 * C * D:4 * C * D + HEADS * C * B * WRAP].rearrange(
            "p (h c b w) -> p h c b w", h=HEADS, c=C, b=B)
        kerp = sb("kerp", [HEADS, 2 * D])
        skipc = sb("skipc", [HEADS, 1])
        ctxr = [sb(f"ctxr{j}", [P, C, B, WRAP]) for j in range(2)]
        toe = [sb(f"toe{j}", [P, 2 * P]) for j in range(2)]
        NKV, NPR = BH * DIAG * HEAD, BH * ROWS * HEAD
        room = sb("room", [P, 2 * C * (NKV + NPR)])
        kv = [room[:, j * C * NKV:(j + 1) * C * NKV].rearrange("p (c b d i) -> p c b d i", c=C, b=BH, d=DIAG)
              for j in range(2)]
        prod = [room[:, 2 * C * NKV + j * C * NPR:2 * C * NKV + (j + 1) * C * NPR].rearrange(
            "p (c b s i) -> p c b s i", c=C, b=BH, s=ROWS) for j in range(2)]
        pick = room[:, 0:B * P].rearrange("p (q n k) -> p q n k", q=4, n=4)
        picked = room[:, B * P:B * P + 4 * D].rearrange("p (q d) -> p q d", q=4)
        VBN = B * NH * (HD + 1)
        shared_room = sb("shared_room", [P, VBN + 2 * C * B * KEEP])
        vbd = shared_room[:, 0:VBN].rearrange("p (b g r d) -> p b g r d", b=B, g=GROUPS, r=4)
        xsel = shared_room[:, VBN:VBN + C * B * KEEP].rearrange("p (c n) -> p c n", c=C)
        keyT = shared_room[:, VBN + C * B * KEEP:VBN + 2 * C * B * KEEP].rearrange("p (c n) -> p c n", c=C)
        conv = [shared_room[:, j * D:(j + 1) * D].rearrange("p (c f b i) -> p c f b i", c=C, f=2, b=BH) for j in range(2)]
        part = [sb(f"part{j}", [P, C, 2, BH, HEAD]) for j in range(2)]
        x1s = [sb(f"x1s{j}", [P, D]) for j in range(2)]
        res2 = [sb(f"res2{j}", [P, D]) for j in range(2)]
        x2r = [sb(f"x2r{j}", [P, D]) for j in range(2)]

        used = [0]

        def late(*shape):
            names = "abc"[:len(shape)]
            size = 1
            for d in shape:
                size *= d
            part = room[:, used[0]:used[0] + size]
            used[0] += size
            if len(shape) == 1:
                return part
            return part.rearrange(f"p ({' '.join(names)}) -> p {' '.join(names)}", **dict(zip(names[1:], shape[1:])))
        gw = sb("gw", [P, C, E])
        w13room = sb("w13room", [P, C * E * 2 * I])
        W13 = C * E * I
        w13s = w13room[:, 0:W13].bitcast(BF16).rearrange("p (c e n) -> p c e n", c=C, e=E)
        xp = [w13room[:, W13 + k * 3 * D // 2:W13 + (k + 1) * 3 * D // 2].bitcast(BF16).rearrange(
            "p (q c s) -> p q c s", q=3, c=C) for k in range(2)]
        rest = [sb(f"rest{j}", [P, C, S]) for j in range(2)]
        w2s = roomy[0:KI, :].rearrange("p (e k n) -> p e k n", e=E, k=2)
        sw13s = sb("sw13s", [P, C, 2 * SI], BF16)
        sw2s = sb("sw2s", [P, 3, D])
        zeros = room[:, 0:2 * ROW].rearrange("p (o d) -> p o d", o=2)
        x2T = [sb(f"x2T{j}", [P, C, S]) for j in range(2)]
        x2all = xall
        early = w13room
        qall = early[:, B * D:2 * B * D].rearrange("p (c n) -> p c n", c=C)
        xg = [early[:, (2 * B + 4 * j) * D:(2 * B + 4 * (j + 1)) * D].rearrange("p (c n) -> p c n", c=C) for j in range(2)]
        junk = w13room[:, 0:B * D].rearrange("p (b d) -> p b d", b=B)
        z0 = shared_room[:, 0:B * D].rearrange("p (b d) -> p b d", b=B)
        logit = sb("logit", [P, B, E])
        best = sb("best", [P, B, 8])
        bestix = sb("bestix", [P, B, 8], U32)
        ixf = sb("ixf", [P, NB])
        hot = sb("hot", [P, NB, E], BF16)
        upto = late(E, NB)
        slot = late(NB, E)
        over = late(E, 16)
        tiles = sb("tiles", [P, E])
        endt = sb("endt", [P, E])
        base = sb("base", [P, E])
        posf = sb("posf", [P, NB])
        pos = sb("pos", [P, NB], U32)
        ended = sb("ended", [1, NT, E])
        ownf = sb("ownf", [1, NT])
        owner = sb("owner", [1, NT], mybir.dt.int32)
        sg = sb("sg", [P, B, TOP])
        sgsum = sb("sgsum", [P, B])
        wts = sb("wts", [P, B, TOP])
        ssil = probs[:, :, :].rearrange("p g s -> p (g s)")[:, 0:SI]
        sh = sb("sh", [P, SI])
        shT = sb("shT", [P, 3, S])
        xs = [late(ROW) for j in range(2)]
        idr = [sb(f"idr{k}", [P, 1], U32) for k in range(8)]
        share = [sb(f"share{k}", [P, 1]) for k in range(8)]
        x2S = qT
        sil = [late(I) for j in range(2)]
        hid = [late(I) for j in range(2)]
        hidT = [late(2, P)[0:KI] for j in range(2)]
        ys = [late(D) for j in range(2)]
        SLOTS = 2
        yg = w13room[:, 0:B * TOP * D].rearrange(
            "p (t b d) -> p t b d", b=B, t=TOP)
        st3 = sb("st3", [P, B, 6])
        mv3 = sb("mv3", [P, B, 2])
        ve3 = sb("ve3", [P, B])
        rs3 = sb("rs3", [P, B])
        nm3 = sb("nm3", [P, B])
        x2Td = nc.dram_tensor("x2Td", (B, P, C, S), F32).ap()
        xsd = nc.dram_tensor("xsd", (NT * P, ROW), F32).ap()
        ypd = nc.dram_tensor("ypd", ((NB + 2) * P, D), F32).ap()

        kerd = nc.dram_tensor("kerd", (HEADS, 2 * D), F32).ap()
        x1d = nc.dram_tensor("x1d", (B, S, D), F32).ap()

        p_kv = ps("p_kv", [P, 512])
        p_qs = ps("p_qs", [P, 2, 512])
        p_q = p_qs[:, 0, :].rearrange("p (c s) -> p c s", c=C)
        p_s = p_qs[:, 1, :]
        p_valq = p_qs[:, :, :].rearrange("p a (c s) -> p (a c) s", c=C)
        p_t = ps("p_t", [P, GROUPS, S])
        p_o = ps("p_o", [P, 512])
        p_y = ps("p_y", [P, 512])
        p_x2 = ps("p_x2", [P, 512])
        p_x = p_x2[:, 0:C * S].rearrange("p (c s) -> p c s", c=C)
        p_8 = ps("p_8", [P, 512])
        p_conv = [[p_kv[:, 0:320], p_q[:, :, :].rearrange("p c s -> p (c s)")[:, 0:320]],
                  [p_s[:, 0:320], p_8[:, 0:320]]]
        p_back = p_o[:, 0:256]
        p_proj = p_qs[:, 0, 0:D]
        p_logit = p_o[:, 2 * P:2 * P + E]
        p_part = [bank[:, 0:P].rearrange("p (c b i) -> p c b i", c=C, b=BH)
                  for bank in (p_t[:, :, :].rearrange("p g s -> p (g s)"), p_y)]
        p_rank, p_sum = p_o[:, :], p_y[:, :]
        p_fin = {0: p_8[:, :], 2: p_o[:, :], 4: p_y[:, :], 6: p_x2[:, :],
                 B // SLOTS - 1: p_t[:, :, :].rearrange("p g s -> p (g s)")}
        PAIRS_PE = sorted(p_fin)
        p_a, p_b = p_kv[:, 0:SI], p_q[:, :, :].rearrange("p c s -> p (c s)")[:, 0:SI]
        p_hT = p_s[:, 0:3 * S].rearrange("p (k s) -> p k s", k=3)
        p_z = p_t[:, 0:2, :].rearrange("p g s -> p (g s)")
        p_xs = p_x
        p_ab = [p_kv[:, 0:SI], p_q[:, :, :].rearrange("p c s -> p (c s)")[:, 0:SI]]
        p_hid = p_s[0:KI, 0:2 * P].rearrange("p (k s) -> p k s", k=2)
        p_ye = p_t[:, 0:2, :].rearrange("p g s -> p (g s)")
        p_qall = [[p_kv[:, :], p_8[:, :]], [p_t[:, :, :].rearrange("p g s -> p (g s)"), p_x2[:, :]]]
        p_picked = [p_kv[:, :].rearrange("p (q d) -> p q d", q=2), p_8[:, :].rearrange("p (q d) -> p q d", q=2)]
        p_sel = [p_y[:, :], p_o[:, :]]
        p_key = [p_t[:, :, :].rearrange("p g s -> p (g s)"), p_x2[:, :]]
        p_val = [p_valq[:, 0:2, :], p_valq[:, 2:4, :]]
        p_neg = p_s[0:2 * NH, 0:S // 2].bitcast(BF16)
        o_v = p_o[:, 0:NH * (HD + 1)].rearrange("p (g r d) -> p g r d", g=GROUPS, r=4)

        cst_in = sem("cst_in")
        w_in = sem("w_in")
        xall_in = [sem(f"xall_in{q}") for q in range(4)]
        wq_in = sem("wq_in")
        cstb_in = sem("cstb_in")
        late_in = sem("late_in")
        x_in = [sem(f"x_in{j}") for j in range(2)]
        qall_done = sem("qall_done")
        qall_out = sem("qall_out")
        gate_in = sem("gate_in")
        w13_in = sem("w13_in")
        imp_done = sem("imp_done")
        setup = sem("setup")
        impT_done = sem("impT_done")
        mask_done = sem("mask_done")
        maskT_done = sem("maskT_done")
        maskT_copied = sem("maskT_copied")
        count_done = sem("count_done")
        pick_done = sem("pick_done")
        dve = sem("dve")
        gathered = sem("gathered")
        picked_out = sem("picked_out")
        turned = sem("turned")
        xsel_out = sem("xsel_out")
        key_done = sem("key_done")
        key_out = sem("key_out")
        val_done = sem("val_done")
        val_out = sem("val_out")
        kbd_ready = sem("kbd_ready")
        neg2_ready = sem("neg2_ready")
        q_out = sem("q_out")
        s_done = sem("s_done")
        negm_ready = sem("negm_ready")
        n_done = sem("n_done")
        n_out = sem("n_out")
        z_ready = sem("z_ready")
        t_done = sem("t_done")
        p_ready = sem("p_ready")
        o_done = sem("o_done")
        attn_ready = sem("attn_ready")
        a_done = sem("a_done")
        aT_ready = sem("aT_ready")
        y_done = sem("y_done")
        xbo_ready = sem("xbo_ready")
        res_ready = sem("res_ready")
        mv_ready = sem("mv_ready")
        pool = sem("pool")
        rstd_ready = sem("rstd_ready")
        x1_ready = sem("x1_ready")
        out_sem = sem("out_sem")
        x1T_done = sem("x1T_done")
        x1q_ready = sem("x1q_ready")
        x1_stored = [sem(f"x1_stored{j}") for j in range(2)]
        ker_in = sem("ker_in")
        ker_zero = sem("ker_zero")
        ker_sum = sem("ker_sum")
        ker_out = sem("ker_out")
        head_in = [sem(f"head_in{j}") for j in range(2)]
        kv_made = sem("kv_made")
        conv_done = sem("conv_done")
        prod_done = sem("prod_done")
        sum_done = sem("sum_done")
        x1_back = [sem(f"x1_back{j}") for j in range(2)]
        part_done = sem("part_done")
        part_ready = sem("part_ready")
        back_done = sem("back_done")
        res2_ready = sem("res2_ready")
        stats2 = sem("stats2")
        mv2_ready = sem("mv2_ready")
        rstd2_ready = sem("rstd2_ready")
        x2_ready = sem("x2_ready")
        x2T_done = sem("x2T_done")
        x2T_ready = sem("x2T_ready")
        logit_done = sem("logit_done")
        logit_ready = sem("logit_ready")
        ffn_in = sem("ffn_in")
        zero_ready = sem("zero_ready")
        xsd_zeroed = sem("xsd_zeroed")
        route = sem("route")
        hot_ready = sem("hot_ready")
        rank_done = sem("rank_done")
        pos_ready = sem("pos_ready")
        owner_ready = sem("owner_ready")
        scattered = [sem(f"scattered{k}") for k in range(2)]
        wts_ready = sem("wts_ready")
        sg_ready = sem("sg_ready")
        sa_done = sem("sa_done")
        ssil_ready = sem("ssil_ready")
        sh_ready = sem("sh_ready")
        shT_done = sem("shT_done")
        shT_ready = sem("shT_ready")
        z_done = sem("z_done")
        z0_ready = sem("z0_ready")
        xsT_done = sem("xsT_done")
        high_ready = sem("high_ready")
        rest_ready = sem("rest_ready")
        mid_ready = sem("mid_ready")
        low_ready = sem("low_ready")
        shigh_ready = sem("shigh_ready")
        srest_ready = sem("srest_ready")
        smid_ready = sem("smid_ready")
        slow_ready = sem("slow_ready")
        ab_done = sem("ab_done")
        sil_ready = sem("sil_ready")
        hid_ready = sem("hid_ready")
        hidT_done = sem("hidT_done")
        hidT_ready = sem("hidT_ready")
        ye_done = sem("ye_done")
        ys_ready = sem("ys_ready")
        fin = sem("fin")
        mv3_ready = sem("mv3_ready")
        ve3_ready = sem("ve3_ready")
        rs3_ready = sem("rs3_ready")
        st3_ready = sem("st3_ready")
        pair_sum = sem("pair_sum")
        out_ready = sem("out_ready")
        out_stored = sem("out_stored")
        w2_in = sem("w2_in")
        x2T_stored = [sem(f"x2T_stored{j}") for j in range(2)]
        id_ready = sem("id_ready")
        pairs_next = sem("pairs_next")
        fin_done = sem("fin_done")
        x2T_in = [sem(f"x2T_in{j}") for j in range(2)]
        xs_in = [sem(f"xs_in{j}") for j in range(2)]
        ys_stored = [sem(f"ys_stored{j}") for j in range(2)]
        y_in = [sem(f"y_in{k}") for k in range(B // SLOTS)]
        x2_stored = [sem(f"x2_stored{j}") for j in range(2)]

        x_v = x.rearrange("b s d -> s b d")

        def steps(eng, step, n=B, first=2, last=2, ways=2):
            for b in range(first):
                step(b, b % ways)
            assert (n - first - last) % ways == 0
            with eng.Fori(0, (n - first - last) // ways) as i:
                for k in range(ways):
                    step(i * ways + (first + k), (first + k) % ways)
            for b in range(n - last, n):
                step(b, b % ways)

        def at(ap, b):
            if known(b):
                return ap[b]
            names = "pqrs"[:len(ap.shape) - 1]
            part = ap[(bass.ds(b, 1),) + (slice(None),) * (len(ap.shape) - 1)]
            return part.rearrange(f"o {' '.join(names)} -> (o {names[0]}) {' '.join(names[1:])}")

        def one(b):
            return slice(b, b + 1) if known(b) else bass.ds(b, 1)

        def place_values(copy, n, r):
            src = p_valq[n * KEEP:(n + 1) * KEEP, :, :].rearrange("p n (g r d) -> p n g r d", g=GROUPS, r=4)[:, :, :, r]
            dst = vbd[r * KEEP:(r + 1) * KEEP, :, :, r, 0:HD].rearrange("p (n q) g d -> p q n g d", q=4)[:, n]
            return copy(dst, src)

        def known(b):
            return isinstance(b, int)

        block = ctx.enter_context(nc.Block())

        @block.sync
        def _(sp):
            sp.dma_start(rowb[:, :, :], rows.rearrange("(o a) d -> o a d", o=1).to_broadcast([P, 3, D])).then_inc(cst_in, 16)
            sp.dma_start(colb[:, :], cols).then_inc(cst_in, 16)
            sp.dma_start(cst[:, 0:C_NEW], consts[:, 0:C_NEW]).then_inc(cst_in, 16)
            for q in range(4):
                sp.dma_start(xall[:, q * 4:q * 4 + 4, 0:D], x_v[:, q * 4:q * 4 + 4, :]).then_inc(xall_in[q], 16)
            sp.dma_start(cstb[:, :], constb).then_inc(cstb_in, 16)
            sp.wait_ge(x_in[1], 32)
            sp.dma_start(cst[:, C_NEW:C_W], consts[:, C_NEW:C_W]).then_inc(late_in, 16)

            def store(b, j):
                sp.wait_ge(x1_ready, b + 1)
                sp.dma_start(at(x1d, b), x1r[j][:, :]).then_inc(x1_stored[j], 16)
            def load_head(h, j):
                if known(h) and h < 2:
                    if h == 0:
                        sp.wait_ge(ker_out, 16)
                else:
                    sp.wait_ge(kv_made, h * 2 - 2)
                    sp.wait_ge(conv_done, h * 2 - 2)
                sp.dma_start(ctxr[j][:, :, :, :], at(ctxd, h)).then_inc(head_in[j], 16)
                row = kerd[one(h), D - P + 1:D - P + 2]
                sp.dma_start(toe[j][:, :], bass.AP(row.tensor, row.offset, [[1, P], [1, 2 * P]])).then_inc(head_in[j], 16)

            load_head(0, 0)
            load_head(1, 1)
            steps(sp, store)

            def load_x1(h, j):
                if known(h) and h < 2:
                    if h == 0:
                        for k in range(2):
                            sp.wait_ge(x1_stored[k], 8 * B)
                else:
                    sp.wait_ge(res2_ready, h - 1)
                sp.dma_start(x1s[j][:, :], x1d[:, h * HEAD:(h + 1) * HEAD, :] if known(h) else
                             x1d[:, bass.ds(h * HEAD, HEAD), :]).then_inc(x1_back[j], 16)

            def store_x2(h, j):
                sp.wait_ge(x2_ready, h + 1)
                sp.dma_start(x2all[:, one(h), 0:D].rearrange("p o d -> p (o d)"), x2r[j][:, :]).then_inc(x2_stored[j], 16)

            def load_x2T(b, j):
                if known(b) and b < 2:
                    sp.wait_ge(x2T_stored[b], 16)
                else:
                    sp.wait_ge(srest_ready, b - 1)
                sp.dma_start(x2S[j][:, :, :], at(x2Td, b)).then_inc(x2T_in[j], 16)

            def store_x2T(h, j):
                sp.wait_ge(x2T_ready, h + 1)
                sp.dma_start(at(x2Td, h), x2T[j][:, :, :]).then_inc(x2T_stored[j], 16)

            def second(h, j):
                if not (known(h) and h < 2):
                    load_head(h, j)
                if not (known(h) and h < 1):
                    load_x1(h - 1, 1 - j)
                if not (known(h) and h < 4):
                    store_x2(h - 4, j)
                if not (known(h) and h < 5):
                    store_x2T(h - 5, 1 - j)
                if known(h) and h == HEADS - 1:
                    for b in range(2):
                        load_x2T(b, b)
            steps(sp, second, n=HEADS, first=5, last=1)
            load_x1(HEADS - 1, 1)
            store_x2(HEADS - 4, 0)
            store_x2T(HEADS - 5, 1)
            for h in range(HEADS - 4, HEADS):
                if h + 1 < HEADS:
                    store_x2(h + 1, 1 - h % 2)
                store_x2T(h, h % 2)
            for j in range(2):
                sp.wait_ge(x2T_stored[j], 8 * HEADS)
            steps(sp, lambda b, j: load_x2T(b + 2, j), n=HEADS - 2)

            xs_v = xsd.rearrange("(t p) d -> t p d", p=P)

            def load_tile(t, j):
                if known(t) and t < 2:
                    if t == 0:
                        for k in range(2):
                            sp.wait_ge(scattered[k], 16 * NB // 2)
                else:
                    sp.wait_ge(xsT_done, t - 1)
                    sp.wait_ge(id_ready, t - 1)
                sp.dma_start(xs[j][:, :], at(xs_v, t)).then_inc(xs_in[j], 16)
            steps(sp, load_tile, n=NT, last=1)
            for j in range(2):
                sp.wait_ge(ys_stored[j], 16 * ((NT + 1 - j) // 2))
            yp_v = ypd[0:NB * P, :].rearrange("(i b p) d -> i p b d", i=TOP, p=P)
            for k in range(B // SLOTS):
                for i in range(TOP):
                    sp.dma_start(yg[:, i, k * SLOTS:(k + 1) * SLOTS, :],
                                 at(yp_v, i)[:, k * SLOTS:(k + 1) * SLOTS, :]).then_inc(y_in[k], 16)
            for h in range(HEADS):
                sp.wait_ge(out_ready, h + 1)
                sp.dma_start(out[:, h * HEAD:(h + 1) * HEAD, :], x2all[:, h, 0:D]).then_inc(out_stored, 16)
            sp.wait_ge(out_stored, 16 * HEADS)

        @block.tensor
        def _(pe):
            def queries(g):
                if g == 0:
                    pe.wait_ge(wq_in, 16)
                pe.wait_ge(x_in[g % 2], 16 + 16 * (g // 2))
                if g == 2:
                    pe.wait_ge(picked_out, 2)
                for m in range(C):
                    for c in range(C):
                        last = pe.matmul(p_qall[g % 2][m], wq[:, c, m * P:(m + 1) * P], xg[g % 2][:, c, :],
                                         start=(c == 0), stop=(c == C - 1))
                last.then_inc(qall_done, 1)
            pe.wait_ge(cst_in, 48)
            queries(0)
            pe.wait_ge(imp_done, 1)
            pe.transpose(p_y[0:B, 0:P], imp[:, :], ident).then_inc(impT_done, 1)
            queries(1)
            pe.wait_ge(mask_done, 1)
            pe.transpose(p_s[:, 0:B], chosenT[:, :], cst[0:B, C_ID:C_ID + B]).then_inc(maskT_done, 1)
            pe.wait_ge(maskT_copied, 1)
            pe.matmul(p_o[:, 0:B], tri, chosen[:, :], start=True, stop=True).then_inc(count_done, 1)
            pe.wait_ge(setup, 3)
            pe.wait_ge(pick_done, 1)
            pe.wait_ge(qall_out, 1)
            for q in range(4):
                for n in range(4):
                    last = pe.matmul(p_picked[q // 2][:, q % 2, :], pick[:, q, n, :], xall[:, q * 4 + n, 0:D],
                                     start=(n == 0), stop=(n == 3))
                if q % 2 == 1:
                    last.then_inc(gathered, 1)
            pe.wait_ge(picked_out, 2)
            for c in range(C):
                for q in range(4):
                    last = pe.transpose(p_sel[c][:, q * P:(q + 1) * P], picked[:, q, c * P:(c + 1) * P], ident)
                last.then_inc(turned, 1)
            pe.wait_ge(w_in, 48)
            pe.wait_ge(cstb_in, 16)
            queries(2)
            pe.wait_ge(qall_out, 2)
            pe.wait_ge(xsel_out, C)
            for m in range(C):
                for c in range(C):
                    last = pe.matmul(p_key[m], wk[:, c, m * P:(m + 1) * P], xsel[:, c, :],
                                     start=(c == 0), stop=(c == C - 1))
            last.then_inc(key_done, 1)
            for n in range(B // 4):
                o = p_val[n // 2][:, n % 2, :]
                for c in range(C):
                    pe.matmul(o, xsel[:, c, n * P:(n + 1) * P], wv[:, c, :], start=(c == 0), stop=False)
                last = pe.matmul(o, cst[0:1, C_ONES:C_ONES + P], rowb[0:1, 2, :], start=False, stop=True)
            last.then_inc(val_done, 1)
            pe.wait_ge(key_out, 1)
            queries(3)
            pe.wait_ge(val_out, 2)
            pe.wait_ge(qall_out, 4)

            def scores(b, j):
                pe.wait_ge(kbd_ready, b + 1)
                pe.wait_ge(q_out, b + 1)
                if not (known(b) and b < 1):
                    pe.wait_ge(n_out, b)
                for c in range(C):
                    last = pe.matmul(p_s[:, c * 256:(c + 1) * 256], qT[j][:, c, :], kbd[j][:, c, :, :],
                                     start=True, stop=True)
                last.then_inc(s_done, 1)

            def turn_max(b, j):
                pe.wait_ge(neg2_ready, b + 1)
                pe.transpose(p_neg, neg2[j][:, :, :].rearrange("p t h -> p (t h)"), identb).then_inc(n_done, 1)

            def scores_T(b, j):
                pe.wait_ge(n_out, b + 1)
                if not (known(b) and b < 1):
                    pe.wait_ge(p_ready, b)
                for g in range(GROUPS):
                    pe.matmul(p_t[:, g, :], kbd[j][:, g // 2, (g % 2) * 4:(g % 2) * 4 + 4, :], qT[j][:, g // 2, :],
                              start=True, stop=False)
                    last = pe.matmul(p_t[:, g, :], headrow[:, g * P:(g + 1) * P], negT[:, :],
                                     start=False, stop=True)
                last.then_inc(t_done, 1)

            def weigh(b, j):
                pe.wait_ge(p_ready, b + 1)
                for g in range(GROUPS):
                    last = pe.matmul(o_v[:, g, :, :], probs[:, g, :],
                                     vbd[:, one(b), g, :, :].rearrange("p o r d -> p (o r) d"), start=True, stop=True)
                last.then_inc(o_done, 1)

            def turn_attn(b, j):
                pe.wait_ge(attn_ready, b + 1)
                for c in range(C):
                    last = pe.transpose(p_y[:, c * P:(c + 1) * P], attn[:, c * P:(c + 1) * P], ident)
                last.then_inc(a_done, 1)

            def project(b, j):
                pe.wait_ge(aT_ready, b + 1)
                if not (known(b) and b < 1):
                    pe.wait_ge(res_ready, b)
                for c in range(C):
                    last = pe.matmul(p_proj, attnT[:, c, :], wo[:, c, :], start=(c == 0), stop=(c == C - 1))
                last.then_inc(y_done, 1)

            def turn_x1(b, j):
                pe.wait_ge(x1_ready, b + 1)
                if not (known(b) and b < 1):
                    pe.wait_ge(x1q_ready, b)
                for c in range(C):
                    last = pe.transpose(p_x[:, c, :], x1r[j][:, c * P:(c + 1) * P], ident)
                last.then_inc(x1T_done, 1)

            scores(0, 0)
            turn_max(0, 0)
            scores_T(0, 0)
            scores(1, 1)
            weigh(0, 0)
            turn_max(1, 1)
            scores_T(1, 1)
            turn_attn(0, 0)

            def step(b, j):
                def has(d):
                    return not known(b) or b + d < B
                if has(2):
                    scores(b + 2, j)
                if has(1):
                    weigh(b + 1, 1 - j)
                project(b, j)
                if has(2):
                    turn_max(b + 2, j)
                if not (known(b) and b < 2):
                    turn_x1(b - 2, j)
                if has(2):
                    scores_T(b + 2, j)
                if has(1):
                    turn_attn(b + 1, 1 - j)
            steps(pe, step, first=3, last=3)
            turn_x1(B - 2, 0)

            def convolve(h, f, j):
                u = h * 2 + f
                pe.wait_ge(head_in[j], 32 + 32 * (h // 2) if known(h) else (h - j) * 16 + 32)
                pe.wait_ge(kv_made, u + 1)
                if not (known(h) and h < 1):
                    pe.wait_ge(prod_done, u - 1)
                k = [kv[f][:, c, :, :, :] for c in range(C)]
                pe.matmul(p_conv[f][0], toe[j][:, 0:P], k[0], start=True, stop=True)
                pe.matmul(p_conv[f][1], toe[j][:, P:2 * P], k[0], start=True, stop=False)
                pe.matmul(p_conv[f][1], toe[j][:, 0:P], k[1], start=False, stop=True).then_inc(conv_done, 1)
            pe.wait_ge(q_out, B)
            pe.wait_ge(n_out, B)
            pe.wait_ge(p_ready, B)
            pe.wait_ge(res_ready, B)
            convolve(0, 0, 0)
            turn_x1(B - 1, 1)
            convolve(0, 1, 0)


            def add(h, f, j):
                u = h * 2 + f
                pe.wait_ge(prod_done, u + 1)
                if not (known(h) and h < 1):
                    pe.wait_ge(part_ready, u - 1)
                for s in range(BY_PE):
                    last = pe.matmul(p_part[f], ident, prod[f][:, :, :, s, :], start=(s == 0), stop=(s == BY_PE - 1))
                last.then_inc(part_done, 1)

            def turn_back(h, j):
                pe.wait_ge(sum_done, h * 2 + 2)
                pe.wait_ge(part_ready, h * 2 + 2)
                if not (known(h) and h < 1):
                    pe.wait_ge(res2_ready, h)
                if not (known(h) and h < 4):
                    pe.wait_ge(logit_ready, h - 3)
                for c in range(C):
                    for share in (conv, part):
                        last = pe.matmul(p_back[:, c * P:(c + 1) * P],
                                         share[j][:, c, :, :, :].rearrange("p f b i -> p (f b i)"), ident,
                                         start=(share is conv), stop=(share is part))
                last.then_inc(back_done, 1)

            def turn_x2(h, j):
                pe.wait_ge(x2_ready, h + 1)
                if not (known(h) and h < 1):
                    pe.wait_ge(x2T_ready, h)
                for c in range(C):
                    last = pe.transpose(p_x[:, c, :], x2r[j][:, c * P:(c + 1) * P], ident)
                last.then_inc(x2T_done, 1)

            def score(h, j, turned):
                pe.wait_ge(x2T_ready, h + 1)
                if not (known(h) and h < 1):
                    pe.wait_ge(logit_ready, h)
                pe.wait_ge(res2_ready, turned)
                for c in range(C):
                    last = pe.matmul(p_logit, x2T[j][:, c, :], gw[:, c, :], start=(c == 0), stop=(c == C - 1))
                last.then_inc(logit_done, 1)
            def shared_up(b, j):
                pe.wait_ge(slow_ready, b + 1)
                for q in range(3):
                    for c in range(C):
                        for k, p in enumerate((p_a, p_b)):
                            last = pe.matmul(p, xp[j][:, q, c, :], sw13s[:, c, k * SI:(k + 1) * SI],
                                             start=(q == 0 and c == 0), stop=(q == 2 and c == C - 1))
                last.then_inc(sa_done, 1)

            pe.wait_ge(gate_in, 16)

            def second(h, j):
                more = not (known(h) and h == HEADS - 1)
                if not (known(h) and h < 3):
                    turn_x2(h - 3, 1 - j)
                if not (known(h) and h < 4):
                    score(h - 4, j, h - 1)
                if more:
                    convolve(h + 1, 0, 1 - j)
                if not (known(h) and h < 1):
                    turn_back(h - 1, 1 - j)
                add(h, 0, j)
                if more:
                    convolve(h + 1, 1, 1 - j)
                add(h, 1, j)
            steps(pe, second, n=HEADS, first=4, last=2)
            turn_x2(HEADS - 3, 1)
            score(HEADS - 4, 0, HEADS - 1)
            turn_back(HEADS - 1, 1)
            score(HEADS - 3, 1, HEADS)
            pe.wait_ge(ffn_in, 16 * 2)
            shared_up(0, 0)
            for h in (HEADS - 2, HEADS - 1):
                turn_x2(h, h % 2)
                score(h, h % 2, HEADS)

            def shared_turn(b, j):
                pe.wait_ge(sh_ready, b + 1)
                if not (known(b) and b < 1):
                    pe.wait_ge(shT_ready, b)
                for k, (lo, n) in enumerate(SP_):
                    last = pe.transpose(p_hT[0:n, k, :], sh[:, lo:lo + n], ident)
                last.then_inc(shT_done, 1)

            def shared_down(b, j):
                pe.wait_ge(shT_ready, b + 1)
                if not (known(b) and b < 1):
                    pe.wait_ge(z0_ready, b)
                for k, (lo, n) in enumerate(SP_):
                    last = pe.matmul(p_z, shT[0:n, k, :], sw2s[0:n, k, :], start=(k == 0), stop=(k == 2))
                last.then_inc(z_done, 1)

            def rank():
                pe.wait_ge(hot_ready, 1)
                pe.matmul(p_rank, cstb[:, B_STRI:B_STRI + P], hot[:, :, :], start=True, stop=True)
                pe.matmul(p_sum, cstb[:, B_ONES:B_ONES + P], hot[:, :, :].rearrange("p n e -> p e n"), start=True, stop=True
                          ).then_inc(rank_done, 1)

            owners = []

            def shared(b, j):
                shared_turn(b, j)
                if not (known(b) and b == B - 1):
                    shared_up(b + 1, 1 - j)
                if known(b) and b >= B - 2:
                    turn_in(b - (B - 2), j)
                if known(b) and b == B - 1:
                    pe.wait_ge(owner_ready, 1)
                    pe.wait_ge(w13_in, 16 * E)
                    owners.append(expert(0))
                    up(0, 0, owners[0])
                    owners.append(expert(1))
                shared_down(b, j)
                if known(b) and b == 0:
                    rank()

            def expert(t):
                return pe.value_load(owner[0:1, one(t)], min_val=0, max_val=E - 1)

            def turn_in(t, j):
                pe.wait_ge(xs_in[j], 16 + 16 * (t // 2) if known(t) else (t - j) * 8 + 16)
                if not (known(t) and t < 1):
                    pe.wait_ge(rest_ready, t)
                for c in range(C):
                    last = pe.transpose(p_xs[:, c, :], xs[j][:, c * P:(c + 1) * P], ident)
                last.then_inc(xsT_done, 1)

            def up(t, j, e):
                pe.wait_ge(low_ready, t + 1)
                for q in range(3):
                    for c in range(C):
                        last = pe.matmul(p_ab[j], xp[j][:, q, c, :],
                                         w13s[:, c, bass.ds(e, 1), :].rearrange("p o n -> p (o n)"),
                                         start=(q == 0 and c == 0), stop=(q == 2 and c == C - 1))
                last.then_inc(ab_done, 1)

            def turn_mid(t, j):
                pe.wait_ge(hid_ready, t + 1)
                if not (known(t) and t < 1):
                    pe.wait_ge(hidT_ready, t)
                for k in range(2):
                    last = pe.transpose(p_hid[:, k, :], hid[j][:, k * KI:(k + 1) * KI], ident)
                last.then_inc(hidT_done, 1)

            def down(t, j, e):
                pe.wait_ge(hidT_ready, t + 1)
                if known(t) and t < 1:
                    pe.wait_ge(w2_in, 16 * W2_PARTS)
                    pe.wait_ge(z0_ready, B)
                else:
                    pe.wait_ge(ys_ready, t)
                for k in range(2):
                    last = pe.matmul(p_ye, hidT[j][:, k, :],
                                     w2s[:, bass.ds(e, 1), k, :].rearrange("p o n -> p (o n)"),
                                     start=(k == 0), stop=(k == 1))
                last.then_inc(ye_done, 1)

            def tile(t, j, e, following, late):
                def has(d):
                    return not known(t) or t + d < NT
                turn_mid(t, j)
                if has(2):
                    turn_in(t + 2, j)
                if has(1):
                    up(t + 1, 1 - j, following)
                found = expert(t + 2) if late else None
                down(t, j, e)
                return found

            def run(t, j, n, e=None, following=None):
                if e is None:
                    e, following = expert(t), expert(t + 1)
                for k in range(n):
                    e, following = following, tile(t + k, (j + k) % 2, e, following, k < n - 1 and not (known(t) and t + k + 2 >= NT))
            steps(pe, shared)
            run(0, 0, FIRST, *owners)
            with pe.Fori(0, NG) as i:
                run(i * TURN + FIRST, FIRST % 2, TURN)
            run(FIRST + NG * TURN, (FIRST + NG * TURN) % 2, NT - FIRST - NG * TURN)

            def shared_part(k):
                pe.matmul(p_fin[k], ident, z0[:, k * SLOTS:(k + 1) * SLOTS, :].rearrange("p b d -> p (b d)"),
                          start=True, stop=False)

            pe.wait_ge(rest_ready, NT)
            for k in PAIRS_PE[:-1]:
                shared_part(k)
            for k in PAIRS_PE:
                pe.wait_ge(y_in[k], 16 * TOP)
                for i in range(TOP):
                    last = pe.matmul(p_fin[k], ident,
                                     yg[:, i, k * SLOTS:(k + 1) * SLOTS, :].rearrange("p b d -> p (b d)"),
                                     start=False, stop=(i == TOP - 1))
                last.then_inc(fin_done, 1)
                if k == PAIRS_PE[0]:
                    pe.wait_ge(ys_ready, NT)
                    shared_part(PAIRS_PE[-1])

        @block.vector
        def _(v):
            done = [0]

            def chain(ins):
                ins.then_inc(dve, 1)
                done[0] += 1
                v.wait_ge(dve, done[0])

            v.memset(pick[:, :, :, :], 0.0)
            v.memset(vbd[:, :, :, :, :], 0.0).then_inc(setup, 1)
            v.wait_ge(setup, 1)
            for r in range(4):
                v.memset(vbd[32 * r:32 * r + 32, :, :, r, HD:HD + 1], 1.0)
            v.memset(half[:, 0:1], EPS)
            v.memset(half[:, 1:2], -0.5).then_inc(setup, 1)
            v.wait_ge(cst_in, 48)
            v.tensor_scalar(bqs[:, :], colb[:, 0:C], SCALE, None, ALU.mult).then_inc(setup, 1)
            for b in range(B):
                if b % 4 == 0:
                    v.wait_ge(xall_in[b // 4], 16)
                last = v.tensor_tensor_reduce(junk[:, b, :], xall[:, b, 0:D], rowb[:, 0, :], 1.0, 0.0, ALU.mult, ALU.add,
                                              imp[:, b:b + 1])
            chain(last)
            v.tensor_scalar(imp[:, :], imp[:, :], colb[:, 4:5], None, ALU.add).then_inc(imp_done, 1)
            v.wait_ge(impT_done, 1)
            chain(v.tensor_copy(impT[:, 0, :], p_y[0:B, 0:P]))
            for n in range(4):
                chain(v.max(top8[:, n, :], impT[:, n, :]))
                chain(v.match_replace(impT[:, n + 1, :], top8[:, n, :], impT[:, n, :], NEG))
            v.tensor_scalar(chosenT[:, :], impT[:, 4, :], NEG, None, ALU.is_equal).then_inc(mask_done, 1)
            v.wait_ge(maskT_done, 1)
            v.tensor_copy(chosen[:, :], p_s[:, 0:B]).then_inc(maskT_copied, 1)
            v.wait_ge(maskT_copied, 1)
            v.wait_ge(count_done, 1)
            chain(v.tensor_tensor(place[:, :], chosen[:, :], p_o[:, 0:B], ALU.mult))
            v.tensor_tensor(bass.AP(pick.tensor, pick.offset,
                                    [list(pick.ap[0]), [4 * P, 4], [P + KEEP, 4], [1, KEEP]]),
                            iota.rearrange("p (q n k) -> p q n k", q=1, n=1).to_broadcast([P, 4, 4, KEEP]),
                            place[:, :].rearrange("p (q n k) -> p q n k", q=4, k=1).to_broadcast([P, 4, 4, KEEP]),
                            ALU.is_equal).then_inc(pick_done, 1)
            v.wait_ge(gathered, 1)
            v.tensor_copy(picked[:, 0:2, :], p_picked[0]).then_inc(picked_out, 1)
            v.wait_ge(turned, 1)
            v.tensor_copy(xsel[:, 0, :], p_sel[0]).then_inc(xsel_out, 1)
            v.wait_ge(val_done, 1)
            for n in (0, 1):
                for r in range(4):
                    last = place_values(v.tensor_copy, n, r)
            last.then_inc(val_out, 1)

            for j in range(2):
                last = v.memset(prod[j][:, :, :, :, :], 0.0)
            last.then_inc(setup, 1)
            links = done[0] + 8

            def chain_at(b, n):
                if known(b) and b == B - 1:
                    return links + 6 * b - 3 + n
                return b * 6 + (links + n)

            def chase(b, j, n):
                v.wait_ge(s_done, b + 1)
                if not (known(b) and b < 1):
                    v.wait_ge(neg2_ready, b)
                v.tensor_reduce(mx[:, :], p_s[:, :].rearrange("p (h k) -> p h k", k=KEEP), AX.X, ALU.max,
                                negate=True).then_inc(dve, 1)
                v.wait_ge(dve, n(1))
                v.tensor_scalar(neg2[j][:, 0, :], mx[:, :], 0.0, None, ALU.min).then_inc(dve, 1)
                v.wait_ge(dve, n(2))
                v.scalar_tensor_tensor(out=neg2[j][:, 1, :], in0=mx[:, :], scalar=0.0, in1=neg2[j][:, 0, :],
                                       op0=ALU.min, op1=ALU.subtract).then_inc(dve, 1)
                v.wait_ge(dve, n(3))
                v.tensor_tensor(negm[j][:, :], neg2[j][:, 0, :], neg2[j][:, 1, :], ALU.add).then_inc(neg2_ready, 1)

            def normalise(b, j, n):
                v.wait_ge(z_ready, b + 1)
                v.wait_ge(o_done, b + 1)
                ov = o_v.rearrange("p g r d -> p (g r) d")
                v.scalar_tensor_tensor(out=den[:, :], in0=zero_e[j][:, :], scalar=float(S - KEEP),
                                       in1=ov[:, :, HD], op0=ALU.mult, op1=ALU.add).then_inc(dve, 1)
                v.wait_ge(dve, n(1))
                v.reciprocal(rec[:, :], den[:, :]).then_inc(dve, 1)
                v.wait_ge(dve, n(2))
                v.tensor_tensor(attn[:, :].rearrange("p (h d) -> p h d", d=HD), ov[:, :, 0:HD],
                                rec[:, :].rearrange("p (h o) -> p h o", o=1).to_broadcast([P, NH, HD]),
                                ALU.mult).then_inc(attn_ready, 1)

            def layer1(b, j):
                v.wait_ge(xbo_ready, b + 1)
                v.wait_ge(y_done, b + 1)
                if not (known(b) and b < 2):
                    v.wait_ge(x1_ready, b - 1)
                v.tensor_tensor(res[j][:, :], p_proj, xbo[j][:, :], ALU.add).then_inc(res_ready, 1)
                v.wait_ge(res_ready, b + 1)
                v.bn_stats(stats[:, :], res[j][:, :]).then_inc(dve, 1)
                v.wait_ge(dve, chain_at(b, {B - 2: 3, B - 1: 1}.get(b, 6) if known(b) else 6))
                if not (known(b) and b == 0):
                    x1_out(b - 1, 1 - j)
                v.bn_aggr(mv[j][:, :], stats[:, :]).then_inc(mv_ready, 1)

            def x1_out(b, j):
                v.wait_ge(rstd_ready, b + 1)
                if not (known(b) and b < 2):
                    v.wait_ge(x1_stored[j], (b - j) * 8)
                    v.wait_ge(x1T_done, b - 1)
                v.tensor_scalar(x1r[j][:, :], res[j][:, :], mv[j][:, 0:1], rstd[j][:, 0:1], ALU.subtract,
                                ALU.mult).then_inc(x1_ready, 1)

            chase(0, 0, lambda n: done[0] + n)
            chase(1, 1, lambda n: done[0] + 3 + n)
            normalise(0, 0, lambda n: done[0] + 6 + n)

            def step(b, j):
                if not known(b) or b + 2 < B:
                    chase(b + 2, j, lambda n: chain_at(b, n))
                if not known(b) or b + 1 < B:
                    before = 0 if known(b) and b + 2 >= B else 3
                    normalise(b + 1, 1 - j, lambda n: chain_at(b, before + n))
                layer1(b, j)
            steps(v, step, first=3, last=3)
            x1_out(B - 1, 1)

            def window(ap, n):
                return bass.AP(ap.tensor, ap.offset, [list(ap.ap[0]), [WRAP, BH], [1, n], [1, HEAD]])

            def products(h, f, j):
                u = h * 2 + f
                v.wait_ge(conv_done, u + 1)
                if not (known(h) and h < 1):
                    v.wait_ge(sum_done, u - 1)
                    v.wait_ge(part_done, u - 1)
                if not (known(h) and u == 0):
                    v.wait_ge(prod_done, u)
                for c in range(C):
                    q = x1q[:, one(h), c, f * BH:(f + 1) * BH, 0:HEAD]
                    y = p_conv[f][c].rearrange("p (b d i) -> p b d i", b=BH, d=DIAG)
                    v.tensor_tensor(prod[f][:, c, :, 0:DIAG, :], y, window(q, DIAG), ALU.mult)
                    o = prod[f][:, c, :, :, :]
                    o = bass.AP(o.tensor, o.offset + DIAG * HEAD + 1, [list(o.ap[0]), [ROWS * HEAD, BH],
                                                                      [2 * HEAD + 1, 3], [1, HEAD]])
                    qq = bass.AP(q.tensor, q.offset, [list(q.ap[0]), [WRAP, BH], [0, 3], [1, HEAD]])
                    last = v.tensor_tensor(o, y[:, :, 1:4, :], qq, ALU.mult)
                last.then_inc(prod_done, 1)

            def sums(h, f, j):
                if not (known(h) and h < 2):
                    v.wait_ge(back_done, h - 1)
                for c in range(C):
                    last = v.tensor_reduce(conv[j][:, c, f, :, :], prod[f][:, c, :, BY_PE:ROWS, :].rearrange("p b s i -> p b i s"),
                                           AX.X, ALU.add)
                last.then_inc(sum_done, 1)

            v.wait_ge(setup, 4)
            v.wait_ge(x1q_ready, B)
            v.wait_ge(o_done, B)

            def second(b, j):
                v.wait_ge(x1_back[j], 16 + 16 * (b // 2) if known(b) else (b - j) * 8 + 16)
                v.wait_ge(back_done, b + 1)
                if not (known(b) and b < 2):
                    v.wait_ge(x2_ready, b - 1)
                v.tensor_tensor(res2[j][:, :], p_back, x1s[j][:, :], ALU.add).then_inc(res2_ready, 1)
                if not (known(b) and b < 3):
                    scores_out(b - 3, 1 - j)
                v.wait_ge(res2_ready, b + 1)
                v.bn_stats(stats[:, :], res2[j][:, :]).then_inc(stats2, 1)
                v.wait_ge(stats2, b + 1)
                if known(b) and b == 0:
                    v.bn_aggr(mv[j][:, :], stats[:, :]).then_inc(mv2_ready, 1)
                else:
                    x2(b - 1, 1 - j)
                    v.bn_aggr(mv[j][:, :], stats[:, :]).then_inc(mv2_ready, 1)

            def x2(b, j):
                v.wait_ge(rstd2_ready, b + 1)
                if not (known(b) and b < 2):
                    v.wait_ge(x2_stored[j], (b - j) * 8)
                v.tensor_scalar(x2r[j][:, :], res2[j][:, :], mv[j][:, 0:1], rstd[j][:, 0:1], ALU.subtract,
                                ALU.mult).then_inc(x2_ready, 1)

            def scores_out(b, j):
                v.wait_ge(logit_done, b + 1)
                if known(b):
                    v.tensor_copy(logit[:, b, :], p_logit).then_inc(logit_ready, 1)
                else:
                    v.tensor_scalar(logit[:, one(b), :].rearrange("p o e -> p (o e)"), p_logit, 1.0, None,
                                    ALU.mult).then_inc(logit_ready, 1)

            def second_step(h, j):
                products(h, 0, j)
                if not (known(h) and h < 1):
                    sums(h - 1, 1, 1 - j)
                products(h, 1, j)
                sums(h, 0, j)
                if not (known(h) and h < 1):
                    second(h - 1, 1 - j)
            steps(v, second_step, n=HEADS, first=4, last=0)
            v.wait_ge(prod_done, 2 * HEADS)
            sums(HEADS - 1, 1, 1)
            def shared_rest(b, j):
                v.wait_ge(shigh_ready, b + 1)
                v.tensor_tensor(rest[j][:, :, :], x2S[j][:, :, :], xp[j][:, 0, :, :], ALU.subtract
                                ).then_inc(srest_ready, 1)

            def shared_low(b, j):
                v.wait_ge(smid_ready, b + 1)
                v.tensor_tensor(xp[j][:, 2, :, :], rest[j][:, :, :], xp[j][:, 1, :, :], ALU.subtract
                                ).then_inc(slow_ready, 1)

            for b in range(2):
                shared_rest(b, b)
            for b in range(2):
                shared_low(b, b)
            second(HEADS - 1, 1)
            x2(HEADS - 1, 1)
            def shared_h(b, j):
                v.wait_ge(ssil_ready, b + 1)
                v.tensor_tensor(sh[:, :], ssil[:, :], p_b, ALU.mult).then_inc(sh_ready, 1)

            scores_out(HEADS - 3, 1)
            shared_h(0, 0)
            scores_out(HEADS - 2, 0)
            scores_out(HEADS - 1, 1)

            def shared_z(b, j):
                v.wait_ge(z_done, b + 1)
                v.tensor_tensor(z0[:, one(b), :].rearrange("p o d -> p (o d)"), p_z,
                                x2all[:, one(b), 0:D].rearrange("p o d -> p (o d)"), ALU.add).then_inc(z0_ready, 1)
            def shared(b, j):
                if known(b) and b < 3:
                    return
                more = not (known(b) and b >= B - 2)
                if more:
                    shared_rest(b + 2, j)
                if not (known(b) and b == B - 1):
                    shared_h(b + 1, 1 - j)
                if more:
                    shared_low(b + 2, j)
                if known(b) and b == B - 2:
                    first_rest(0, 0)
                if known(b) and b == B - 1:
                    low(0, 0)
                    first_rest(1, 1)
                    low(1, 1)
                    hidden(0, 0)
                shared_z(b, j)
                if known(b) and b == 3:
                    ended_tiles()
                if known(b) and b == 4:
                    tile_owners()

            n = [0]

            def then(ins):
                ins.then_inc(route, 1)
                n[0] += 1
                v.wait_ge(route, n[0])
            v.wait_ge(logit_ready, B)
            for b in range(B):
                last = v.max(best[:, b, :], logit[:, b, :])
            then(last)
            for b in range(B):
                last = v.max_index(bestix[:, b, :], best[:, b, :], logit[:, b, :])
            then(last)
            then(v.tensor_copy(ixf[:, :].rearrange("p (b k) -> p b k", k=TOP), bestix[:, :, 0:TOP]))
            v.tensor_tensor(hot[:, :, :],
                            cst[:, C_N:C_N + E].rearrange("p (o e) -> p o e", o=1).to_broadcast([P, NB, E]),
                            ixf[:, :].rearrange("p (n o) -> p n o", o=1).to_broadcast([P, NB, E]),
                            ALU.is_equal).then_inc(hot_ready, 1)
            v.wait_ge(hot_ready, 1)
            for j in range(2):
                v.wait_ge(x2_stored[j], 8 * B)
            shared_rest(2, 0)
            shared_h(1, 1)
            shared_low(2, 0)
            shared_z(0, 0)
            v.wait_ge(rank_done, 1)
            v.wait_ge(late_in, 16)
            then(v.tensor_tensor_scan(upto[:, :, :].rearrange("p e n -> p (e n)"),
                                      cst[:, C_NEW:C_NEW + E * NB], p_sum, 0.0, ALU.mult, ALU.add))
            then(v.tensor_tensor(over[:, :, :],
                                 upto[:, :, NB - 1:NB].to_broadcast([P, E, 16]),
                                 cst[:, C_M:C_M + 16].rearrange("p (o m) -> p o m", o=1).to_broadcast([P, E, 16]),
                                 ALU.is_gt))
            then(v.tensor_reduce(tiles[:, :], over[:, :, :], AX.X, ALU.add))
            then(v.tensor_tensor_scan(endt[:, :], cst[:, C_ONES:C_ONES + E], tiles[:, :], 0.0, ALU.mult, ALU.add))
            then(v.tensor_tensor(base[:, :], endt[:, :], tiles[:, :], ALU.subtract))
            then(v.tensor_tensor(slot[:, :, :], upto[:, :, :].rearrange("p e n -> p n e"),
                                 p_sum.rearrange("p (e n) -> p n e", e=E), ALU.subtract))
            shared_rest(3, 1)
            shared_h(2, 0)
            shared_low(3, 1)
            shared_z(1, 1)
            then(v.tensor_tensor(slot[:, :, :], slot[:, :, :], p_rank.rearrange("p (n e) -> p n e", e=E), ALU.add))
            then(v.tensor_scalar(base[:, :], base[:, :], float(P), None, ALU.mult))
            v.wait_ge(sg_ready, 1)
            then(v.tensor_scalar(sg[:, :, :], sg[:, :, :], 1.0, None, ALU.add))
            then(v.reciprocal(sg[:, :, :], sg[:, :, :]))
            then(v.tensor_tensor(sgsum[:, :], sg[:, :, 0], sg[:, :, 1], ALU.add))
            then(v.reciprocal(sgsum[:, :], sgsum[:, :]))
            v.tensor_tensor(wts[:, :, :], sg[:, :, :],
                            sgsum[:, :].rearrange("p (b o) -> p b o", o=1).to_broadcast([P, B, TOP]),
                            ALU.mult).then_inc(wts_ready, 1)
            then(v.tensor_tensor(slot[:, :, :], slot[:, :, :],
                                 base[:, :].rearrange("p (o e) -> p o e", o=1).to_broadcast([P, NB, E]), ALU.add))
            shared_rest(4, 0)
            shared_h(3, 1)
            shared_low(4, 0)
            shared_z(2, 0)
            then(v.tensor_tensor(slot[:, :, :], slot[:, :, :], hot[:, :, :], ALU.mult))
            then(v.tensor_reduce(posf[:, :], slot[:, :, :], AX.X, ALU.add))
            v.tensor_copy(pos[:, :], posf[:, :]).then_inc(pos_ready, 1)
            def ended_tiles():
                then(v.tensor_tensor(ended[:, :, :],
                                     endt[0:1, :].rearrange("p (o e) -> p o e", o=1).to_broadcast([1, NT, E]),
                                     cst[0:1, C_N:C_N + NT].rearrange("p (t o) -> p t o", o=1).to_broadcast([1, NT, E]),
                                     ALU.is_le))

            def tile_owners():
                then(v.tensor_reduce(ownf[:, :], ended[:, :, :], AX.X, ALU.add))
                v.tensor_scalar(owner[:, :], ownf[:, :], float(E - 1), None, ALU.min).then_inc(owner_ready, 1)

            def hidden(t, j):
                v.wait_ge(sil_ready, t + 1)
                v.tensor_tensor(hid[j][:, :], sil[j][:, :], p_ab[j][:, I:2 * I], ALU.mult).then_inc(hid_ready, 1)

            def y_out(t, k):
                j = k % 2
                v.wait_ge(ye_done, t + 1)
                v.wait_ge(id_ready, t + 1)
                if not (known(t) and t < 2):
                    v.wait_ge(ys_stored[j], (t - j) * 8)
                v.tensor_scalar(ys[j][:, :], p_ye, share[k][:, 0:1], None, ALU.mult).then_inc(ys_ready, 1)
            def first_rest(t, j):
                v.wait_ge(high_ready, t + 1)
                v.tensor_tensor(rest[j][:, :, :], p_xs[:, :, :], xp[j][:, 0, :, :], ALU.subtract).then_inc(rest_ready, 1)

            def low(t, j):
                v.wait_ge(mid_ready, t + 1)
                v.tensor_tensor(xp[j][:, 2, :, :], rest[j][:, :, :], xp[j][:, 1, :, :], ALU.subtract
                                ).then_inc(low_ready, 1)
            steps(v, shared, first=6)

            def tile(t, k):
                j = k % 2
                more = not (known(t) and t + 2 >= NT)
                if more:
                    first_rest(t + 2, j)
                if not (known(t) and t == NT - 1):
                    hidden(t + 1, 1 - j)
                if more:
                    low(t + 2, j)
                y_out(t, k)
            steps(v, tile, n=NT, first=4, last=3, ways=8)

            m = 0
            for k in range(0, B, SLOTS):
                r = slice(k, k + SLOTS)
                pair = k // SLOTS
                if pair not in PAIRS_PE:
                    if pair == 1:
                        v.wait_ge(pair_sum, 1)
                    else:
                        v.wait_ge(y_in[pair], 16 * TOP)
                        v.tensor_tensor(z0[:, r, :], yg[:, 1, r, :], z0[:, r, :], ALU.add).then_inc(fin, 1)
                        m += 1
                        v.wait_ge(fin, m)
                    v.tensor_tensor(z0[:, r, :], yg[:, 0, r, :], z0[:, r, :], ALU.add).then_inc(fin, 1)
                    m += 1
                    v.wait_ge(fin, m)
                else:
                    v.wait_ge(fin_done, PAIRS_PE.index(pair) + 1)
                for b in range(k, k + SLOTS):
                    last = v.bn_stats(st3[:, b, :], z0[:, b, :] if pair not in PAIRS_PE else
                                      p_fin[pair][:, (b - k) * D:(b - k + 1) * D])
                last.then_inc(st3_ready, 1)
                v.wait_ge(st3_ready, k // SLOTS + 1)
                for b in range(k, k + SLOTS):
                    last = v.bn_aggr(mv3[:, b, :], st3[:, b, :])
                last.then_inc(mv3_ready, 1)

        @block.scalar
        def _(a):
            def load_x(g):
                if g >= 2:
                    a.wait_ge(qall_done, g - 1)
                a.dma_start(xg[g % 2][:, :, :], xT[g]).then_inc(x_in[g % 2], 16)
            a.dma_start(wq[:, :, :], Wq.rearrange("(c p) n -> p c n", p=P)).then_inc(wq_in, 16)
            load_x(0)
            a.wait_ge(xall_in[0], 16)
            load_x(1)
            for w, dram in ((wk, Wk), (wv, Wv), (wo, Wo)):
                a.dma_start(w[:, :, :], dram.rearrange("(c p) n -> p c n", p=P)).then_inc(w_in, 16)
            a.wait_ge(setup, 3)

            def queries_all(g):
                a.wait_ge(qall_done, g + 1)
                for c in range(C):
                    last = a.activation(qall[:, c, g * 4 * S:(g + 1) * 4 * S], p_qall[g % 2][c], ACT.Identity,
                                        bias=bqs[:, c:c + 1], scale=SCALE)
                last.then_inc(qall_out, 1)
            queries_all(0)
            load_x(2)
            queries_all(1)
            load_x(3)
            a.wait_ge(gathered, 2)
            a.copy(picked[:, 2:4, :], p_picked[1]).then_inc(picked_out, 1)
            a.wait_ge(turned, C)
            a.copy(xsel[:, 1, :], p_sel[1]).then_inc(xsel_out, 1)
            queries_all(2)
            a.wait_ge(key_done, 1)
            for m in range(C):
                last = a.activation(keyT[:, m, :], p_key[m], ACT.Identity, bias=colb[:, C + m:C + m + 1])
            last.then_inc(key_out, 1)
            a.wait_ge(val_done, 1)
            for n in (2, 3):
                for r in range(4):
                    last = place_values(a.copy, n, r)
            last.then_inc(val_out, 1)

            queries_all(3)
            a.wait_ge(qall_out, 4)

            def queries_out(b, j):
                a.copy(qT[j][:, :, :], qall[:, :, b * S:(b + 1) * S] if known(b) else qall[:, :, bass.ds(b * S, S)]
                       ).then_inc(q_out, 1)

            def max_out(b, j):
                a.wait_ge(n_done, b + 1)
                if not (known(b) and b < 1):
                    a.wait_ge(t_done, b)
                a.copy(negT[:, :], p_neg).then_inc(n_out, 1)
                a.activation(zero_e[j][:, :], negm[j][:, :], ACT.Exp).then_inc(z_ready, 1)

            def exps(b, j):
                a.wait_ge(t_done, b + 1)
                if not (known(b) and b < 1):
                    a.wait_ge(o_done, b)
                a.activation(probs[:, :, :], p_t[:, :, :], ACT.Exp).then_inc(p_ready, 1)

            def attn_out(b, j):
                a.wait_ge(a_done, b + 1)
                a.copy(attnT[:, :, :], p_y[:, 0:256].rearrange("p (c s) -> p c s", c=C)).then_inc(aT_ready, 1)

            def x1q_copy(b):
                for lo, n in ((0, HEAD), (HEAD, WRAP - HEAD)):
                    last = a.copy(x1q[:, :, :, one(b), lo:lo + n].rearrange("p h c o i -> p c h (o i)"),
                                  p_x[:, :, :].rearrange("p c (h i) -> p c h i", i=HEAD)[:, :, :, 0:n])
                last.then_inc(x1q_ready, 1)
            queries_out(0, 0)
            queries_out(1, 1)
            max_out(0, 0)
            exps(0, 0)
            queries_out(2, 0)
            max_out(1, 1)
            exps(1, 1)

            def step(b, j):
                def has(d):
                    return not known(b) or b + d < B
                if not (known(b) and b < 3):
                    a.wait_ge(x1T_done, b - 2)
                attn_out(b, j)
                if has(3):
                    queries_out(b + 3, 1 - j)
                if not (known(b) and b < 3):
                    x1q_copy(b - 3)
                if has(2):
                    max_out(b + 2, j)
                    exps(b + 2, j)
            steps(a, step, first=3, last=3)
            a.wait_ge(x1T_done, B - 2)
            x1q_copy(B - 3)
            for b in (B - 2, B - 1):
                a.wait_ge(x1T_done, b + 1)
                x1q_copy(b)

            def part_out(h, f, j):
                a.wait_ge(part_done, h * 2 + (f + 1))
                if not (known(h) and h < 2):
                    a.wait_ge(back_done, h - 1)
                a.copy(part[j][:, :, f, :, :], p_part[f]).then_inc(part_ready, 1)

            def x2T_copy(h, j):
                a.wait_ge(x2T_done, h + 1)
                if not (known(h) and h < 2):
                    a.wait_ge(x2T_stored[j], (h - j) * 8)
                a.copy(x2T[j][:, :, :], p_x[:, :, :]).then_inc(x2T_ready, 1)

            def second(h, j):
                if not (known(h) and h < 3):
                    x2T_copy(h - 3, 1 - j)
                part_out(h, 0, j)
                part_out(h, 1, j)
            steps(a, second, n=HEADS, first=4, last=0)

            def shared_high(b, j):
                a.wait_ge(x2T_in[j], 16 + 16 * (b // 2) if known(b) else (b - j) * 8 + 16)
                a.copy(xp[j][:, 0, :, :], x2S[j][:, :, :]).then_inc(shigh_ready, 1)

            def shared_mid(b, j):
                a.wait_ge(srest_ready, b + 1)
                a.copy(xp[j][:, 1, :, :], rest[j][:, :, :]).then_inc(smid_ready, 1)
            x2T_copy(HEADS - 3, 1)
            for b in range(2):
                shared_high(b, b)
            for b in range(2):
                shared_mid(b, b)
            def shared_silu(b, j):
                a.wait_ge(sa_done, b + 1)
                a.activation(ssil[:, :], p_a, ACT.Silu).then_inc(ssil_ready, 1)

            shared_silu(0, 0)
            x2T_copy(HEADS - 2, 0)
            x2T_copy(HEADS - 1, 1)

            def shared_hT(b, j):
                a.wait_ge(shT_done, b + 1)
                a.copy(shT[:, 0:2, :], p_hT[:, 0:2, :])
                a.copy(shT[0:SP_[2][1], 2, :], p_hT[0:SP_[2][1], 2, :]).then_inc(shT_ready, 1)
            def shared(b, j):
                more = not (known(b) and b >= B - 2)
                if known(b) and b == B - 1:
                    mid(0, 0)
                shared_hT(b, j)
                if more:
                    shared_high(b + 2, j)
                if not (known(b) and b == B - 1):
                    shared_silu(b + 1, 1 - j)
                if more:
                    shared_mid(b + 2, j)
                if known(b) and b == 0:
                    a.wait_ge(route, 1)
                    a.activation(sg[:, :, :], best[:, :, 0:TOP], ACT.Exp, scale=-1.0).then_inc(sg_ready, 1)
                if known(b) and b == B - 2:
                    high(0, 0)
                if known(b) and b == B - 1:
                    high(1, 1)
                    mid(1, 1)
                    silu(0, 0)

            def high(t, j):
                a.wait_ge(xsT_done, t + 1)
                a.copy(xp[j][:, 0, :, :], p_xs[:, :, :]).then_inc(high_ready, 1)

            def mid(t, j):
                a.wait_ge(rest_ready, t + 1)
                a.copy(xp[j][:, 1, :, :], rest[j][:, :, :]).then_inc(mid_ready, 1)

            def silu(t, j):
                a.wait_ge(ab_done, t + 1)
                a.activation(sil[j][:, :], p_ab[j][:, 0:I], ACT.Silu).then_inc(sil_ready, 1)

            def hidT_copy(t, j):
                a.wait_ge(hidT_done, t + 1)
                a.copy(hidT[j][:, :, :], p_hid).then_inc(hidT_ready, 1)
            steps(a, shared)

            def tile(t, j):
                def has(d):
                    return not known(t) or t + d < NT
                hidT_copy(t, j)
                if has(2):
                    high(t + 2, j)
                if has(1):
                    silu(t + 1, 1 - j)
                if has(2):
                    mid(t + 2, j)
            steps(a, tile, n=NT, first=3, last=2)

            for k in range(0, B, SLOTS):
                a.wait_ge(rs3_ready, 2 * (k // SLOTS + 1))
                pair = k // SLOTS
                for b in range(k, k + SLOTS):
                    z = z0[:, b, :] if pair not in PAIRS_PE else p_fin[pair][:, (b - k) * D:(b - k + 1) * D]
                    a.activation(x2all[:, b, 0:D], z, ACT.Identity, bias=nm3[:, b:b + 1],
                                 scale=rs3[:, b:b + 1]).then_inc(out_ready, 1)

        @block.gpsimd
        def _(g):
            g.memset(kerp[:, :], 0.0).then_inc(ker_zero, 1)
            g.wait_ge(ker_zero, 1)
            g.dma_start(kerp[:, D:2 * D], ker).then_inc(ker_in, 16)
            g.dma_start(skipc[:, :], skip).then_inc(ker_in, 16)
            g.wait_ge(ker_in, 32)
            g.tensor_tensor(kerp[:, D:D + 1], kerp[:, D:D + 1], skipc[:, :], ALU.add).then_inc(ker_sum, 1)
            g.wait_ge(ker_sum, 1)
            g.dma_start(kerd, kerp[:, :]).then_inc(ker_out, 16)
            g.dma_start(gw[:, :, :], gate).then_inc(gate_in, 16)
            g.wait_ge(x_in[1], 16)
            g.dma_start(sw13s[:, :, :], sw13).then_inc(ffn_in, 16)
            g.dma_start(sw2s[:, :, :], sw2).then_inc(ffn_in, 16)
            g.wait_ge(setup, 3)

            def blocks(b, j):
                g.tensor_tensor(kbd[j][:, :, :, :],
                                keyT[:, :, b * KEEP:(b + 1) * KEEP].rearrange("p c (o k) -> p c o k", o=1)
                                .to_broadcast([P, C, 8, KEEP]) if known(b) else
                                keyT[:, :, bass.ds(b * KEEP, KEEP)].rearrange("p c (o k) -> p c o k", o=1)
                                .to_broadcast([P, C, 8, KEEP]),
                                headmask.rearrange("p (c h k) -> p c h k", c=1, k=1).to_broadcast([P, C, 8, KEEP]),
                                ALU.mult).then_inc(kbd_ready, 1)

            def residual(b, j):
                g.tensor_tensor(xbo[j][:, :], xall[:, one(b), 0:D].rearrange("p o d -> p (o d)"), rowb[:, 1, :],
                                ALU.add).then_inc(xbo_ready, 1)

            def norm(b, j):
                g.wait_ge(mv_ready, b + 1)
                g.tensor_tensor(vare[:, :], mv[j][:, 1:2], half[:, 0:1], ALU.add).then_inc(pool, 1)
                g.wait_ge(pool, b + 1)
                g.tensor_tensor(rstd[j][:, :], vare[:, :], half[:, 1:2], ALU.pow).then_inc(rstd_ready, 1)

            for q in range(4):
                g.wait_ge(xall_in[q], 16)
            residual(0, 0)
            residual(1, 1)
            g.wait_ge(key_out, 1)
            blocks(0, 0)
            blocks(1, 1)
            g.wait_ge(t_done, 1)
            blocks(2, 0)
            g.memset(zeros[:, :, :], 0.0).then_inc(zero_ready, 1)
            g.wait_ge(zero_ready, 1)
            g.wait_ge(late_in, 16)
            g.tensor_copy(zeros[:, :, D].bitcast(U32), cst[:, C_PAIR + NB:C_PAIR + NB + 2]).then_inc(zero_ready, 1)
            g.wait_ge(zero_ready, 2)
            xs_z = xsd.rearrange("(t p) d -> p t d", p=P)
            for j in range(2):
                g.dma_start(xs_z[:, j:NT:2, :], zeros[:, j:j + 1, :].to_broadcast([P, (NT + 1 - j) // 2, ROW])
                            ).then_inc(xsd_zeroed, 16)

            def multiply(h, f, j):
                u = h * 2 + f
                g.wait_ge(head_in[j], 32 + 32 * (h // 2) if known(h) else (h - j) * 16 + 32)
                if not (known(h) and h < 1):
                    g.wait_ge(conv_done, u - 1)
                for c in range(C):
                    k = ctxr[j][:, c, f * BH:(f + 1) * BH, 0:HEAD]
                    a0 = bass.AP(k.tensor, k.offset, [list(k.ap[0]), [WRAP, BH], [0, DIAG], [1, HEAD]])
                    a1 = bass.AP(k.tensor, k.offset, [list(k.ap[0]), [WRAP, BH], [1, DIAG], [1, HEAD]])
                    last = g.tensor_tensor(kv[f][:, c, :, :, :], a0, a1, ALU.mult)
                last.then_inc(kv_made, 1)

            def step(b, j):
                if not (known(b) and b < 1):
                    if not known(b) or b + 3 < B:
                        g.wait_ge(t_done, b + 2)
                    g.wait_ge(res_ready, b)
                    norm(b - 1, 1 - j)
                else:
                    g.wait_ge(t_done, 2)
                if not known(b) or b + 3 < B:
                    blocks(b + 3, 1 - j)
                if not (known(b) and (b < 1 or b + 1 >= B)):
                    residual(b + 1, 1 - j)
                if known(b) and b >= B - 2:
                    g.wait_ge(xsd_zeroed, 32)
                    multiply(0, b - (B - 2), 0)
            steps(g, step, first=3, last=3)
            norm(B - 1, 1)

            def norm2(b, j):
                g.wait_ge(mv2_ready, b + 1)
                g.tensor_tensor(vare[:, :], mv[j][:, 1:2], half[:, 0:1], ALU.add).then_inc(pool, 1)
                g.wait_ge(pool, B + b + 1 if known(b) else b + (B + 1))
                g.tensor_tensor(rstd[j][:, :], vare[:, :], half[:, 1:2], ALU.pow).then_inc(rstd2_ready, 1)

            g.wait_ge(q_out, B)
            assert HEADS == E

            def second(h, j):
                g.dma_start(w13s[:, :, one(h), :], w13[:, :, one(h), :]).then_inc(w13_in, 16)
                if not (known(h) and h < 1):
                    multiply(h, 0, j)
                    multiply(h, 1, j)
                if not (known(h) and h < 3):
                    norm2(h - 3, 1 - j)
            steps(g, second, n=HEADS, first=4, last=0)
            g.wait_ge(prod_done, 2 * HEADS)
            for h in range(HEADS - 3, HEADS):
                norm2(h, h % 2)

            def norm3(k):
                r = slice(k * SLOTS, (k + 1) * SLOTS)
                g.wait_ge(mv3_ready, k + 1)
                g.tensor_scalar(nm3[:, r], mv3[:, r, 0], -1.0, None, ALU.mult).then_inc(ve3_ready, 1)
                g.tensor_tensor(ve3[:, r], mv3[:, r, 1], half[:, 0:1].to_broadcast([P, SLOTS]), ALU.add
                                ).then_inc(ve3_ready, 1)
                g.wait_ge(ve3_ready, 2 * (k + 1))
                g.tensor_tensor(rs3[:, r], ve3[:, r], half[:, 1:2].to_broadcast([P, SLOTS]), ALU.pow
                                ).then_inc(rs3_ready, 1)
                g.wait_ge(rs3_ready, 2 * k + 1)
                g.tensor_tensor(nm3[:, r], nm3[:, r], rs3[:, r], ALU.mult).then_inc(rs3_ready, 1)

            for k in range(W2_PARTS):
                g.wait_ge(sa_done, k // 2 + 1)
                r = slice(k * E // W2_PARTS, (k + 1) * E // W2_PARTS)
                g.dma_start(w2s[:, r, :, :], w2[:, r, :, :]).then_inc(w2_in, 16)
            g.wait_ge(xsd_zeroed, 32)
            for j in range(2):
                g.wait_ge(x2_stored[j], 8 * B)
            g.wait_ge(pos_ready, 1)
            g.wait_ge(wts_ready, 1)
            for i in range(TOP):
                for k in range(2):
                    half_b = slice(k * B // 2, (k + 1) * B // 2)
                    if i > 0:
                        g.wait_ge(scattered[k], 16 * B // 2)
                    first = C_PAIR + i * B
                    g.tensor_copy(x2all[:, half_b, D].bitcast(U32),
                                  cst[:, first + k * B // 2:first + (k + 1) * B // 2]).then_inc(pairs_next, 1)
                    g.tensor_copy(x2all[:, half_b, D + 1], wts[:, half_b, i]).then_inc(pairs_next, 1)
                    g.wait_ge(pairs_next, 2 * (2 * i + k + 1))
                    for b in range(k * B // 2, (k + 1) * B // 2):
                        n = b * TOP + i
                        g.indirect_dma_start(xsd, bass.IndirectOffsetOnAxis(pos[:, n:n + 1], 0), x2all[:, b, :], None
                                             ).then_inc(scattered[k], 16)

            def places(t, k):
                g.wait_ge(xs_in[k % 2], 16 + 16 * (t // 2) if known(t) else (t - k % 2) * 8 + 16)
                if not (known(t) and t < 8):
                    g.wait_ge(ys_stored[k % 2], (t - 6 - k % 2) * 8)
                g.tensor_tensor(share[k][:, :], xs[k % 2][:, D + 1:D + 2], cst[:, C_M:C_M + 1], ALU.add)
                g.tensor_tensor(idr[k][:, :], xs[k % 2][:, D:D + 1].bitcast(U32), cst[:, C_M:C_M + 1].bitcast(U32),
                                ALU.add).then_inc(id_ready, 1)

            def store_tile(t, k):
                g.wait_ge(ys_ready, t + 1)
                g.wait_ge(id_ready, min(t + 3, NT) if known(t) else t + 3)
                if not (known(t) and t + 3 >= NT):
                    places(t + 3, (k + 3) % 8)
                g.indirect_dma_start(ypd, bass.IndirectOffsetOnAxis(idr[k][:, 0:1], 0), ys[k % 2][:, :], None
                                     ).then_inc(ys_stored[k % 2], 16)
            places(0, 0)
            places(1, 1)
            places(2, 2)
            steps(g, store_tile, n=NT, first=4, last=3, ways=8)

            pair = slice(SLOTS, 2 * SLOTS)
            g.wait_ge(y_in[1], 16 * TOP)
            g.tensor_tensor(yg[:, 0, pair, :], yg[:, 0, pair, :], yg[:, 1, pair, :], ALU.add).then_inc(pair_sum, 1)
            for k in range(B // SLOTS):
                norm3(k)


def tables():
    import numpy as np
    t = np.zeros((P, C_W), np.float32)
    i = np.arange(P)
    t[:, C_ID:C_ID + P] = np.eye(P)
    t[:, C_TRI:C_TRI + P] = i[:, None] <= i[None, :]
    t[:, C_IOTA:C_IOTA + KEEP] = np.arange(1, KEEP + 1)
    t[:, C_HM:C_HM + 8] = i[:, None] // HD == np.arange(8)[None, :]
    t[:, C_ONES:C_ONES + P] = 1.0
    t[:, C_N:C_N + 64] = np.arange(64)
    t[:, C_M:C_M + 16] = np.arange(16) * P
    t[:, C_NEW:C_NEW + E * NB] = np.arange(E * NB) % NB != 0
    t[:, C_PAIR:C_PAIR + NB + 2] = i[:, None] + np.arange(NB + 2) * P
    return t


def tables_bf16(bf16):
    import numpy as np
    t = np.zeros((P, B_W), np.float32)
    t[:, 0:P] = np.eye(P)
    n = np.arange(GROUPS * P)
    t[0:2 * NH, P:B_STRI] = np.arange(2 * NH)[:, None] % NH == (n // P * 4 + n % P // KEEP)[None, :]
    t[:, B_STRI:B_ONES] = np.arange(P)[:, None] < np.arange(P)[None, :]
    t[:, B_ONES:] = 1.0
    return t.astype(bf16)


def kernel(**inputs):
    import numpy as np
    import concourse.bacc as bacc
    from concourse.bass_utils import run_bass_kernel_spmd

    nc = bacc.Bacc("TRN2", target_bir_lowering=False, num_devices=1)
    a = {k: np.asarray(v) for k, v in inputs.items()}
    x = a["x"]
    bq, bk, bi = a["L0_attn_bq"], a["L0_attn_bk"], a["L0_attn_bi"]
    arrays = {
        "x": x,
        "constb": tables_bf16(a["L0_ffn_w1"].dtype),
        "xT": np.ascontiguousarray(x.reshape(4, 4, S, C, P).transpose(0, 4, 3, 1, 2).reshape(4, P, C, 4 * S)),
        "ctx": np.ascontiguousarray(np.take(
            a["ctx_2048"].reshape(B, HEADS, HEAD, C, P)[:, :, :, :, ::-1], np.arange(WRAP) % HEAD, axis=2
        ).transpose(1, 4, 3, 0, 2)),
        "ker": a["L0_xattn_ssm_kernel"],
        "skip": a["L0_xattn_D"].reshape(HEADS, 1),
        "Wq": a["L0_attn_Wq"], "Wk": a["L0_attn_Wk"], "Wv": a["L0_attn_Wv"], "Wo": a["L0_attn_Wo"],
        "cols": np.ascontiguousarray(np.concatenate([bq.reshape(C, P).T, bk.reshape(C, P).T,
                                                     np.broadcast_to(bi, (P, 1))], axis=1)),
        "rows": np.stack([a["L0_attn_Wi"].reshape(-1), a["L0_attn_bo"], a["L0_attn_bv"]]),
        "consts": tables(),
        "gate": np.ascontiguousarray(a["L0_ffn_gate_w"].T.reshape(C, P, E).transpose(1, 0, 2)),
        "w13": np.ascontiguousarray(np.concatenate([a["L0_ffn_w1"], a["L0_ffn_w3"]], axis=1)
                                    .reshape(E, 2 * I, C, P).transpose(3, 2, 0, 1)),
        "w2": np.ascontiguousarray(a["L0_ffn_w2"].reshape(E, D, 2, KI).transpose(3, 0, 2, 1)),
        "sw13": np.ascontiguousarray(np.concatenate([a["L0_ffn_sw1"], a["L0_ffn_sw3"]], axis=0)
                                     .reshape(2 * SI, C, P).transpose(2, 1, 0)),
        "sw2": np.ascontiguousarray(np.pad(a["L0_ffn_sw2"], ((0, 0), (0, 3 * P - SI))).reshape(D, 3, P)
                                    .transpose(2, 1, 0)),
    }
    args = [nc.dram_tensor(f"in_{n}_dram", v.shape, mybir.dt.from_np(v.dtype), kind="ExternalInput").ap()
            for n, v in arrays.items()]
    out = nc.dram_tensor("out_0_dram", (B, S, D), F32, kind="ExternalOutput").ap()
    decoder_layer(nc, *args, out)
    r = run_bass_kernel_spmd(nc, [{f"in_{n}_dram": v for n, v in arrays.items()}], core_ids=[0])
    return r.results[0]["out_0_dram"]
```
